# Optimizing a Trainium2 kernel written in Bass

```python
import numpy as np
import jax
import jax.numpy as jnp

def _softmax(x, axis=-1):
    return jax.nn.softmax(x, axis=axis)

def _gelu(x):
    return jax.nn.gelu(x, approximate=True)

def _silu(x):
    return jax.nn.silu(x)

def _sigmoid(x):
    return jax.nn.sigmoid(x)

def _layernorm(x, axis=-1, eps=1e-05):
    m = jnp.mean(x, axis=axis, keepdims=True)
    v = jnp.var(x, axis=axis, keepdims=True)
    return (x - m) / jnp.sqrt(v + eps)

def _scatter_add(tgt, idx, src, axis=0):
    return tgt.at[idx].add(src)

def _segment_sum(src, seg, n):
    return jax.ops.segment_sum(src, seg, n)
kernel_name = 'mk_decoder_preln_d1_seqx_r4_586e8d'

def setup_inputs(seed: int=0):
    np.random.seed(seed)
    _w = jnp.asarray

    def _rec_inputs():
        import jax
        import jax.numpy as jnp
        _rk = jax.random.key(seed)
        x = -0.000125 + 0.9999 * jax.random.normal(jax.random.fold_in(_rk, 1), (4, 512, 256), jnp.float32)
        _lenS = 512 - jax.random.randint(jax.random.fold_in(_rk, 7), (4,), 0, max(1, 512 // 4) + 1, jnp.int32)
        _lenS2 = 512 - jax.random.randint(jax.random.fold_in(_rk, 8), (4,), 0, max(1, 512 // 4) + 1, jnp.int32)
        _ctx_1024P = jax.random.normal(jax.random.fold_in(_rk, 11), (4, 16, 256), jnp.float32)
        _ctx_1024c = jax.random.dirichlet(jax.random.fold_in(_rk, 511), 0.3 * jnp.ones((16,), jnp.float32), (4, 512))
        _ctx_1024t = jnp.einsum('bsk,bkd->bsd', _ctx_1024c, _ctx_1024P)
        _ctx_1024t = _ctx_1024t * jax.lax.rsqrt(jnp.mean(jnp.square(_ctx_1024t)) + 1e-12) * 0.953939
        ctx_1024 = -1.52775e-05 + 0.999936 * (_ctx_1024t + 0.3 * jax.random.normal(jax.random.fold_in(_rk, 611), (4, 512, 256), jnp.float32))
        _validS = jnp.arange(512)[None, :] < _lenS[:, None]
        _validS2 = jnp.arange(512)[None, :] < _lenS2[:, None]
        _causal = jnp.tril(jnp.ones((512, 512), dtype=bool))
        mask_BxS2_bk1 = jnp.broadcast_to(_validS2[:, :], (4, 512))
        return (x, ctx_1024, mask_BxS2_bk1)
    x, ctx_1024, mask_BxS2_bk1 = _rec_inputs()

    def _L0_attn_setup():
        import jax, jax.numpy as jnp
        import numpy as np
        BATCH, SEQ, D_EMBED, N_HEADS, D_HEAD = (1, 512, 256, 16, 64)
        MASK_VAL = 10000000000.0
        key = jax.random.key(seed)
        ks = jax.random.split(key, 5)
        s = 1.0 / np.sqrt(D_EMBED).astype(np.float32)
        return {'x': jax.random.normal(ks[0], (BATCH, SEQ, D_EMBED), jnp.float32), 'W_Q': jax.random.normal(ks[1], (N_HEADS, D_HEAD, D_EMBED), jnp.float32) * s, 'W_K': jax.random.normal(ks[2], (N_HEADS, D_HEAD, D_EMBED), jnp.float32) * s, 'W_V': jax.random.normal(ks[3], (N_HEADS, D_HEAD, D_EMBED), jnp.float32) * s, 'W_O': jax.random.normal(ks[4], (N_HEADS, D_EMBED, D_HEAD), jnp.float32) * s}
    _L0_attn_all = _L0_attn_setup()
    _L0_attn_in = {k: v for k, v in _L0_attn_all.items() if k in ('W_Q', 'W_K', 'W_V', 'W_O')}
    del _L0_attn_all

    def _L0_xattn_setup():
        import jax, jax.numpy as jnp
        import numpy as np
        EPS = 1e-12

        def _l2_normalize(x, axis):
            n = jnp.sqrt(jnp.sum(x * x, axis=axis, keepdims=True))
            return x / jnp.maximum(n, EPS)
        key = jax.random.key(seed)
        ks = jax.random.split(key, 13)
        b, n, d, h = (8, 1024, 256, 16)
        scale = 0.02
        inp = {'query': jax.random.normal(ks[0], (b, n, d), jnp.float32), 'key': jax.random.normal(ks[1], (b, n, d), jnp.float32), 'value': jax.random.normal(ks[2], (b, n, d), jnp.float32), 'key_padding_mask': jax.random.randint(ks[3], (b, n), 0, 2).astype(bool), 'Wq': jax.random.normal(ks[4], (d, d), jnp.float32) * scale, 'bq': jax.random.normal(ks[5], (d,), jnp.float32) * scale, 'Wk': jax.random.normal(ks[6], (d, d), jnp.float32) * scale, 'bk': jax.random.normal(ks[7], (d,), jnp.float32) * scale, 'Wv': jax.random.normal(ks[8], (d, d), jnp.float32) * scale, 'bv': jax.random.normal(ks[9], (d,), jnp.float32) * scale, 'Wo': jax.random.normal(ks[10], (d, d), jnp.float32) * scale, 'bo': jax.random.normal(ks[11], (d,), jnp.float32) * scale}
        return inp
    _L0_xattn_all = _L0_xattn_setup()
    _L0_xattn_in = {k: v for k, v in _L0_xattn_all.items() if k in ('Wq', 'bq', 'Wk', 'bk', 'Wv', 'bv', 'Wo', 'bo')}
    del _L0_xattn_all

    def _L0_ffn_setup():
        import jax, jax.numpy as jnp
        import numpy as np
        DIM = 256
        DEPTH = 2
        HEADS = 8
        DIM_HEAD = 64
        WINDOW = 128
        INNER = HEADS * DIM_HEAD
        HID = int(DIM * 4 * 2 / 3)
        B, N = (2, 2048)
        QK_SCALE = 8.0

        def shift_token(t):
            t1, t2 = jnp.split(t, 2, axis=-1)
            t2 = jnp.pad(t2, ((0, 0), (1, 0), (0, 0)))[:, :-1]
            return jnp.concatenate([t1, t2], axis=-1)

        def l2norm(t):
            return t / jnp.clip(jnp.linalg.norm(t, axis=-1, keepdims=True), 1e-12)

        def rotate_half(x):
            x1, x2 = jnp.split(x, 2, axis=-1)
            return jnp.concatenate([-x2, x1], axis=-1)

        def rotary_xpos(q, k):
            n = q.shape[-2]
            half_idx = jnp.arange(0, DIM_HEAD, 2, dtype=jnp.float32)
            inv_freq = 1.0 / 10000.0 ** (half_idx / DIM_HEAD)
            t = jnp.arange(n, dtype=jnp.float32)
            freqs = t[:, None] * inv_freq[None, :]
            freqs = jnp.concatenate([freqs, freqs], axis=-1)
            base = (half_idx + 0.4 * DIM_HEAD) / (1.4 * DIM_HEAD)
            power = (t - n // 2) / float(WINDOW // 2)
            scale = base[None, :] ** power[:, None]
            scale = jnp.concatenate([scale, scale], axis=-1)
            cos, sin = (jnp.cos(freqs), jnp.sin(freqs))
            q = q * cos * scale + rotate_half(q) * sin * scale
            k = k * cos / scale + rotate_half(k) * sin / scale
            return (q, k)

        def local_attention(q, k, v):
            b, h, n, d = q.shape
            w = n // WINDOW
            bq = q.reshape(b, h, w, WINDOW, d) * QK_SCALE
            bk = k.reshape(b, h, w, WINDOW, d)
            bv = v.reshape(b, h, w, WINDOW, d)

            def look_around(t):
                p = jnp.pad(t, ((0, 0), (0, 0), (1, 0), (0, 0), (0, 0)))
                return jnp.concatenate([p[:, :, :w], p[:, :, 1:]], axis=3)
            bk, bv = (look_around(bk), look_around(bv))
            bt = jnp.arange(n).reshape(w, WINDOW)
            btp = jnp.pad(bt, ((1, 0), (0, 0)), constant_values=-1)
            btk = jnp.concatenate([btp[:w], btp[1:]], axis=1)
            sim = jnp.einsum('bhwid,bhwjd->bhwij', bq, bk)
            i = bt[:, :, None]
            j = btk[:, None, :]
            mask = (i < j) | (i > j + WINDOW) | (j == -1)
            sim = jnp.where(mask, -jnp.finfo(sim.dtype).max, sim)
            attn = jax.nn.softmax(sim, axis=-1)
            out = jnp.einsum('bhwij,bhwjd->bhwid', attn, bv)
            return out.reshape(b, h, n, d)

        def _layer(x, wqkv, qs, ksc, wo, lg, lb, w1, b1, w2, b2):
            b, n, _ = x.shape
            h = shift_token(x)
            qkv = h @ wqkv
            q, k, v = jnp.split(qkv, 3, axis=-1)
            to_heads = lambda t: t.reshape(b, n, HEADS, DIM_HEAD).transpose(0, 2, 1, 3)
            q, k, v = (to_heads(q), to_heads(k), to_heads(v))
            q = l2norm(q) * qs
            k = l2norm(k) * ksc
            q, k = rotary_xpos(q, k)
            o = local_attention(q, k, v)
            o = o.transpose(0, 2, 1, 3).reshape(b, n, INNER)
            x = x + o @ wo
            h = shift_token(x)
            mu = h.mean(-1, keepdims=True)
            var = h.var(-1, keepdims=True)
            h = (h - mu) / jnp.sqrt(var + 1e-05) * lg + lb
            h = h @ w1 + b1
            a, g = jnp.split(h, 2, axis=-1)
            h = a * jax.nn.gelu(g, approximate=False)
            x = x + h @ w2 + b2
            return x
        key = jax.random.key(seed)
        ks = jax.random.split(key, 6)
        return {'x': jax.random.normal(ks[0], (B, N, DIM), jnp.float32), 'wqkv': jax.random.normal(ks[1], (DEPTH, DIM, 3 * INNER), jnp.float32) * 0.02, 'q_scale': jnp.ones((DEPTH, DIM_HEAD), jnp.float32), 'k_scale': jnp.ones((DEPTH, DIM_HEAD), jnp.float32), 'wo': jax.random.normal(ks[2], (DEPTH, INNER, DIM), jnp.float32) * 0.02, 'ln_g': jnp.ones((DEPTH, DIM), jnp.float32), 'ln_b': jnp.zeros((DEPTH, DIM), jnp.float32), 'w1': jax.random.normal(ks[3], (DEPTH, DIM, 2 * HID), jnp.float32) * 0.02, 'b1': jnp.zeros((DEPTH, 2 * HID), jnp.float32), 'w2': jax.random.normal(ks[4], (DEPTH, HID, DIM), jnp.float32) * 0.02, 'b2': jnp.zeros((DEPTH, DIM), jnp.float32)}
    _L0_ffn_all = _L0_ffn_setup()
    _L0_ffn_in = {k: v for k, v in _L0_ffn_all.items() if k in ('wqkv', 'q_scale', 'k_scale', 'wo', 'ln_g', 'ln_b', 'w1', 'b1', 'w2', 'b2')}
    del _L0_ffn_all
    return {'x': x, 'ctx_1024': ctx_1024, 'mask_BxS2_bk1': mask_BxS2_bk1, 'L0_attn_W_Q': _L0_attn_in['W_Q'], 'L0_attn_W_K': _L0_attn_in['W_K'], 'L0_attn_W_V': _L0_attn_in['W_V'], 'L0_attn_W_O': _L0_attn_in['W_O'], 'L0_xattn_Wq': _L0_xattn_in['Wq'], 'L0_xattn_bq': _L0_xattn_in['bq'], 'L0_xattn_Wk': _L0_xattn_in['Wk'], 'L0_xattn_bk': _L0_xattn_in['bk'], 'L0_xattn_Wv': _L0_xattn_in['Wv'], 'L0_xattn_bv': _L0_xattn_in['bv'], 'L0_xattn_Wo': _L0_xattn_in['Wo'], 'L0_xattn_bo': _L0_xattn_in['bo'], 'L0_ffn_wqkv': _L0_ffn_in['wqkv'], 'L0_ffn_q_scale': _L0_ffn_in['q_scale'], 'L0_ffn_k_scale': _L0_ffn_in['k_scale'], 'L0_ffn_wo': _L0_ffn_in['wo'], 'L0_ffn_ln_g': _L0_ffn_in['ln_g'], 'L0_ffn_ln_b': _L0_ffn_in['ln_b'], 'L0_ffn_w1': _L0_ffn_in['w1'], 'L0_ffn_b1': _L0_ffn_in['b1'], 'L0_ffn_w2': _L0_ffn_in['w2'], 'L0_ffn_b2': _L0_ffn_in['b2']}

def reference(x, ctx_1024, mask_BxS2_bk1, L0_attn_W_Q, L0_attn_W_K, L0_attn_W_V, L0_attn_W_O, L0_xattn_Wq, L0_xattn_bq, L0_xattn_Wk, L0_xattn_bk, L0_xattn_Wv, L0_xattn_bv, L0_xattn_Wo, L0_xattn_bo, L0_ffn_wqkv, L0_ffn_q_scale, L0_ffn_k_scale, L0_ffn_wo, L0_ffn_ln_g, L0_ffn_ln_b, L0_ffn_w1, L0_ffn_b1, L0_ffn_w2, L0_ffn_b2):
    import jax
    import jax.numpy as jnp

    def _L0_attn_ref(x, W_Q, W_K, W_V, W_O):
        import jax, jax.numpy as jnp
        import numpy as np
        BATCH, SEQ, D_EMBED, N_HEADS, D_HEAD = (1, 512, 256, 16, 64)
        MASK_VAL = 10000000000.0
        q = jnp.einsum('ahe,bce->bach', W_Q, x)
        k = jnp.einsum('ahe,bce->bach', W_K, x)
        v = jnp.einsum('ahe,bce->bach', W_V, x)
        n = x.shape[1]
        scores = jnp.einsum('bach,baCh->bacC', k, q)
        causal = jnp.tril(jnp.ones((n, n), dtype=bool))
        masked = jnp.where(causal, scores, jnp.float32(-MASK_VAL))
        attn = jax.nn.softmax(masked / np.float32(np.sqrt(D_HEAD)), axis=-1)
        z = jnp.einsum('bacC,baCh->bach', attn, v)
        out = jnp.einsum('aeh,bach->bce', W_O, z)
        return out

    def _L0_xattn_ref(query, key, value, key_padding_mask, Wq, bq, Wk, bk, Wv, bv, Wo, bo):
        import jax, jax.numpy as jnp
        import numpy as np
        EPS = 1e-12

        def _l2_normalize(x, axis):
            n = jnp.sqrt(jnp.sum(x * x, axis=axis, keepdims=True))
            return x / jnp.maximum(n, EPS)
        b, n, d = query.shape
        h = 16
        dh = d // h
        q = query @ Wq.T + bq
        k = key @ Wk.T + bk
        v = value @ Wv.T + bv
        q = 1.0 + jax.nn.elu(q)
        k = 1.0 + jax.nn.elu(k)
        k = jnp.where(key_padding_mask[:, :, None], 0.0, k)
        q = q.reshape(b, n, h, dh).transpose(0, 2, 1, 3)
        k = k.reshape(b, n, h, dh).transpose(0, 2, 1, 3)
        v = v.reshape(b, n, h, dh).transpose(0, 2, 1, 3)
        q = _l2_normalize(q, axis=2)
        k = _l2_normalize(k, axis=3)
        kv = jnp.einsum('bhnd,bhne->bhde', k, v)
        out = jnp.einsum('bhnd,bhde->bhne', q, kv)
        out = out.transpose(0, 2, 1, 3).reshape(b, n, d)
        return out @ Wo.T + bo

    def _L0_ffn_ref(x, wqkv, q_scale, k_scale, wo, ln_g, ln_b, w1, b1, w2, b2):
        import jax, jax.numpy as jnp
        import numpy as np
        DIM = 256
        DEPTH = 2
        HEADS = 8
        DIM_HEAD = 64
        WINDOW = 128
        INNER = HEADS * DIM_HEAD
        HID = int(DIM * 4 * 2 / 3)
        B, N = (2, 2048)
        QK_SCALE = 8.0

        def shift_token(t):
            t1, t2 = jnp.split(t, 2, axis=-1)
            t2 = jnp.pad(t2, ((0, 0), (1, 0), (0, 0)))[:, :-1]
            return jnp.concatenate([t1, t2], axis=-1)

        def l2norm(t):
            return t / jnp.clip(jnp.linalg.norm(t, axis=-1, keepdims=True), 1e-12)

        def rotate_half(x):
            x1, x2 = jnp.split(x, 2, axis=-1)
            return jnp.concatenate([-x2, x1], axis=-1)

        def rotary_xpos(q, k):
            n = q.shape[-2]
            half_idx = jnp.arange(0, DIM_HEAD, 2, dtype=jnp.float32)
            inv_freq = 1.0 / 10000.0 ** (half_idx / DIM_HEAD)
            t = jnp.arange(n, dtype=jnp.float32)
            freqs = t[:, None] * inv_freq[None, :]
            freqs = jnp.concatenate([freqs, freqs], axis=-1)
            base = (half_idx + 0.4 * DIM_HEAD) / (1.4 * DIM_HEAD)
            power = (t - n // 2) / float(WINDOW // 2)
            scale = base[None, :] ** power[:, None]
            scale = jnp.concatenate([scale, scale], axis=-1)
            cos, sin = (jnp.cos(freqs), jnp.sin(freqs))
            q = q * cos * scale + rotate_half(q) * sin * scale
            k = k * cos / scale + rotate_half(k) * sin / scale
            return (q, k)

        def local_attention(q, k, v):
            b, h, n, d = q.shape
            w = n // WINDOW
            bq = q.reshape(b, h, w, WINDOW, d) * QK_SCALE
            bk = k.reshape(b, h, w, WINDOW, d)
            bv = v.reshape(b, h, w, WINDOW, d)

            def look_around(t):
                p = jnp.pad(t, ((0, 0), (0, 0), (1, 0), (0, 0), (0, 0)))
                return jnp.concatenate([p[:, :, :w], p[:, :, 1:]], axis=3)
            bk, bv = (look_around(bk), look_around(bv))
            bt = jnp.arange(n).reshape(w, WINDOW)
            btp = jnp.pad(bt, ((1, 0), (0, 0)), constant_values=-1)
            btk = jnp.concatenate([btp[:w], btp[1:]], axis=1)
            sim = jnp.einsum('bhwid,bhwjd->bhwij', bq, bk)
            i = bt[:, :, None]
            j = btk[:, None, :]
            mask = (i < j) | (i > j + WINDOW) | (j == -1)
            sim = jnp.where(mask, -jnp.finfo(sim.dtype).max, sim)
            attn = jax.nn.softmax(sim, axis=-1)
            out = jnp.einsum('bhwij,bhwjd->bhwid', attn, bv)
            return out.reshape(b, h, n, d)

        def _layer(x, wqkv, qs, ksc, wo, lg, lb, w1, b1, w2, b2):
            b, n, _ = x.shape
            h = shift_token(x)
            qkv = h @ wqkv
            q, k, v = jnp.split(qkv, 3, axis=-1)
            to_heads = lambda t: t.reshape(b, n, HEADS, DIM_HEAD).transpose(0, 2, 1, 3)
            q, k, v = (to_heads(q), to_heads(k), to_heads(v))
            q = l2norm(q) * qs
            k = l2norm(k) * ksc
            q, k = rotary_xpos(q, k)
            o = local_attention(q, k, v)
            o = o.transpose(0, 2, 1, 3).reshape(b, n, INNER)
            x = x + o @ wo
            h = shift_token(x)
            mu = h.mean(-1, keepdims=True)
            var = h.var(-1, keepdims=True)
            h = (h - mu) / jnp.sqrt(var + 1e-05) * lg + lb
            h = h @ w1 + b1
            a, g = jnp.split(h, 2, axis=-1)
            h = a * jax.nn.gelu(g, approximate=False)
            x = x + h @ w2 + b2
            return x
        for l in range(DEPTH):
            x = _layer(x, wqkv[l], q_scale[l], k_scale[l], wo[l], ln_g[l], ln_b[l], w1[l], b1[l], w2[l], b2[l])
        return x
    x = x + _L0_attn_ref(_layernorm(x, axis=-1), L0_attn_W_Q, L0_attn_W_K, L0_attn_W_V, L0_attn_W_O)
    x = x + _L0_xattn_ref(_layernorm(x, axis=-1), ctx_1024, ctx_1024, mask_BxS2_bk1, L0_xattn_Wq, L0_xattn_bq, L0_xattn_Wk, L0_xattn_bk, L0_xattn_Wv, L0_xattn_bv, L0_xattn_Wo, L0_xattn_bo)
    x = x + _L0_ffn_ref(_layernorm(x, axis=-1), L0_ffn_wqkv, L0_ffn_q_scale, L0_ffn_k_scale, L0_ffn_wo, L0_ffn_ln_g, L0_ffn_ln_b, L0_ffn_w1, L0_ffn_b1, L0_ffn_w2, L0_ffn_b2)
    return x

_drawn_inputs = setup_inputs


def setup_inputs(seed=0):
    import zlib

    import numpy as np

    out = dict(_drawn_inputs(seed))
    spreads = {'L0_ffn_q_scale': (1.0, 0.6),
     'L0_ffn_k_scale': (1.0, 0.6),
     'L0_ffn_ln_g': (1.0, 0.6),
     'L0_ffn_ln_b': (0.0, 0.8),
     'L0_ffn_b1': (0.0, 0.8),
     'L0_ffn_b2': (0.0, 0.1)}
    factors = {'L0_xattn_bq': 64.0, 'L0_xattn_Wk': 7.982, 'L0_xattn_bk': 64.0, 'L0_xattn_bo': 3.539}
    for name, (base, spread) in spreads.items():
        noise = np.random.default_rng([zlib.crc32(name.encode()), seed]).standard_normal(out[name].shape)
        drawn = base * np.exp(spread * noise) if base else spread * noise
        out[name] = jnp.asarray(drawn.astype(out[name].dtype))
    for name, factor in factors.items():
        out[name] = (out[name] * factor).astype(out[name].dtype)
    return out
```

```python
from contextlib import ExitStack

import numpy as np

import concourse.bass as bass
from concourse import mybir

F32 = mybir.dt.float32
U8 = mybir.dt.uint8
ALU = mybir.AluOpType
ACT = mybir.ActivationFunctionType
AX = mybir.AxisListType

P = 128
B, S, D = 4, 512, 256
T = S // P
E2 = D // P
AH, ADH = 16, 64
PAIRS = AH // 2
XH, XDH = 16, 16
DEPTH, FH, FDH = 2, 8, 64
INNER = FH * FDH
FPAIRS = FH // 2
HID = int(D * 4 * 2 / 3)
NF = 6
FT = -(-HID // NF)
FL = HID - FT * (NF - 1)
W = 128
QK_SCALE = 8.0
NEG = -1e30
LN_EPS = 1e-5
NORM_EPS = 1e-12
TRI = [P * (i + 1) for i in range(T)]
TRI_AT = [sum(TRI[:i]) for i in range(T + 1)]
KEYB = [S - P * j for j in range(T)]
KEYB_AT = [0, 512, 1024, 896]
T_TILES = ((0,), (1, 3), (2,))
LOC = 2 * P
LOC_N = P + LOC * (T - 1)
GELU_T = 2


def loc_at(w):
    return 0 if w == 0 else P + LOC * (w - 1)


def constants():
    ident = np.eye(P, dtype=np.float32)
    i = np.arange(P)[:, None]
    j = np.arange(P)[None, :]
    causal = np.zeros((P, S), np.float32)
    causal[:, S - P:] = np.where(j <= i, 0.0, NEG)
    local = np.concatenate([np.where(i <= j, 0.0, NEG), np.where(j <= i, 0.0, NEG)], 1).astype(np.float32)
    heads = (i // XDH == j // XDH).astype(np.float32)
    half = np.arange(0, FDH, 2, dtype=np.float32)
    inv_freq = (1.0 / np.float32(10000.0) ** (half / np.float32(FDH))).astype(np.float32)
    t = np.arange(S, dtype=np.float32)
    freqs = t[:, None] * inv_freq[None, :]
    freqs = np.concatenate([freqs, freqs], -1)
    base = ((half + np.float32(0.4 * FDH)) / np.float32(1.4 * FDH)).astype(np.float32)
    power = ((t - S // 2) / np.float32(W // 2)).astype(np.float32)
    scale = (base[None, :] ** power[:, None]).astype(np.float32)
    scale = np.concatenate([scale, scale], -1)
    cos, sin = np.cos(freqs), np.sin(freqs)
    sign = np.where(np.arange(FDH) < FDH // 2, -1.0, 1.0).astype(np.float32)
    rot = np.stack([cos * scale, sin * sign * scale, cos / scale, sin * sign / scale])
    rot = rot.reshape(4, T, P, FDH).transpose(2, 0, 1, 3).astype(np.float32)
    return {"c_ident": ident, "c_causal": causal, "c_local": local, "c_heads": heads,
            "c_rot": np.ascontiguousarray(rot)}


def build(nc, a, out, x2_dram):
    with ExitStack() as ctx:
        def sem(name):
            return ctx.enter_context(nc.semaphore(name))

        def sbt(stack, name, shape, dt=F32):
            return stack.enter_context(nc.sbuf_tensor(name, shape, dt))

        psum = [ctx.enter_context(nc.psum_tensor(f"psum{i}", [P, 512], F32)) for i in range(8)]
        full = [sem(f"full{i}") for i in range(8)]
        read = [sem(f"read{i}") for i in range(8)]

        ident = sbt(ctx, "ident", [P, P])
        causal = sbt(ctx, "causal", [P, S])
        local = sbt(ctx, "local", [P, LOC])
        neg_half = sbt(ctx, "neg_half", [P, 16])
        y = sbt(ctx, "y", [P, B, T, D])
        wqkv = sbt(ctx, "wqkv", [P, E2, 3 * INNER])
        wo = sbt(ctx, "wo", [P, FPAIRS, D])
        w1 = sbt(ctx, "w1", [P, E2, 2 * HID])
        stats = sbt(ctx, "stats", [P, 2, T, 12])
        mv = sbt(ctx, "mv", [P, 2, T, 2])
        rstd = sbt(ctx, "rstd", [P, 2, T])

        ab = ExitStack()
        x = sbt(ab, "x", [P, B, T, D])
        xnT = sbt(ab, "xnT", [P, E2, B, S])
        woT = sbt(ab, "woT", [P, PAIRS, D])
        xwq = sbt(ab, "xwq", [P, E2, D])
        xwkv = sbt(ab, "xwkv", [P, E2, 2 * D])
        xwo = sbt(ab, "xwo", [P, E2, D])
        xbkv = sbt(ab, "xbkv", [P, 2 * D])
        xbo = sbt(ab, "xbo", [P, D])
        xbq = sbt(ab, "xbq", [P, E2])
        xmask = sbt(ab, "xmask", [P, B, T], U8)
        xkeep = sbt(ab, "xkeep", [P, B, T])
        heads = sbt(ab, "heads", [P, P])
        r1 = ExitStack()
        rowmax = sbt(r1, "rowmax", [P, 2, 2, T])
        negmax = sbt(r1, "negmax", [P, 2, 2, T])
        den = sbt(r1, "den", [P, 2, 2, T])
        rden = sbt(r1, "rden", [P, 2, 2, T])
        qz = sbt(r1, "qz", [P, 2, S])
        wst = sbt(r1, "wst", [P, 3, E2, P])
        kT = sbt(r1, "kT", [P, S])
        v = sbt(r1, "v", [P, 2, T, P])
        pT = sbt(r1, "pT", [P, 2, TRI_AT[T]])
        probs = sbt(r1, "probs", [P, 2, 2, TRI_AT[T]])
        r1.close()
        r1 = ExitStack()
        ctxT = sbt(r1, "ctxT", [P, E2, B, S])
        kv = sbt(r1, "kv", [P, 2, T, 2 * D])
        xn = sbt(r1, "xn", [P, 2, T, D])
        r1.close()
        hold = sbt(ab, "hold", [P, 11136])
        r2 = ExitStack()
        zT = sbt(r2, "zT", [P, PAIRS, B, S])
        r2.close()
        r2 = ExitStack()
        kf = sbt(r2, "kf", [P, 2, T, D])
        ktmp = sbt(r2, "ktmp", [P, T, D])
        knorm = sbt(r2, "knorm", [P, 2, T, XH])
        kvm = sbt(r2, "kvm", [P, B, E2, P])
        kvs = sbt(r2, "kvs", [P, 2, E2, P])
        qm = sbt(r2, "qm", [P, E2, S])
        qr = sbt(r2, "qr", [P, E2, S])
        qT = sbt(r2, "qT", [P, 2, E2, S])
        qss = sbt(r2, "qss", [P, 2, E2])
        oxT = sbt(r2, "oxT", [P, 2, E2, S])
        r2.close()
        ab.close()

        w2 = sbt(ctx, "w2", [FT, NF, D])
        rot = sbt(ctx, "rot", [P, 4, T, FDH])
        qk_scale = sbt(ctx, "qk_scale", [P, 2, FDH])
        tab = sbt(ctx, "tab", [P, 4, T, FDH])
        lng = sbt(ctx, "lng", [P, E2])
        lnb = sbt(ctx, "lnb", [P, E2])
        b1 = sbt(ctx, "b1", [FT, 2, NF])
        b2 = sbt(ctx, "b2", [P, D])
        hT = sbt(ctx, "hT", [P, E2, S + 1])
        sq = sbt(ctx, "sq", [P, 2, INNER])
        ra = sbt(ctx, "ra", [P, 2, INNER])
        rb = sbt(ctx, "rb", [P, 2, INNER])
        ss = sbt(ctx, "ss", [P, 2, FH])
        rn = sbt(ctx, "rn", [P, 2, T, 2, FH])
        lqz = sbt(ctx, "lqz", [P, 2, FPAIRS, 2, S])
        lkT = sbt(ctx, "lkT", [P, 2, FPAIRS, S])
        lv = sbt(ctx, "lv", [P, 2, T, INNER])
        lp = sbt(ctx, "lp", [P, 2, 2, LOC_N])
        lpT = sbt(ctx, "lpT", [P, 2, LOC_N])
        lmax = sbt(ctx, "lmax", [P, 2, 2, T])
        lneg = sbt(ctx, "lneg", [P, 2, 2, T])
        lden = sbt(ctx, "lden", [P, 2, 2, T])
        lrden = sbt(ctx, "lrden", [P, 2, 2, T])
        loT = sbt(ctx, "loT", [P, FPAIRS, S])
        hs = sbt(ctx, "hs", [P, T, P])
        hn = sbt(ctx, "hn", [P, T, D])
        hnT = sbt(ctx, "hnT", [P, E2, S])
        gl = sbt(ctx, "gl", [FT, GELU_T, S])
        hid = sbt(ctx, "hid", [FT, NF, S])

        ld_const, ld_xw, ld_wo = sem("ld_const"), sem("ld_xw"), sem("ld_wo")
        ld_ctx = [sem(f"ld_ctx{b}") for b in range(B)]
        ld_x = [sem(f"ld_x{b}") for b in range(B)]
        ld_qk, ld_v = sem("ld_qk"), sem("ld_v")
        set0 = sem("set0")
        ln_stats, ln_mv = sem("ln_stats"), sem("ln_mv")
        ln_eps, ln_rstd = sem("ln_eps"), sem("ln_rstd")
        ln_done = sem("ln_done")
        s_neg, s_rden = sem("s_neg"), sem("s_rden")
        s_exp, s_prob = sem("s_exp"), sem("s_prob")
        k_keep, k_min, k_fin, k_ss, k_rec, k_done = (
            sem(n) for n in ("k_keep", "k_min", "k_fin", "k_ss", "k_rec", "k_done"))
        k_exp, k_sq, k_sqrt = sem("k_exp"), sem("k_sq"), sem("k_sqrt")
        q_relu, q_exp, q_sq = sem("q_relu"), sem("q_exp"), sem("q_sq")
        q_fin, q_max, kvs_done = sem("q_fin"), sem("q_max"), sem("kvs_done")
        q_rn, bo_done = sem("q_rn"), sem("bo_done")
        x2_st = sem("x2_st")
        ld_rot, ld_small, ld_wqkv, ld_lwo, ld_w1, ld_w2 = (
            sem(n) for n in ("ld_rot", "ld_small", "ld_wqkv", "ld_lwo", "ld_w1", "ld_w2"))
        set1 = sem("set1")
        l_tab, l_ss, l_ssm, l_neg, l_rden = (
            sem(n) for n in ("l_tab", "l_ss", "l_ssm", "l_neg", "l_rden"))
        l_sq, l_exp = sem("l_sq"), sem("l_exp")
        l_q, l_kadd, l_rn, l_k, l_prob = (sem(n) for n in ("l_q", "l_kadd", "l_rn", "l_k", "l_prob"))
        hs_ld = sem("hs_ld")
        f_stats, f_mv, f_hn = sem("f_stats"), sem("f_mv"), sem("f_hn")
        f_eps, f_rstd, f_b2 = sem("f_eps"), sem("f_rstd"), sem("f_b2")
        x2_ld = [sem(f"x2_ld{b}") for b in range(B)]
        fin_done, out_st = sem("fin_done"), sem("out_st")
        passed_v, passed_p = sem("passed_v"), sem("passed_p")

        NU = PAIRS * B

        def use_s(u, h, k):
            return k, 2 * u + h

        def use_x(b, e):
            return (3, b) if e == 0 else (4 + b % 2, b // 2)

        def use_t(u, h, k):
            n = 3 * h + k
            return 3 + n % 2, 3 * u + n // 2 + (B // 2 if n % 2 else B)

        def use_z(u):
            return 5, u + B // 2

        def use_q(u):
            return 6, 2 * u

        def use_v(u):
            return 6, 2 * u + 1

        def use_k(u):
            return 7, u

        count = [2 * NU] * 3 + [B + 3 * NU, B // 2 + 3 * NU, B // 2 + NU, 2 * NU, NU]
        plan = {}

        def take(key, bank):
            plan[key] = (bank, count[bank])
            count[bank] += 1

        for b in range(B):
            for tp in range(2):
                take(("wo", b, tp), (2 * b + tp) % 3)
        for b in range(B):
            for t in range(T):
                take(("kv", b, t), 5 + (T * b + t) % 3)
            take(("x1T", b, 0), 3)
            take(("x1T", b, 1), 4)
            if b:
                take(("KV", b - 1), 2)
        take(("KV", B - 1), 2)
        for s in range(B + 2):
            if s < B:
                take(("xq", s, 0), 0)
                take(("xq", s, 1), 1)
            if 1 <= s <= B:
                take(("xo", s - 1, 0), 2)
                take(("xo", s - 1, 1), 5)
            if s >= 2:
                take(("xw", s - 2, 0), 6)
                take(("xw", s - 2, 1), 7)
        base = list(count)

        NLU = B * FPAIRS
        count = [0] * 8
        turns = {"g": 0, "t": 0}
        banks = {"g": (2, 6, 7), "t": (3, 4)}

        def turn(key, which):
            take(key, banks[which][turns[which] % len(banks[which])])
            turns[which] += 1

        def plan_q(b, t):
            if t == 0:
                turn(("hT", b, 0), "t")
                turn(("hT", b, 1), "t")
            for what in "vqk":
                turn((what, b, t), "g")

        def plan_tqk(b, t):
            turn(("Tq", b, t), "t")
            turn(("Tk", b, t), "t")

        def plan_s(u):
            for h in range(2):
                take(("S", u, h, 0), 0)
                take(("S", u, h, 1), 1)

        def plan_mlp(b, j):
            if j == 0:
                turn(("lwo", b, 0), "g")
                turn(("lwo", b, 1), "g")
            if j == 1:
                turn(("hnT", b, 0), "t")
                turn(("hnT", b, 1), "t")
            if j in (1, 2):
                for f in range(3 * (j - 1), 3 * j):
                    turn(("w1g", b, f), "g")
                    turn(("w1a", b, f), "g")
            if j == 3:
                turn(("w2", b, 0), "g")
                turn(("w2", b, 1), "g")

        for t in range(T):
            plan_q(0, t)
            if t:
                plan_tqk(0, t - 1)
        plan_tqk(0, T - 1)
        plan_s(0)
        for b in range(B):
            for j in range(FPAIRS):
                u = b * FPAIRS + j
                if b + 1 < B:
                    plan_q(b + 1, j)
                if b:
                    plan_mlp(b - 1, j)
                for h in range(2):
                    turn(("T", u, h, 0), "t")
                    turn(("T", u, h, 1), "t")
                if b + 1 < B:
                    plan_tqk(b + 1, j)
                take(("O", u), 5)
                if u + 1 < NLU:
                    plan_s(u + 1)
        for j in range(FPAIRS):
            plan_mlp(B - 1, j)
        per_layer = list(count)

        def lay(key, l):
            bank, n = plan[key]
            return bank, l * per_layer[bank] + (base[bank] + n)

        def wait_free(pe, use):
            bank, n = use
            if not (isinstance(n, int) and n == 0):
                pe.wait_ge(read[bank], n)
            return psum[bank]

        def wait_full(eng, use):
            bank, n = use
            eng.wait_ge(full[bank], n + 1)
            return psum[bank]

        def wait_read(eng, use):
            bank, n = use
            eng.wait_ge(read[bank], n + 1)

        def pass_wait(eng, passed):
            eng.sem_inc(passed, 1)

        def frows(f):
            return FT if f < NF - 1 else FL

        def x2_back(b):
            flat = lqz[:, b // 2, 2 * (b % 2):2 * (b % 2) + 2, :, :].rearrange("p a h s -> p (a h s)")
            return flat[:, 0:T * D].rearrange("p (t e) -> p t e", e=D)

        block = ctx.enter_context(nc.Block())

        @block.sync
        def _(sp):
            for name, t in (("c_ident", ident), ("c_causal", causal), ("c_local", local)):
                sp.dma_start(t[:, :], a[name]).then_inc(ld_const, 16)
            for b in range(B):
                sp.dma_start(x[:, b, :, :], a["x"][b].rearrange("(t p) e -> p t e", p=P)).then_inc(ld_x[b], 16)
            sp.dma_start(wst[:, 0:2], a["w_pairs"][0, :, 0:2]).then_inc(ld_qk, 16)
            sp.dma_start(wst[:, 2], a["w_pairs"][0, :, 2]).then_inc(ld_v, 16)
            sp.dma_start(woT[:, :, :], a["attn_wo"].rearrange("(k p) e -> p k e", p=P)).then_inc(ld_wo, 16)
            for t, src in ((xwq, "xwq"), (xwkv, "xwkv"), (xwo, "xwo")):
                sp.dma_start(t[:, :, :], a[src].rearrange("(k p) e -> p k e", p=P)).then_inc(ld_xw, 16)
            sp.dma_start(xbkv[:, :], a["xbkv"].partition_broadcast(P)).then_inc(ld_xw, 16)
            sp.dma_start(xbo[:, :], a["xbo"].partition_broadcast(P)).then_inc(ld_xw, 16)
            sp.dma_start(xbq[:, :], a["xbq"]).then_inc(ld_xw, 16)
            sp.dma_start(xmask[:, :, :], a["mask"]).then_inc(ld_xw, 16)
            sp.dma_start(heads[:, :], a["c_heads"]).then_inc(ld_xw, 16)

            def layer_qkv_weights(l):
                sp.dma_start(wqkv[:, :, :], a["wqkv"][l].rearrange("(k p) c -> p k c", p=P)).then_inc(ld_wqkv, 16)

            def layer_mlp_weights(l):
                sp.dma_start(wo[:, :, :], a["wo"][l].rearrange("(k p) c -> p k c", p=P)).then_inc(ld_lwo, 16)
                sp.dma_start(w1[:, :, :], a["w1"][l].rearrange("(k p) c -> p k c", p=P)).then_inc(ld_w1, 16)

            def layer_w2(l):
                main = a["w2"][l, 0:FT * (NF - 1), :].rearrange("(k p) c -> p k c", p=FT)
                sp.dma_start(w2[:, 0:NF - 1, :], main).then_inc(ld_w2, 16)
                sp.dma_start(w2[0:FL, NF - 1, :], a["w2"][l, FT * (NF - 1):HID, :]).then_inc(ld_w2, 16)

            def layer_small(l):
                sp.dma_start(qk_scale[:, 0, :], a["q_scale"][l].partition_broadcast(P)).then_inc(ld_small, 16)
                sp.dma_start(qk_scale[:, 1, :], a["k_scale"][l].partition_broadcast(P)).then_inc(ld_small, 16)
                sp.dma_start(lng[:, :], a["ln_g"][l]).then_inc(ld_small, 16)
                sp.dma_start(lnb[:, :], a["ln_b"][l]).then_inc(ld_small, 16)
                sp.dma_start(b1[:, :, :], a["b1"][l]).then_inc(ld_small, 16)
                sp.dma_start(b2[:, :], a["b2"][l].partition_broadcast(P)).then_inc(ld_small, 16)

            layer_qkv_weights(0)
            layer_mlp_weights(0)
            with sp.Fori(1, PAIRS) as p:
                wait_full(sp, use_k(p * B - 1))
                sp.dma_start(wst[:, 0:2], a["w_pairs"][p, :, 0:2]).then_inc(ld_qk, 16)
                wait_full(sp, use_v(p * B - 1))
                sp.dma_start(wst[:, 2], a["w_pairs"][p, :, 2]).then_inc(ld_v, 16)
            wait_full(sp, use_z(NU - 1))
            for b in range(B):
                sp.dma_start(ctxT[:, :, b, :], a["ctxT"][b].rearrange("(k p) s -> p k s", p=P)).then_inc(ld_ctx[b], 16)
            for b in range(B):
                wait_read(sp, plan["xw", b, 0])
                wait_read(sp, plan["xw", b, 1])
                sp.dma_start(x2_dram[b].rearrange("(t p) e -> p t e", p=P), x[:, b, :, :]).then_inc(x2_st, 16)
            sp.wait_ge(ln_done, 3 * B)
            sp.wait_ge(x2_st, 16 * B)
            sp.dma_start(rot[:, :, :, :], a["c_rot"]).then_inc(ld_rot, 16)
            layer_small(0)
            layer_w2(0)
            sp.wait_ge(set1, 3)
            for l in range(DEPTH):
                for b in range(B):
                    wait_read(sp, lay(("lwo", b, 0), l))
                    wait_read(sp, lay(("lwo", b, 1), l))
                    if l or b:
                        sp.wait_ge(f_hn, l * B + b)
                    sp.dma_start(hs[1:P, :, :], y[0:P - 1, b, :, P:D]).then_inc(hs_ld, 16)
                    sp.dma_start(hs[0:1, 1:T, :], y[P - 1:P, b, 0:T - 1, P:D]).then_inc(hs_ld, 16)
                    if b == B - 1 and l + 1 < DEPTH:
                        wait_full(sp, lay(("k", B - 1, T - 1), l))
                        layer_qkv_weights(l + 1)
                        wait_full(sp, lay(("w2", B - 1, 0), l))
                        wait_full(sp, lay(("w2", B - 1, 1), l))
                        layer_mlp_weights(l + 1)
                        layer_w2(l + 1)
                        sp.wait_ge(f_b2, (l + 1) * B)
                        layer_small(l + 1)
            for h in range(2):
                wait_full(sp, lay(("S", NLU - 1, 1, h), DEPTH - 1))
            for b in range(B):
                sp.dma_start(x2_back(b), x2_dram[b].rearrange("(t p) e -> p t e", p=P)).then_inc(x2_ld[b], 16)
            for b in range(B):
                sp.wait_ge(fin_done, b + 1)
                sp.dma_start(out[b].rearrange("(t p) e -> p t e", p=P), y[:, b, :, :]).then_inc(out_st, 16)
            sp.wait_ge(out_st, 16 * B)

        @block.gpsimd
        def _(pool):
            pool.memset(neg_half[:, :], -0.5).then_inc(set0, 1)
            pool.memset(qz[:, :, :], 0.0).then_inc(set0, 1)
            pool.wait_ge(set0, 1)

            def norm_rstd(n):
                pool.wait_ge(ln_mv, T * (n + 1))
                pool.tensor_scalar(rstd[:, n % 2, :], mv[:, n % 2, :, 1], LN_EPS, None, ALU.add).then_inc(ln_eps, 1)
                pool.wait_ge(ln_eps, n + 1)
                pool.tensor_tensor(rstd[:, n % 2, :], rstd[:, n % 2, :], neg_half[:, 0:T], ALU.pow)\
                    .then_inc(ln_rstd, 1)

            for b in range(B):
                norm_rstd(b)

            def probabilities(u, j):
                for h in range(2):
                    pool.wait_ge(s_rden, 2 * u + (h + 1))
                    for i in range(T):
                        pr = probs[:, j % 2, h, TRI_AT[i]:TRI_AT[i + 1]]
                        ins = pool.tensor_tensor(pr, pr, rden[:, j % 2, h, i:i + 1].broadcast_to([P, TRI[i]]),
                                                 ALU.mult)
                    ins.then_inc(s_prob, 1)

            with pool.Fori(0, PAIRS) as p:
                for j in range(B):
                    probabilities(p * B + j, j)

            pool.wait_ge(ld_xw, 16 * 8)
            for b in range(B):
                norm_rstd(B + b)
                pool.wait_ge(ln_done, B + b + 1)
                for t in range(T):
                    ins = pool.tensor_tensor(x[:, b, t, :], x[:, b, t, :], xbo[:, :], ALU.add)
                ins.then_inc(bo_done, 1)
            for s in range(B + 2):
                if s < B:
                    pool.wait_ge(q_max, s + 1)
                    pool.tensor_tensor(qss[:, s % 2, :], qss[:, s % 2, :], neg_half[:, 0:E2], ALU.pow)\
                        .then_inc(q_rn, 1)
                if s >= 2:
                    norm_rstd(2 * B + s - 2)

            pool.wait_ge(ln_done, 3 * B)
            pool.wait_ge(x2_st, 16 * B)
            pool.memset(lqz[:, :, :, :, :], 0.0).then_inc(set1, 1)
            pool.memset(hT[:, 1, 0:1], 0.0).then_inc(set1, 1)
            pool.memset(hs[0:1, 0, :], 0.0).then_inc(set1, 1)

            def local_probabilities(u, l):
                for h in range(2):
                    pool.wait_ge(l_rden, l * (2 * NLU) + (2 * u + h + 1))
                    pr = lp[:, u % 2, h, 0:P]
                    pool.tensor_tensor(pr, pr, lrden[:, u % 2, h, 0:1].broadcast_to([P, P]), ALU.mult)
                    pr = lp[:, u % 2, h, P:LOC_N].rearrange("p (w c) -> p w c", c=LOC)
                    r = lrden[:, u % 2, h, 1:T].rearrange("p (w o) -> p w o", o=1).broadcast_to([P, T - 1, LOC])
                    pool.tensor_tensor(pr, pr, r, ALU.mult).then_inc(l_prob, 1)

            def rotate(b, t, l):
                n = T * b + t + 1
                wait_read(pool, lay(("q", b, t), l))
                pool.tensor_tensor(ra[:, 0, :], ra[:, 0, :], rb[:, 0, :], ALU.add).then_inc(l_q, 1)
                wait_read(pool, lay(("k", b, t), l))
                pool.tensor_tensor(ra[:, 1, :], ra[:, 1, :], rb[:, 1, :], ALU.add).then_inc(l_kadd, 1)
                pool.wait_ge(l_ssm, l * (2 * B * T) + 2 * n)
                pool.tensor_tensor(rn[:, b % 2, t, :, :], ss[:, :, :],
                                   neg_half[:, 0:2 * FH].rearrange("p (a h) -> p a h", a=2), ALU.pow)\
                    .then_inc(l_rn, 1)
                pool.wait_ge(l_rn, l * (B * T) + n)
                pool.wait_ge(l_kadd, l * (B * T) + n)
                k3 = ra[:, 1, :].rearrange("p (h d) -> p h d", d=FDH)
                r = rn[:, b % 2, t, 1, :].rearrange("p (h o) -> p h o", o=1).broadcast_to([P, FH, FDH])
                pool.tensor_tensor(k3, k3, r, ALU.mult).then_inc(l_k, 1)

            def mlp_rstd(b, l):
                n = b + 1
                pool.wait_ge(f_mv, l * (T * B) + T * n)
                pass_wait(pool, passed_p)
                pool.tensor_scalar(rstd[:, 0, :], mv[:, 0, :, 1], LN_EPS, None, ALU.add).then_inc(f_eps, 1)
                pool.wait_ge(f_eps, l * B + n)
                pool.tensor_tensor(rstd[:, 0, :], rstd[:, 0, :], neg_half[:, 0:T], ALU.pow).then_inc(f_rstd, 1)

            def mlp_bias(b, l):
                pool.wait_ge(f_hn, l * B + (b + 1))
                for t in range(T):
                    ins = pool.tensor_tensor(y[:, b, t, :], y[:, b, t, :], b2[:, :], ALU.add)
                ins.then_inc(f_b2, 1)

            with pool.Fori(0, DEPTH) as l:
                pool.wait_ge(ld_small, l * (16 * 6) + 16 * 6)
                for t in range(T):
                    rotate(0, t, l)
                for b in range(B):
                    for j in range(FPAIRS):
                        if b and j == 1:
                            mlp_rstd(b - 1, l)
                        local_probabilities(b * FPAIRS + j, l)
                        if b + 1 < B:
                            rotate(b + 1, j, l)
                        if b and j == 1:
                            mlp_bias(b - 1, l)
                mlp_rstd(B - 1, l)
                mlp_bias(B - 1, l)

        @block.scalar
        def _(act):
            def copy(dst, src):
                return act.activation(dst, src, ACT.Copy)

            for b in range(B):
                for e in range(E2):
                    bank = wait_full(act, use_x(b, e))
                    copy(xnT[:, e, b, :], bank[:, :]).then_inc(read[use_x(b, e)[0]], 1)

            def evac_q(u):
                bank = wait_full(act, use_q(u))
                copy(qz[0:ADH, 0, :], bank[0:ADH, :])
                copy(qz[ADH:P, 1, :], bank[ADH:P, :]).then_inc(read[6], 1)

            def evac_v(u, j):
                bank = wait_full(act, use_v(u))
                copy(v[:, j % 2, :, :], bank[:, :].rearrange("p (t c) -> p t c", c=P)).then_inc(read[6], 1)

            def exponentials(u, j):
                for h in range(2):
                    act.wait_ge(s_neg, 2 * u + (h + 1))
                    for i in range(T):
                        pr = probs[:, j % 2, h, TRI_AT[i]:TRI_AT[i + 1]]
                        ins = act.activation(pr, pr, ACT.Exp, bias=negmax[:, j % 2, h, i:i + 1], scale=ADH ** -0.5,
                                             accum_out=den[:, j % 2, h, i:i + 1])
                    ins.then_inc(s_exp, 1)

            def evac_pT(u, n):
                h, k = divmod(n, 3)
                bank = wait_full(act, use_t(u, h, k))
                at = KEYB_AT[T_TILES[k][0]]
                w = sum(KEYB[j] for j in T_TILES[k])
                copy(pT[:, h, at:at + w], bank[:, 0:w]).then_inc(read[use_t(u, h, k)[0]], 1)

            def slot(u, j, ahead):
                if ahead >= 1:
                    exponentials(u + 1, j + 1)
                if ahead >= 2:
                    evac_q(u + 2)
                for n in (1, 3, 5):
                    evac_pT(u, n)
                if ahead >= 2:
                    evac_v(u + 2, j)

            act.wait_ge(set0, 2)
            evac_q(0)
            evac_v(0, 0)
            exponentials(0, 0)
            evac_q(1)
            evac_v(1, 1)
            with act.Fori(0, PAIRS - 1) as p:
                for j in range(B):
                    slot(p * B + j, j, 2)
            for j in range(B):
                slot(NU - B + j, j, B - 1 - j)

            for b in range(B):
                for e in range(E2):
                    bank = wait_full(act, plan["x1T", b, e])
                    copy(xnT[:, e, b, :], bank[:, :]).then_inc(read[plan["x1T", b, e][0]], 1)
                act.wait_ge(k_min, b + 1)
                act.activation(ktmp[:, :, :], ktmp[:, :, :], ACT.Exp).then_inc(k_exp, 1)
                act.wait_ge(k_fin, b + 1)
                act.activation(ktmp[:, :, :], kf[:, b % 2, :, :], ACT.Square).then_inc(k_sq, 1)
                act.wait_ge(k_ss, b + 1)
                act.activation(knorm[:, b % 2, :, :], knorm[:, b % 2, :, :], ACT.Sqrt).then_inc(k_sqrt, 1)
            for s in range(B + 1):
                if s < B:
                    for e in range(E2):
                        bank = wait_full(act, plan["xq", s, e])
                        act.activation(qr[:, e, :], bank[:, :], ACT.Relu, bias=xbq[:, e:e + 1]).then_inc(q_relu, 1)
                    for e in range(E2):
                        wait_read(act, plan["xq", s, e])
                        act.activation(qm[:, e, :], qm[:, e, :], ACT.Exp).then_inc(q_exp, 1)
                    for e in range(E2):
                        act.wait_ge(q_fin, 2 * s + e + 1)
                        act.activation(qm[:, e, :], qT[:, s % 2, e, :], ACT.Square,
                                       accum_out=qss[:, s % 2, e:e + 1]).then_inc(q_sq, 1)
                if s >= 1:
                    for e in range(E2):
                        use = plan["xo", s - 1, e]
                        bank = wait_full(act, use)
                        copy(oxT[:, (s - 1) % 2, e, :], bank[:, :]).then_inc(read[use[0]], 1)

            def evac_hT(b, l):
                use = lay(("hT", b, 0), l)
                bank = wait_full(act, use)
                copy(hT[:, 0, 0:S], bank[:, :]).then_inc(read[use[0]], 1)

            def qkv_tile(b, t, l):
                use = lay(("v", b, t), l)
                bank = wait_full(act, use)
                copy(lv[:, b % 2, t, :], bank[:, :]).then_inc(read[use[0]], 1)
                for i, what in enumerate("qk"):
                    bank = wait_full(act, lay((what, b, t), l))
                    if b or t:
                        act.wait_ge(l_ss, l * (2 * B * T) + (2 * (T * b + t - 1) + i + 1))
                    act.activation(sq[:, i, :], bank[:, :], ACT.Square).then_inc(l_sq, 1)

            def evac_tq(b, t, l):
                use = lay(("Tq", b, t), l)
                src = wait_full(act, use)[:, :].rearrange("p (j s) -> p j s", s=P)
                cols = slice(t * P, (t + 1) * P)
                copy(lqz[0:FDH, b % 2, :, 0, cols], src[0:FDH])
                copy(lqz[FDH:P, b % 2, :, 1, cols], src[FDH:P]).then_inc(read[use[0]], 1)

            def local_exponentials(u, l):
                b, j = divmod(u, FPAIRS)
                for h in range(2):
                    act.wait_ge(l_neg, l * (2 * NLU) + (2 * u + h + 1))
                    for w in range(T):
                        pr = lp[:, u % 2, h, loc_at(w):loc_at(w + 1)]
                        ins = act.activation(pr, pr, ACT.Exp, bias=lneg[:, u % 2, h, w:w + 1],
                                             scale=rn[:, b % 2, w, 0, 2 * j + h:2 * j + h + 1],
                                             accum_out=lden[:, u % 2, h, w:w + 1])
                    ins.then_inc(l_exp, 1)

            def mlp(b, j, l):
                if j == 1:
                    for e in range(E2):
                        use = lay(("hnT", b, e), l)
                        bank = wait_full(act, use)
                        act.activation(hnT[:, e, :], bank[:, :], ACT.Identity, bias=lnb[:, e:e + 1],
                                       scale=lng[:, e:e + 1]).then_inc(read[use[0]], 1)
                if j in (1, 2):
                    for f in range(3 * (j - 1), 3 * j):
                        use = lay(("w1g", b, f), l)
                        bank = wait_full(act, use)
                        if f >= GELU_T:
                            wait_read(act, lay(("w1a", b, f - GELU_T), l))
                        m = frows(f)
                        act.activation(gl[0:m, f % GELU_T, :], bank[0:m, :], ACT.Gelu, bias=b1[0:m, 1, f:f + 1])\
                            .then_inc(read[use[0]], 1)

            act.wait_ge(set1, 3)
            with act.Fori(0, DEPTH) as l:
                act.wait_ge(ld_small, l * (16 * 6) + 16 * 6)
                evac_hT(0, l)
                for t in range(T):
                    qkv_tile(0, t, l)
                    if t:
                        evac_tq(0, t - 1, l)
                evac_tq(0, T - 1, l)
                local_exponentials(0, l)
                for b in range(B):
                    for j in range(FPAIRS):
                        u = b * FPAIRS + j
                        if b + 1 < B:
                            if j == 0:
                                evac_hT(b + 1, l)
                            qkv_tile(b + 1, j, l)
                        if b:
                            mlp(b - 1, j, l)
                        for h in range(2):
                            use = lay(("T", u, h, 0), l)
                            bank = wait_full(act, use)
                            copy(lpT[:, h, 0:S], bank[:, :]).then_inc(read[use[0]], 1)
                        if b + 1 < B:
                            evac_tq(b + 1, j, l)
                        use = lay(("O", u), l)
                        bank = wait_full(act, use)
                        copy(loT[:, j, :], bank[:, :]).then_inc(read[use[0]], 1)
                        if u + 1 < NLU:
                            local_exponentials(u + 1, l)
                for j in range(FPAIRS):
                    mlp(B - 1, j, l)

        @block.vector
        def _(dve):
            def norm_stats(n, src):
                for t in range(T):
                    dve.bn_stats(stats[:, n % 2, t, 0:6], src[:, t, :]).then_inc(ln_stats, 1)
                dve.wait_ge(ln_stats, T * (n + 1))
                for t in range(T):
                    dve.bn_aggr(mv[:, n % 2, t, :], stats[:, n % 2, t, 0:6]).then_inc(ln_mv, 1)

            def norm_apply(n, src, dst):
                dve.wait_ge(ln_mv, T * (n + 1))
                dve.wait_ge(ln_rstd, n + 1)
                for t in range(T):
                    ins = dve.tensor_scalar(dst[:, t, :], src[:, t, :], mv[:, n % 2, t, 0:1], rstd[:, n % 2, t:t + 1],
                                            ALU.subtract, ALU.mult)
                ins.then_inc(ln_done, 1)

            dve.wait_ge(ld_const, 16 * 3)
            for b in range(B + 1):
                if b < B:
                    dve.wait_ge(ld_x[b], 16)
                    norm_stats(b, x[:, b])
                if b >= 1:
                    if b >= 3:
                        wait_full(dve, use_x(b - 3, 0))
                        wait_full(dve, use_x(b - 3, 1))
                    norm_apply(b - 1, x[:, b - 1], xn[:, (b - 1) % 2])

            def evac_k(u):
                bank = wait_full(dve, use_k(u))
                dve.tensor_copy(kT[:, :], bank[:, :]).then_inc(read[7], 1)

            def masked_scores(u, j):
                for h in range(2):
                    for k, blocks in enumerate(((3,), (2, 0), (1,))):
                        bank = wait_full(dve, use_s(u, h, k))
                        pass_wait(dve, passed_v)
                        at = 0
                        for i in blocks:
                            ins = dve.tensor_tensor_reduce(
                                probs[:, j % 2, h, TRI_AT[i]:TRI_AT[i + 1]], bank[:, at:at + TRI[i]],
                                causal[:, S - TRI[i]:S], 1.0, -3e38, ALU.add, ALU.max, rowmax[:, j % 2, h, i:i + 1])
                            at += TRI[i]
                        ins.then_inc(read[k], 1)
                    for k in range(3):
                        wait_read(dve, use_s(u, h, k))
                    dve.tensor_scalar(negmax[:, j % 2, h, :], rowmax[:, j % 2, h, :], -ADH ** -0.5, None, ALU.mult)\
                        .then_inc(s_neg, 1)

            def inverse_sums(u, j):
                for h in range(2):
                    dve.wait_ge(s_exp, 2 * u + (h + 1))
                    dve.reciprocal(rden[:, j % 2, h, :], den[:, j % 2, h, :]).then_inc(s_rden, 1)

            def evac_pT(u, n):
                h, k = divmod(n, 3)
                bank = wait_full(dve, use_t(u, h, k))
                at = KEYB_AT[T_TILES[k][0]]
                w = sum(KEYB[j] for j in T_TILES[k])
                dve.tensor_copy(pT[:, h, at:at + w], bank[:, 0:w]).then_inc(read[use_t(u, h, k)[0]], 1)

            def slot(u, j, ahead, z):
                if ahead >= 1:
                    masked_scores(u + 1, j + 1)
                    inverse_sums(u + 1, j + 1)
                if ahead >= 2:
                    evac_k(u + 2)
                for n in (0, 2, 4):
                    evac_pT(u, n)
                bank = wait_full(dve, use_z(u))
                dve.tensor_copy(z, bank[:, :]).then_inc(read[5], 1)

            evac_k(0)
            masked_scores(0, 0)
            inverse_sums(0, 0)
            evac_k(1)
            zflat = zT[:, :, :, :].rearrange("p k b s -> p (k b s)")
            with dve.Fori(0, PAIRS - 1) as p:
                for j in range(B):
                    slot(p * B + j, j, 2, zflat[:, bass.ds((p * B + j) * S, S)])
            for j in range(B):
                slot(NU - B + j, j, B - 1 - j, zT[:, PAIRS - 1, j, :])

            dve.wait_ge(ld_xw, 16 * 8)
            dve.tensor_scalar(xkeep[:, :, :], xmask[:, :, :], -1.0, 1.0, ALU.mult, ALU.add).then_inc(k_keep, 1)

            def add_attention(b):
                for tp in range(2):
                    use = plan["wo", b, tp]
                    bank = wait_full(dve, use)
                    xs = x[:, b, 2 * tp:2 * tp + 2, :]
                    dve.tensor_tensor(xs, bank[:, :].rearrange("p (t e) -> p t e", e=D), xs, ALU.add)\
                        .then_inc(read[use[0]], 1)

            def norm2_stats(b):
                wait_read(dve, plan["wo", b, 0])
                wait_read(dve, plan["wo", b, 1])
                norm_stats(B + b, x[:, b])

            def norm2_apply(b):
                if b >= 2:
                    wait_full(dve, plan["x1T", b - 2, 0])
                    wait_full(dve, plan["x1T", b - 2, 1])
                norm_apply(B + b, x[:, b], xn[:, b % 2])

            def add_kv_bias(b):
                for t in range(T):
                    use = plan["kv", b, t]
                    bank = wait_full(dve, use)
                    dve.tensor_tensor(kv[:, b % 2, t, :], bank[:, :], xbkv[:, :], ALU.add).then_inc(read[use[0]], 1)

            def keys(b):
                for t in range(T):
                    wait_read(dve, plan["kv", b, t])
                k = kv[:, b % 2, :, 0:D]
                dve.tensor_scalar(ktmp[:, :, :], k, 0.0, None, ALU.min).then_inc(k_min, 1)
                dve.wait_ge(k_exp, b + 1)
                dve.scalar_tensor_tensor(kf[:, b % 2, :, :], k, 0.0, ktmp[:, :, :], ALU.max, ALU.add).then_inc(k_fin, 1)
                dve.wait_ge(k_sq, b + 1)
                norm = knorm[:, b % 2, :, :]
                dve.tensor_reduce(norm.rearrange("p t h -> p (t h)"),
                                  ktmp[:, :, :].rearrange("p t (h d) -> p (t h) d", d=XDH), AX.X, ALU.add)\
                    .then_inc(k_ss, 1)
                dve.wait_ge(k_sqrt, b + 1)
                dve.tensor_scalar(norm, norm, NORM_EPS, None, ALU.max).then_inc(k_rec, 1)
                dve.wait_ge(k_rec, 3 * b + 1)
                dve.reciprocal(norm, norm).then_inc(k_rec, 1)
                dve.wait_ge(k_rec, 3 * b + 2)
                dve.wait_ge(k_keep, 1)
                keep = xkeep[:, b, :].rearrange("p (t o) -> p t o", o=1).broadcast_to([P, T, XH])
                dve.tensor_tensor(norm, norm, keep, ALU.mult).then_inc(k_rec, 1)
                dve.wait_ge(k_rec, 3 * b + 3)
                k3 = kf[:, b % 2, :, :].rearrange("p t (h d) -> p (t h) d", d=XDH)
                r = norm.rearrange("p t h -> p (t h)").rearrange("p (g o) -> p g o", o=1)\
                    .broadcast_to([P, T * XH, XDH])
                dve.tensor_tensor(k3, k3, r, ALU.mult).then_inc(k_done, 1)

            def mask_kv(b):
                use = plan["KV", b]
                bank = wait_full(dve, use)
                for e in range(E2):
                    ins = dve.tensor_tensor(kvm[:, b, e, :], bank[:, e * P:(e + 1) * P], heads[:, :], ALU.mult)
                ins.then_inc(read[use[0]], 1)

            add_attention(0)
            norm2_stats(0)
            add_attention(1)
            norm2_stats(1)
            norm2_apply(0)
            add_attention(2)
            norm2_apply(1)
            add_attention(3)
            add_kv_bias(0)
            norm2_stats(2)
            norm2_apply(2)
            keys(0)
            add_kv_bias(1)
            norm2_stats(3)
            norm2_apply(3)
            keys(1)
            mask_kv(0)
            add_kv_bias(2)
            keys(2)
            mask_kv(1)
            add_kv_bias(3)
            keys(3)
            mask_kv(2)
            mask_kv(3)

            for s in range(B + 2):
                if s < B:
                    for e in range(E2):
                        use = plan["xq", s, e]
                        bank = wait_full(dve, use)
                        dve.wait_ge(q_relu, 2 * s + e + 1)
                        dve.tensor_scalar(qm[:, e, :], bank[:, :], xbq[:, e:e + 1], 0.0, ALU.add, ALU.min)\
                            .then_inc(read[use[0]], 1)
                    for e in range(E2):
                        dve.wait_ge(q_exp, 2 * s + e + 1)
                        dve.tensor_tensor(qT[:, s % 2, e, :], qr[:, e, :], qm[:, e, :], ALU.add).then_inc(q_fin, 1)
                if s >= 2:
                    b = s - 2
                    dve.wait_ge(bo_done, b + 1)
                    for tp in range(2):
                        use = plan["xw", b, tp]
                        bank = wait_full(dve, use)
                        xs = x[:, b, 2 * tp:2 * tp + 2, :]
                        dve.tensor_tensor(xs, bank[:, :].rearrange("p (t e) -> p t e", e=D), xs, ALU.add)\
                            .then_inc(read[use[0]], 1)
                    for tp in range(2):
                        wait_read(dve, plan["xw", b, tp])
                    norm_stats(2 * B + b, x[:, b])
                if s < B:
                    dve.wait_ge(q_sq, 2 * s + 2)
                    dve.tensor_scalar(qss[:, s % 2, :], qss[:, s % 2, :], NORM_EPS ** 2, None, ALU.max).then_inc(q_max, 1)
                    dve.wait_ge(q_rn, s + 1)
                    for tp in range(2):
                        wait_read(dve, plan["KV", s])
                    for e in range(E2):
                        dve.tensor_scalar(kvs[:, s % 2, e, :], kvm[:, s, e, :], qss[:, s % 2, e:e + 1], None, ALU.mult)\
                            .then_inc(kvs_done, 1)
                if s >= 2:
                    norm_apply(2 * B + s - 2, x[:, s - 2], y[:, s - 2])

            def tables():
                H = FDH // 2
                for i in range(2):
                    sc = qk_scale[:, i, :].rearrange("p (o d) -> p o d", o=1)
                    dve.tensor_tensor(tab[:, 2 * i, :, :], rot[:, 2 * i, :, :], sc.broadcast_to([P, T, FDH]), ALU.mult)\
                        .then_inc(l_tab, 1)
                    for lo, other in ((0, H), (H, 0)):
                        dve.tensor_tensor(tab[:, 2 * i + 1, :, lo:lo + H], rot[:, 2 * i + 1, :, lo:lo + H],
                                          sc[:, :, other:other + H].broadcast_to([P, T, H]), ALU.mult)\
                            .then_inc(l_tab, 1)

            def evac_hT(b, l):
                use = lay(("hT", b, 1), l)
                bank = wait_full(dve, use)
                dve.tensor_copy(hT[:, 1, 1:S + 1], bank[:, :]).then_inc(read[use[0]], 1)

            def qkv_tile(b, t, l):
                n = T * b + t
                if b == 0 and t:
                    wait_full(dve, lay(("Tk", b, t - 1), l))
                for i, what in enumerate("qk"):
                    use = lay((what, b, t), l)
                    bank = wait_full(dve, use)
                    dve.wait_ge(l_sq, l * (2 * B * T) + (2 * n + i + 1))
                    src = bank[:, :].rearrange("p (h d) -> p h d", d=FDH)
                    cos = tab[:, 2 * i, t:t + 1, :].broadcast_to([P, FH, FDH])
                    dve.tensor_tensor(ra[:, i, :].rearrange("p (h d) -> p h d", d=FDH), src, cos, ALU.mult)
                    swapped = bank[:, :].rearrange("p (h a d) -> p h a d", a=2, d=FDH // 2)[:, :, ::-1, :]
                    sin = tab[:, 2 * i + 1, t:t + 1, :].broadcast_to([P, FH, FDH])\
                        .rearrange("p h (a d) -> p h a d", a=2)
                    dve.tensor_tensor(rb[:, i, :].rearrange("p (h a d) -> p h a d", a=2, d=FDH // 2), swapped, sin,
                                      ALU.mult).then_inc(read[use[0]], 1)
                    if n:
                        dve.wait_ge(l_rn, l * (B * T) + n)
                    dve.tensor_reduce(ss[:, i, :], sq[:, i, :].rearrange("p (h d) -> p h d", d=FDH), AX.X, ALU.add)\
                        .then_inc(l_ss, 1)
                    dve.wait_ge(l_ss, l * (2 * B * T) + (2 * n + i + 1))
                    dve.tensor_scalar(ss[:, i, :], ss[:, i, :], NORM_EPS ** 2, 1.0 if i else QK_SCALE ** -2,
                                      ALU.max, ALU.mult).then_inc(l_ssm, 1)

            def evac_tk(b, t, l):
                use = lay(("Tk", b, t), l)
                bank = wait_full(dve, use)
                dve.tensor_copy(lkT[:, b % 2, :, t * P:(t + 1) * P], bank[:, :].rearrange("p (j s) -> p j s", s=P))\
                    .then_inc(read[use[0]], 1)

            def local_scores(u, l):
                b, j = divmod(u, FPAIRS)
                if j == 0:
                    dve.wait_ge(l_rn, l * (B * T) + (T * b + T))
                for h in range(2):
                    for k in range(2):
                        use = lay(("S", u, h, k), l)
                        bank = wait_full(dve, use)
                        pass_wait(dve, passed_v)
                        at = 0
                        for w in (2 * k, 2 * k + 1):
                            lo, hi = loc_at(w), loc_at(w + 1)
                            ins = dve.tensor_tensor_reduce(
                                lp[:, u % 2, h, lo:hi], bank[:, at:at + hi - lo], local[:, LOC - (hi - lo):LOC], 1.0,
                                -3e38, ALU.add, ALU.max, lmax[:, u % 2, h, w:w + 1])
                            at += hi - lo
                        ins.then_inc(read[use[0]], 1)
                    for k in range(2):
                        wait_read(dve, lay(("S", u, h, k), l))
                    dve.scalar_tensor_tensor(lneg[:, u % 2, h, :], lmax[:, u % 2, h, :], -1.0,
                                             rn[:, b % 2, :, 0, 2 * j + h], ALU.mult, ALU.mult).then_inc(l_neg, 1)

            def local_inverse_sums(u, l):
                for h in range(2):
                    dve.wait_ge(l_exp, l * (2 * NLU) + (2 * u + h + 1))
                    dve.reciprocal(lrden[:, u % 2, h, :], lden[:, u % 2, h, :]).then_inc(l_rden, 1)

            def add_to_y(what, b, l):
                for tp in range(2):
                    use = lay((what, b, tp), l)
                    bank = wait_full(dve, use)
                    ys = y[:, b, 2 * tp:2 * tp + 2, :]
                    dve.tensor_tensor(ys, bank[:, :].rearrange("p (t e) -> p t e", e=D), ys, ALU.add)\
                        .then_inc(read[use[0]], 1)

            def mlp_norm(b, l):
                for tp in range(2):
                    wait_read(dve, lay(("lwo", b, tp), l))
                for t in range(T):
                    dve.bn_stats(stats[:, 0, t, 0:6], y[:, b, t, 0:P]).then_inc(f_stats, 1)
                dve.wait_ge(hs_ld, l * (32 * B) + 32 * (b + 1))
                for t in range(T):
                    dve.bn_stats(stats[:, 0, t, 6:12], hs[:, t, :]).then_inc(f_stats, 1)
                dve.wait_ge(f_stats, l * (2 * T * B) + 2 * T * (b + 1))
                pass_wait(dve, passed_v)
                for t in range(T):
                    dve.bn_aggr(mv[:, 0, t, :], stats[:, 0, t, :]).then_inc(f_mv, 1)
                dve.wait_ge(f_mv, l * (T * B) + T * (b + 1))
                dve.wait_ge(f_rstd, l * B + (b + 1))
                for t in range(T):
                    dve.tensor_scalar(hn[:, t, 0:P], y[:, b, t, 0:P], mv[:, 0, t, 0:1], rstd[:, 0, t:t + 1],
                                      ALU.subtract, ALU.mult)
                    ins = dve.tensor_scalar(hn[:, t, P:D], hs[:, t, :], mv[:, 0, t, 0:1], rstd[:, 0, t:t + 1],
                                            ALU.subtract, ALU.mult)
                ins.then_inc(f_hn, 1)

            def mlp(b, j, l):
                if j == 0:
                    add_to_y("lwo", b, l)
                if j in (1, 2):
                    for f in range(3 * (j - 1), 3 * j):
                        use = lay(("w1a", b, f), l)
                        wait_read(dve, lay(("w1g", b, f), l))
                        bank = wait_full(dve, use)
                        m = frows(f)
                        dve.scalar_tensor_tensor(hid[0:m, f, :], bank[0:m, :], b1[0:m, 0, f:f + 1],
                                                 gl[0:m, f % GELU_T, :], ALU.add, ALU.mult).then_inc(read[use[0]], 1)
                if j == 3:
                    dve.wait_ge(f_b2, l * B + (b + 1))
                    add_to_y("w2", b, l)

            dve.wait_ge(x2_st, 16 * B)
            dve.wait_ge(ln_done, 3 * B)
            dve.wait_ge(set1, 3)
            dve.wait_ge(ld_rot, 16)
            with dve.Fori(0, DEPTH) as l:
                dve.wait_ge(ld_small, l * (16 * 6) + 16 * 6)
                tables()
                evac_hT(0, l)
                dve.wait_ge(l_tab, l * 6 + 6)
                for t in range(T):
                    qkv_tile(0, t, l)
                    if t:
                        evac_tk(0, t - 1, l)
                evac_tk(0, T - 1, l)
                local_scores(0, l)
                for b in range(B):
                    for j in range(FPAIRS):
                        u = b * FPAIRS + j
                        if b and j == 1:
                            mlp_norm(b - 1, l)
                        if b + 1 < B and j == 0:
                            evac_hT(b + 1, l)
                        local_inverse_sums(u, l)
                        if b + 1 < B:
                            qkv_tile(b + 1, j, l)
                        if b:
                            mlp(b - 1, j, l)
                        for h in range(2):
                            use = lay(("T", u, h, 1), l)
                            bank = wait_full(dve, use)
                            dve.tensor_copy(lpT[:, h, S:LOC_N], bank[:, 0:LOC_N - S]).then_inc(read[use[0]], 1)
                        if b + 1 < B:
                            evac_tk(b + 1, j, l)
                        if u + 1 < NLU:
                            local_scores(u + 1, l)
                for j in range(FPAIRS):
                    if j == 1:
                        mlp_norm(B - 1, l)
                    mlp(B - 1, j, l)
            for b in range(B):
                for tp in range(2):
                    wait_read(dve, lay(("w2", b, tp), DEPTH - 1))
                dve.wait_ge(x2_ld[b], 16)
                dve.tensor_tensor(y[:, b, :, :], y[:, b, :, :], x2_back(b), ALU.add).then_inc(fin_done, 1)

        @block.tensor
        def _(pe):
            mm = pe.matmul

            def product(dst, pairs, last=None, **kw):
                for i, (lhsT, rhs) in enumerate(pairs):
                    ins = mm(dst, lhsT, rhs, start=i == 0, stop=i == len(pairs) - 1, **kw)
                return ins

            pe.wait_ge(ld_const, 16 * 3)
            for b in range(B):
                pe.wait_ge(ln_done, b + 1)
                for e in range(E2):
                    bank = wait_free(pe, use_x(b, e))
                    for t in range(T):
                        ins = pe.transpose(bank[:, t * P:(t + 1) * P], xn[:, b % 2, t, e * P:(e + 1) * P], ident[:, :])
                    ins.then_inc(full[use_x(b, e)[0]], 1)

            def project_qk(u, b, p):
                pe.wait_ge(ld_qk, 16 * (p + 1))
                for i, use in enumerate((use_q(u), use_k(u))):
                    bank = wait_free(pe, use)
                    product(bank[:, :], [(wst[:, i, e, :], xnT[:, e, b, :]) for e in range(E2)])\
                        .then_inc(full[use[0]], 1)

            def project_v(u, b, p):
                pe.wait_ge(ld_v, 16 * (p + 1))
                use = use_v(u)
                bank = wait_free(pe, use)
                for t in range(T):
                    ins = product(bank[:, t * P:(t + 1) * P],
                                  [(xnT[:, e, b, t * P:(t + 1) * P], wst[:, 2, e, :]) for e in range(E2)])
                ins.then_inc(full[use[0]], 1)

            def scores(u):
                wait_read(pe, use_q(u))
                wait_read(pe, use_k(u))
                for h in range(2):
                    for k, blocks in enumerate(((3,), (2, 0), (1,))):
                        bank = wait_free(pe, use_s(u, h, k))
                        at = 0
                        for i in blocks:
                            ins = mm(bank[:, at:at + TRI[i]], kT[:, i * P:(i + 1) * P], qz[:, h, 0:TRI[i]],
                                     start=True, stop=True)
                            at += TRI[i]
                        ins.then_inc(full[k], 1)

            def transposes(u, j):
                for h in range(2):
                    pe.wait_ge(s_prob, 2 * u + (h + 1))
                    for k, blocks in enumerate(T_TILES):
                        use = use_t(u, h, k)
                        bank = wait_free(pe, use)
                        at = 0
                        for c in blocks:
                            for i in range(c, T):
                                lo = TRI_AT[i] + c * P
                                ins = pe.transpose(bank[:, at:at + P], probs[:, j % 2, h, lo:lo + P], ident[:, :])
                                at += P
                        ins.then_inc(full[use[0]], 1)

            def weighted_values(u, j):
                for k in (1, 2):
                    wait_read(pe, use_t(u, 1, k))
                wait_read(pe, use_v(u))
                bank = wait_free(pe, use_z(u))
                for c in range(T):
                    for h in range(2):
                        rows = slice(h * ADH, (h + 1) * ADH)
                        ins = mm(bank[rows, c * P:S], v[:, j % 2, c, rows],
                                 pT[:, h, KEYB_AT[c]:KEYB_AT[c] + KEYB[c]], start=c == 0, stop=c == T - 1)
                ins.then_inc(full[5], 1)

            def slot(u, j, p, ahead):
                if ahead >= 1:
                    scores(u + 1)
                if ahead >= 2:
                    project_qk(u + 2, (j + 2) % B, p + (j + 2) // B)
                transposes(u, j)
                weighted_values(u, j)
                if ahead >= 2:
                    project_v(u + 2, (j + 2) % B, p + (j + 2) // B)

            wait_read(pe, use_x(B - 1, 0))
            wait_read(pe, use_x(B - 2, 1))
            wait_read(pe, use_x(B - 1, 1))
            project_qk(0, 0, 0)
            project_v(0, 0, 0)
            scores(0)
            project_qk(1, 1, 0)
            project_v(1, 1, 0)
            with pe.Fori(0, PAIRS - 1) as p:
                for j in range(B):
                    slot(p * B + j, j, p, 2)
            for j in range(B):
                slot(NU - B + j, j, PAIRS - 1, B - 1 - j)

            pe.wait_ge(ld_wo, 16)
            for b in range(B):
                wait_read(pe, use_z(NU - B + b))
                for tp in range(2):
                    use = plan["wo", b, tp]
                    bank = wait_free(pe, use)
                    for i in range(2):
                        t = 2 * tp + i
                        ins = product(bank[:, i * D:(i + 1) * D],
                                      [(zT[:, k, b, t * P:(t + 1) * P], woT[:, k, :]) for k in range(PAIRS)])
                    ins.then_inc(full[use[0]], 1)

            def keys_values(b):
                for t in range(T):
                    use = plan["kv", b, t]
                    bank = wait_free(pe, use)
                    product(bank[:, :], [(ctxT[:, e, b, t * P:(t + 1) * P], xwkv[:, e, :]) for e in range(E2)])\
                        .then_inc(full[use[0]], 1)

            def norm2_T(b):
                pe.wait_ge(ln_done, B + b + 1)
                for e in range(E2):
                    use = plan["x1T", b, e]
                    bank = wait_free(pe, use)
                    for t in range(T):
                        ins = pe.transpose(bank[:, t * P:(t + 1) * P], xn[:, b % 2, t, e * P:(e + 1) * P], ident[:, :])
                    ins.then_inc(full[use[0]], 1)

            def k_t_v(b):
                pe.wait_ge(k_done, b + 1)
                use = plan["KV", b]
                bank = wait_free(pe, use)
                for e in range(E2):
                    ins = product(bank[:, e * P:(e + 1) * P],
                                  [(kf[:, b % 2, t, e * P:(e + 1) * P], kv[:, b % 2, t, D + e * P:D + (e + 1) * P])
                                   for t in range(T)])
                ins.then_inc(full[use[0]], 1)

            pe.wait_ge(ld_xw, 16 * 8)
            for b in range(B):
                pe.wait_ge(ld_ctx[b], 16)
                keys_values(b)
                norm2_T(b)
                if b:
                    k_t_v(b - 1)
            k_t_v(B - 1)
            for s in range(B + 2):
                if s < B:
                    for e in range(E2):
                        wait_read(pe, plan["x1T", s, e])
                    for c in range(E2):
                        use = plan["xq", s, c]
                        bank = wait_free(pe, use)
                        product(bank[:, :], [(xwq[:, e, c * P:(c + 1) * P], xnT[:, e, s, :]) for e in range(E2)])\
                            .then_inc(full[use[0]], 1)
                if 1 <= s <= B:
                    b = s - 1
                    pe.wait_ge(kvs_done, 2 * (b + 1))
                    for e in range(E2):
                        use = plan["xo", b, e]
                        bank = wait_free(pe, use)
                        product(bank[:, :], [(kvs[:, b % 2, e, :], qT[:, b % 2, e, :])]).then_inc(full[use[0]], 1)
                if s >= 2:
                    b = s - 2
                    for e in range(E2):
                        wait_read(pe, plan["xo", b, e])
                    for tp in range(2):
                        use = plan["xw", b, tp]
                        bank = wait_free(pe, use)
                        for i in range(2):
                            t = 2 * tp + i
                            ins = product(bank[:, i * D:(i + 1) * D],
                                          [(oxT[:, b % 2, e, t * P:(t + 1) * P], xwo[:, e, :]) for e in range(E2)])
                        ins.then_inc(full[use[0]], 1)

            def transposed_y(b, l):
                for tp in range(2):
                    wait_read(pe, lay(("w2", b, tp), l - 1))
                for e in range(E2):
                    use = lay(("hT", b, e), l)
                    bank = wait_free(pe, use)
                    for t in range(T):
                        ins = pe.transpose(bank[:, t * P:(t + 1) * P], y[:, b, t, e * P:(e + 1) * P], ident[:, :])
                    ins.then_inc(full[use[0]], 1)

            def qkv_tile(b, t, l):
                if t == 0:
                    transposed_y(b, l)
                    for e in range(E2):
                        wait_read(pe, lay(("hT", b, e), l))
                for what, c in (("v", 2), ("q", 0), ("k", 1)):
                    use = lay((what, b, t), l)
                    bank = wait_free(pe, use)
                    product(bank[:, :], [(hT[:, e, t * P:(t + 1) * P], wqkv[:, e, c * INNER:(c + 1) * INNER])
                                         for e in range(E2)]).then_inc(full[use[0]], 1)

            def transposed_qk(b, t, l):
                for i, (what, done) in enumerate((("Tq", l_q), ("Tk", l_k))):
                    pe.wait_ge(done, l * (B * T) + (T * b + t + 1))
                    use = lay((what, b, t), l)
                    bank = wait_free(pe, use)
                    for j in range(FPAIRS):
                        ins = pe.transpose(bank[:, j * P:(j + 1) * P], ra[:, i, j * P:(j + 1) * P], ident[:, :])
                    ins.then_inc(full[use[0]], 1)

            def local_scores(u, l):
                b, j = divmod(u, FPAIRS)
                if j == 0:
                    wait_read(pe, lay(("Tq", b, T - 1), l))
                    wait_read(pe, lay(("Tk", b, T - 1), l))
                for h in range(2):
                    for k in range(2):
                        use = lay(("S", u, h, k), l)
                        bank = wait_free(pe, use)
                        at = 0
                        for w in (2 * k, 2 * k + 1):
                            lo = max(w - 1, 0) * P
                            n = (w + 1) * P - lo
                            ins = mm(bank[:, at:at + n], lqz[:, b % 2, j, h, w * P:(w + 1) * P],
                                     lkT[:, b % 2, j, lo:lo + n], start=True, stop=True)
                            at += n
                        ins.then_inc(full[use[0]], 1)

            def local_transposes(u, l):
                for h in range(2):
                    pe.wait_ge(l_prob, l * (2 * NLU) + (2 * u + h + 1))
                    for k in range(2):
                        use = lay(("T", u, h, k), l)
                        bank = wait_free(pe, use)
                        at = 0
                        for c in (2 * k, 2 * k + 1):
                            for w in range(c, min(c + 2, T)):
                                lo = loc_at(w) + (P if w == c and w else 0)
                                ins = pe.transpose(bank[:, at:at + P], lp[:, u % 2, h, lo:lo + P], ident[:, :])
                                at += P
                        ins.then_inc(full[use[0]], 1)

            def local_values(u, l):
                b, j = divmod(u, FPAIRS)
                for k in range(2):
                    wait_read(pe, lay(("T", u, 1, k), l))
                if j == 0:
                    wait_read(pe, lay(("v", b, T - 1), l))
                use = lay(("O", u), l)
                bank = wait_free(pe, use)
                for c in range(T):
                    n = LOC if c < T - 1 else P
                    for h in range(2):
                        rows = slice(h * FDH, (h + 1) * FDH)
                        cols = slice((2 * j + h) * FDH, (2 * j + h + 1) * FDH)
                        ins = mm(bank[rows, c * P:c * P + n], lv[:, b % 2, c, cols],
                                 lpT[:, h, c * LOC:c * LOC + n], start=c == 0, stop=c == T - 1, skip_group_check=True)
                ins.then_inc(full[use[0]], 1)

            def mlp(b, j, l):
                if j == 0:
                    wait_read(pe, lay(("O", b * FPAIRS + FPAIRS - 1), l))
                    if b == 0:
                        pe.wait_ge(ld_lwo, l * 16 + 16)
                    for tp in range(2):
                        use = lay(("lwo", b, tp), l)
                        bank = wait_free(pe, use)
                        for i in range(2):
                            t = 2 * tp + i
                            ins = product(bank[:, i * D:(i + 1) * D],
                                          [(loT[:, k, t * P:(t + 1) * P], wo[:, k, :]) for k in range(FPAIRS)])
                        ins.then_inc(full[use[0]], 1)
                if j == 1:
                    pe.wait_ge(f_hn, l * B + (b + 1))
                    for e in range(E2):
                        use = lay(("hnT", b, e), l)
                        bank = wait_free(pe, use)
                        for t in range(T):
                            ins = pe.transpose(bank[:, t * P:(t + 1) * P], hn[:, t, e * P:(e + 1) * P], ident[:, :])
                        ins.then_inc(full[use[0]], 1)
                    for e in range(E2):
                        wait_read(pe, lay(("hnT", b, e), l))
                    if b == 0:
                        pe.wait_ge(ld_w1, l * 16 + 16)
                if j in (1, 2):
                    for f in range(3 * (j - 1), 3 * j):
                        m = frows(f)
                        for what, lo in (("w1g", HID + f * FT), ("w1a", f * FT)):
                            use = lay((what, b, f), l)
                            bank = wait_free(pe, use)
                            product(bank[0:m, :], [(w1[:, e, lo:lo + m], hnT[:, e, :]) for e in range(E2)])\
                                .then_inc(full[use[0]], 1)
                if j == 3:
                    for f in range(NF - 3, NF):
                        wait_read(pe, lay(("w1a", b, f), l))
                    if b == 0:
                        pe.wait_ge(ld_w2, l * 32 + 32)
                    for tp in range(2):
                        use = lay(("w2", b, tp), l)
                        bank = wait_free(pe, use)
                        for i in range(2):
                            t = 2 * tp + i
                            ins = product(bank[:, i * D:(i + 1) * D],
                                          [(hid[0:frows(f), f, t * P:(t + 1) * P], w2[0:frows(f), f, :])
                                           for f in range(NF)])
                        ins.then_inc(full[use[0]], 1)

            pe.wait_ge(ln_done, 3 * B)
            with pe.Fori(0, DEPTH) as l:
                pe.wait_ge(ld_wqkv, l * 16 + 16)
                for t in range(T):
                    qkv_tile(0, t, l)
                    if t:
                        transposed_qk(0, t - 1, l)
                transposed_qk(0, T - 1, l)
                local_scores(0, l)
                for b in range(B):
                    for j in range(FPAIRS):
                        u = b * FPAIRS + j
                        if b + 1 < B:
                            qkv_tile(b + 1, j, l)
                        if b:
                            mlp(b - 1, j, l)
                        local_transposes(u, l)
                        if b + 1 < B:
                            transposed_qk(b + 1, j, l)
                        local_values(u, l)
                        if u + 1 < NLU:
                            local_scores(u + 1, l)
                for j in range(FPAIRS):
                    mlp(B - 1, j, l)


def kernel(x, ctx_1024, mask_BxS2_bk1, L0_attn_W_Q, L0_attn_W_K, L0_attn_W_V, L0_attn_W_O, L0_xattn_Wq, L0_xattn_bq,
           L0_xattn_Wk, L0_xattn_bk, L0_xattn_Wv, L0_xattn_bv, L0_xattn_Wo, L0_xattn_bo, L0_ffn_wqkv, L0_ffn_q_scale,
           L0_ffn_k_scale, L0_ffn_wo, L0_ffn_ln_g, L0_ffn_ln_b, L0_ffn_w1, L0_ffn_b1, L0_ffn_w2, L0_ffn_b2):
    import concourse.bacc as bacc
    from concourse.bass_utils import run_bass_kernel_spmd

    def by_pairs(w):
        return np.asarray(w).reshape(PAIRS, P, E2, P).transpose(0, 3, 2, 1)

    def by_rows(w):
        return np.asarray(w).reshape(*np.shape(w)[:-1], E2, P).swapaxes(-1, -2)

    def hidden_rows(w):
        parts = np.asarray(w).reshape(DEPTH, 2, HID)
        filled = np.concatenate([parts, np.zeros((DEPTH, 2, FT * NF - HID), parts.dtype)], 2)
        return filled.reshape(DEPTH, 2, NF, FT).transpose(0, 3, 1, 2)

    arrays = {
        "x": x,
        "ctxT": np.asarray(ctx_1024).transpose(0, 2, 1),
        "mask": np.asarray(mask_BxS2_bk1).reshape(B, T, P).transpose(2, 0, 1),
        "w_pairs": np.stack([by_pairs(L0_attn_W_Q), by_pairs(L0_attn_W_K), by_pairs(L0_attn_W_V)], 2),
        "attn_wo": np.asarray(L0_attn_W_O).transpose(0, 2, 1).reshape(AH * ADH, D),
        "xwq": np.asarray(L0_xattn_Wq).T, "xbq": by_rows(L0_xattn_bq),
        "xwkv": np.concatenate([np.asarray(L0_xattn_Wk).T, np.asarray(L0_xattn_Wv).T], 1),
        "xbkv": np.concatenate([np.asarray(L0_xattn_bk), np.asarray(L0_xattn_bv)]),
        "xwo": np.asarray(L0_xattn_Wo).T, "xbo": L0_xattn_bo,
        "wqkv": L0_ffn_wqkv, "q_scale": L0_ffn_q_scale, "k_scale": L0_ffn_k_scale, "wo": L0_ffn_wo,
        "ln_g": by_rows(L0_ffn_ln_g), "ln_b": by_rows(L0_ffn_ln_b), "w1": L0_ffn_w1, "b1": hidden_rows(L0_ffn_b1), "w2": L0_ffn_w2, "b2": L0_ffn_b2,
    }
    arrays.update(constants())
    nc = bacc.Bacc("TRN2", target_bir_lowering=False, num_devices=1)
    aps, feeds = {}, {}
    for name, value in arrays.items():
        value = np.ascontiguousarray(value)
        feeds[f"in_{name}"] = value
        aps[name] = nc.dram_tensor(f"in_{name}", value.shape, mybir.dt.from_np(value.dtype), kind="ExternalInput").ap()
    out = nc.dram_tensor("out", (B, S, D), F32, kind="ExternalOutput").ap()
    x2_dram = nc.dram_tensor("x2_scratch", (B, S, D), F32).ap()
    build(nc, aps, out, x2_dram)
    result = run_bass_kernel_spmd(nc, [feeds], core_ids=[0])
    return result.results[0]["out"]
```

```python
from contextlib import ExitStack

import numpy as np

import concourse.bass as bass
from concourse import mybir

F32 = mybir.dt.float32
F32R = mybir.dt.float32r
U8 = mybir.dt.uint8
ALU = mybir.AluOpType
ACT = mybir.ActivationFunctionType
AX = mybir.AxisListType

P = 128
B, S, D = 4, 512, 256
T = S // P
E2 = D // P
AH, ADH = 16, 64
PAIRS = AH // 2
XH, XDH = 16, 16
DEPTH, FH, FDH = 2, 8, 64
INNER = FH * FDH
FPAIRS = FH // 2
HID = int(D * 4 * 2 / 3)
NF = 6
FT = -(-HID // NF)
FL = HID - FT * (NF - 1)
W = 128
QK_SCALE = 8.0
NEG = -1e30
LN_EPS = 1e-5
NORM_EPS = 1e-12
TRI = [P * (i + 1) for i in range(T)]
S_TILES = ((3,), (2,), (1, 0))
TRI_AT = [sum(TRI[:i]) for i in range(T + 1)]
KEYB = [S - P * j for j in range(T)]
KEYB_AT = [0, 512, 1024, 896]
T_TILES = ((0,), (1, 3), (2,))
LOC = 2 * P
LOC_N = P + LOC * (T - 1)
GELU_T = 2


def loc_at(w):
    return 0 if w == 0 else P + LOC * (w - 1)


def constants():
    ident = np.eye(P, dtype=np.float32)
    i = np.arange(P)[:, None]
    j = np.arange(P)[None, :]
    causal = np.zeros((P, S), np.float32)
    causal[:, S - P:] = np.where(j <= i, 0.0, NEG)
    local = np.concatenate([np.where(i <= j, 0.0, NEG), np.where(j <= i, 0.0, NEG)], 1).astype(np.float32)
    heads = (i // XDH == j // XDH).astype(np.float32)
    half = np.arange(0, FDH, 2, dtype=np.float32)
    inv_freq = (1.0 / np.float32(10000.0) ** (half / np.float32(FDH))).astype(np.float32)
    t = np.arange(S, dtype=np.float32)
    freqs = t[:, None] * inv_freq[None, :]
    freqs = np.concatenate([freqs, freqs], -1)
    base = ((half + np.float32(0.4 * FDH)) / np.float32(1.4 * FDH)).astype(np.float32)
    power = ((t - S // 2) / np.float32(W // 2)).astype(np.float32)
    scale = (base[None, :] ** power[:, None]).astype(np.float32)
    scale = np.concatenate([scale, scale], -1)
    cos, sin = np.cos(freqs), np.sin(freqs)
    sign = np.where(np.arange(FDH) < FDH // 2, -1.0, 1.0).astype(np.float32)
    rot = np.stack([cos * scale, sin * sign * scale, cos / scale, sin * sign / scale])
    rot = rot.reshape(4, T, P, FDH).transpose(2, 0, 1, 3).astype(np.float32)
    return {"c_ident": ident, "c_causal": causal, "c_local": local, "c_heads": heads,
            "c_rot": np.ascontiguousarray(rot)}


def build(nc, a, out, x2_dram):
    with ExitStack() as ctx:
        def sem(name):
            return ctx.enter_context(nc.semaphore(name))

        def sbt(stack, name, shape, dt=F32):
            return stack.enter_context(nc.sbuf_tensor(name, shape, dt))

        psum = [ctx.enter_context(nc.psum_tensor(f"psum{i}", [P, 512], F32)) for i in range(8)]
        full = [sem(f"full{i}") for i in range(8)]
        read = [sem(f"read{i}") for i in range(8)]

        ident = sbt(ctx, "ident", [P, P])
        local = sbt(ctx, "local", [P, LOC])
        neg_half = sbt(ctx, "neg_half", [P, 16])
        y = sbt(ctx, "y", [P, B, T, D])
        raw = ExitStack()
        wqkv_raw = sbt(raw, "wqkv_raw", [P, E2, 3 * INNER])
        raw.close()
        wqkv_lo = sbt(ctx, "wqkv_lo", [P, E2, 3 * INNER], F32R)
        wo = sbt(ctx, "wo", [P, FPAIRS, D])
        stats = sbt(ctx, "stats", [P, 2, T, 12])
        mv = sbt(ctx, "mv", [P, 2, T, 2])
        rstd = sbt(ctx, "rstd", [P, 2, T])

        ab = ExitStack()
        causal = sbt(ab, "causal", [P, S])
        x = sbt(ab, "x", [P, B, T, D])
        xnT = sbt(ab, "xnT", [P, E2, B, S])
        woT = sbt(ab, "woT", [P, PAIRS, D])
        xwq = sbt(ab, "xwq", [P, E2, D])
        xwkv = sbt(ab, "xwkv", [P, E2, 2 * D])
        xwo = sbt(ab, "xwo", [P, E2, D])
        xbkv = sbt(ab, "xbkv", [P, 2 * D])
        xbo = sbt(ab, "xbo", [P, D])
        xbq = sbt(ab, "xbq", [P, E2])
        xmask = sbt(ab, "xmask", [P, B, T], U8)
        xkeep = sbt(ab, "xkeep", [P, B, T])
        heads = sbt(ab, "heads", [P, P])
        r1 = ExitStack()
        rowmax = sbt(r1, "rowmax", [P, 2, 2, T])
        negmax = sbt(r1, "negmax", [P, 2, 2, T])
        den = sbt(r1, "den", [P, 2, 2, T])
        rden = sbt(r1, "rden", [P, 2, 2, T])
        q2 = sbt(r1, "q2", [P, 2, S], F32R)
        wst = sbt(r1, "wst", [P, 3, E2, P])
        k2 = sbt(r1, "k2", [P, 2, 2, S], F32R)
        v = sbt(r1, "v", [P, 2, T, P])
        pT = sbt(r1, "pT", [P, 2, TRI_AT[T]])
        probs = sbt(r1, "probs", [P, 2, 2, TRI_AT[T]])
        r1.close()
        r1 = ExitStack()
        ctxT = sbt(r1, "ctxT", [P, E2, B, S])
        kv = sbt(r1, "kv", [P, 2, T, 2 * D])
        xn = sbt(r1, "xn", [P, 2, T, D])
        r1.close()
        hold = sbt(ab, "hold", [P, 128 + 1024 + 768 + 2048 + 1024 + 2 * TRI_AT[T] + 4 * TRI_AT[T]])
        r2 = ExitStack()
        zT = sbt(r2, "zT", [P, PAIRS, B, S])
        r2.close()
        r2 = ExitStack()
        kf = sbt(r2, "kf", [P, 2, T, D])
        ktmp = sbt(r2, "ktmp", [P, T, D])
        knorm = sbt(r2, "knorm", [P, 2, T, XH])
        kvm = sbt(r2, "kvm", [P, B, E2, P])
        kvs = sbt(r2, "kvs", [P, 2, E2, P])
        qm = sbt(r2, "qm", [P, E2, S])
        qr = sbt(r2, "qr", [P, E2, S])
        qT = sbt(r2, "qT", [P, 2, E2, S])
        qss = sbt(r2, "qss", [P, 2, E2])
        oxT = sbt(r2, "oxT", [P, 2, E2, S])
        r2.close()
        ab.close()

        w1 = sbt(ctx, "w1", [P, E2, 2 * HID])
        w2 = sbt(ctx, "w2", [FT, NF, D])
        wqkv_hi = sbt(ctx, "wqkv_hi", [P, E2, 3 * INNER], F32R)
        tab = [sbt(ctx, f"tab{l}", [P, 4, T, FDH]) for l in range(DEPTH)]
        rot = tab[DEPTH - 1]
        qk_scale = sbt(ctx, "qk_scale", [P, DEPTH, 2, FDH])
        lng = sbt(ctx, "lng", [P, DEPTH, E2])
        lnb = sbt(ctx, "lnb", [P, DEPTH, E2])
        b1 = sbt(ctx, "b1", [FT, DEPTH, 2, NF])
        b2 = sbt(ctx, "b2", [P, DEPTH, D])
        hT_hi = sbt(ctx, "hT_hi", [P, E2, S + 1], F32R)
        hT_lo = sbt(ctx, "hT_lo", [P, E2, S + 1], F32R)
        sq = sbt(ctx, "sq", [P, 2, INNER])
        ra = sbt(ctx, "ra", [P, 2, INNER])
        rb = sbt(ctx, "rb", [P, 2, INNER])
        ss = sbt(ctx, "ss", [P, 2, FH])
        rn = sbt(ctx, "rn", [P, 2, T, 2, FH])
        lqz = sbt(ctx, "lqz", [P, 2, FPAIRS, 2, S])
        lkT = sbt(ctx, "lkT", [P, 2, FPAIRS, S])
        lv = sbt(ctx, "lv", [P, 2, T, INNER])
        lp = sbt(ctx, "lp", [P, 2, LOC_N])
        lpT = sbt(ctx, "lpT", [P, 2, LOC_N])
        lmax = sbt(ctx, "lmax", [P, 2, 2, T])
        lneg = sbt(ctx, "lneg", [P, 2, 2, T])
        lden = sbt(ctx, "lden", [P, 2, 2, T])
        lrden = sbt(ctx, "lrden", [P, 2, 2, T])
        loT = sbt(ctx, "loT", [P, FPAIRS, S])
        hs = sbt(ctx, "hs", [P, T, P])
        hn = sbt(ctx, "hn", [P, T, D])
        hnT = sbt(ctx, "hnT", [P, E2, S])
        gl = sbt(ctx, "gl", [FT, GELU_T, S])
        raw = ExitStack()
        wqkv_next = sbt(raw, "wqkv_next", [P, E2, 3 * INNER])
        raw.close()
        hid = sbt(ctx, "hid", [FT, NF, S])

        ld_const, ld_xw, ld_wo = sem("ld_const"), sem("ld_xw"), sem("ld_wo")
        ld_ctx = [sem(f"ld_ctx{b}") for b in range(B)]
        ld_x = [sem(f"ld_x{b}") for b in range(B)]
        ld_qk, ld_v = sem("ld_qk"), sem("ld_v")
        set0 = sem("set0")
        ln_stats, ln_mv = sem("ln_stats"), sem("ln_mv")
        ln_eps, ln_rstd = sem("ln_eps"), sem("ln_rstd")
        ln_done = sem("ln_done")
        q_hi, k_hi, k_both = sem("q_hi"), sem("k_hi"), sem("k_both")
        s_neg, s_rden = sem("s_neg"), sem("s_rden")
        s_exp, s_prob = sem("s_exp"), sem("s_prob")
        k_keep, k_min, k_fin, k_ss, k_rec, k_done = (
            sem(n) for n in ("k_keep", "k_min", "k_fin", "k_ss", "k_rec", "k_done"))
        k_exp, k_sq, k_sqrt = sem("k_exp"), sem("k_sq"), sem("k_sqrt")
        q_relu, q_exp, q_sq = sem("q_relu"), sem("q_exp"), sem("q_sq")
        q_fin, q_max, kvs_done = sem("q_fin"), sem("q_max"), sem("kvs_done")
        q_rn, bo_done = sem("q_rn"), sem("bo_done")
        x2_st = sem("x2_st")
        ld_rot, ld_small, ld_wqkv, ld_lwo, ld_w1, ld_w2 = (
            sem(n) for n in ("ld_rot", "ld_small", "ld_wqkv", "ld_lwo", "ld_w1", "ld_w2"))
        x2_b2 = sem("x2_b2")
        set1 = sem("set1")
        w_hi, w_lo = sem("w_hi"), sem("w_lo")
        h_hi = sem("h_hi")
        l_tab, l_ss, l_ssm, l_neg, l_rden = (
            sem(n) for n in ("l_tab", "l_ss", "l_ssm", "l_neg", "l_rden"))
        l_sq, l_exp = sem("l_sq"), sem("l_exp")
        l_q, l_rn, l_kadd, l_k, l_prob = (sem(n) for n in ("l_q", "l_rn", "l_kadd", "l_k", "l_prob"))
        hs_ld = sem("hs_ld")
        f_stats, f_mv, f_hn = (sem(n) for n in ("f_stats", "f_mv", "f_hn"))
        f_eps, f_rstd, f_b2 = (sem(n) for n in ("f_eps", "f_rstd", "f_b2"))
        x2_ld = [sem(f"x2_ld{b}") for b in range(B)]
        fin_done, out_st = sem("fin_done"), sem("out_st")
        passed_v, passed_p = sem("passed_v"), sem("passed_p")

        NU = PAIRS * B

        def use_s(u, h, k):
            return k, 2 * u + h

        def use_x(b, e):
            return (3, b) if e == 0 else (4 + b % 2, b // 2)

        def use_t(u, h, k):
            n = 3 * h + k
            return 3 + n % 2, 3 * u + n // 2 + (B // 2 if n % 2 else B)

        def use_z(u):
            return 5, u + B // 2

        def use_q(u):
            return 6, u

        def use_v(u):
            return 7, 2 * u + 1

        def use_k(u):
            return 7, 2 * u

        count = [2 * NU] * 3 + [B + 3 * NU, B // 2 + 3 * NU, B // 2 + NU, NU, 2 * NU]
        plan = {}

        def take(key, bank):
            plan[key] = (bank, count[bank])
            count[bank] += 1

        for b in range(B):
            for tp in range(2):
                take(("awo", b, tp), (2 * b + tp) % 3)
        for b in range(B):
            for t in range(T):
                take(("kv", b, t), 5 + (T * b + t) % 3)
            take(("x1T", b, 0), 3)
            take(("x1T", b, 1), 4)
            if b:
                take(("KV", b - 1), 2)
        take(("KV", B - 1), 2)
        for s in range(B + 2):
            if s < B:
                take(("xq", s, 0), 0)
                take(("xq", s, 1), 1)
            if 1 <= s <= B:
                take(("xo", s - 1, 0), 2)
                take(("xo", s - 1, 1), 5)
            if s >= 2:
                take(("xw", s - 2, 0), 6)
                take(("xw", s - 2, 1), 7)
        base = list(count)

        STEPS = DEPTH * B
        SET1 = 4
        UNITS = STEPS * FPAIRS

        def slot(m, j):
            u = m * FPAIRS + j
            qkv = [("qkv", m + 1, j, what) for what in "vqk"] if m + 1 < STEPS else []
            turned = [("Tqk", m + 1, j)] if m + 1 < STEPS else []
            head, gap, tail = list(qkv), [[], [], []], []
            if m and j == 0:
                wo_part = [("wo", m - 1, 0), ("wo", m - 1, 1), ("stats", m - 1)]
                head = wo_part + qkv if m == B - 1 else qkv + wo_part
                tail = [("norm", m - 1)]
            if m and j == 1:
                head = qkv[:2] + [("hnT", m - 1)] + qkv[2:]
            if m and j in (1, 2):
                gap = [[("w1", m - 1, f)] for f in range(NF // 2 * (j - 1), NF // 2 * j)]
            if m and j == 2:
                tail = [("bias", m - 1)]
            if m and j == 3:
                gap = [[("w2", m - 1, 0)], [], [("w2", m - 1, 1)]]
            if m == STEPS - 1 and j < B - 2:
                tail = tail + [("sum", j)]
            last = []
            if j == FPAIRS - 1 and m + 2 < STEPS:
                last.append(("hT", m + 2))
            if u + 1 < UNITS:
                last.append(("S", u + 1))
            if m and j == 0:
                last.append(("apply", m - 1))
            return ([("soft", u)] + head + gap[0] + [("T", u, 0)] + gap[1] + [("T", u, 1)] + gap[2] + turned
                    + [("AV", u)] + tail + last)

        first = [("hT", 0)]
        for t in range(T):
            first += [("qkv", 0, t, what) for what in "vqk"]
            if t:
                first.append(("Tqk", 0, t - 1))
        first += [("hT", 1), ("Tqk", 0, T - 1), ("S", 0)]
        m = STEPS - 1
        final = [("wo", m, 0), ("wo", m, 1), ("stats", m), ("norm", m), ("apply", m), ("hnT", m), ("bias", m)]
        final += [("w1", m, f) for f in range(NF)] + [("w2", m, 0), ("w2", m, 1)]
        order = list(first)
        for m in range(STEPS):
            for j in range(FPAIRS):
                order += slot(m, j)
        order += final

        turns = {"g": 0, "t": 0}
        banks = {"g": (2, 6, 7), "t": (3, 4)}

        def turn(key, which):
            take(key, banks[which][turns[which] % len(banks[which])])
            turns[which] += 1

        for what, *at in order:
            if what == "hT" or what == "hnT":
                for e in range(E2):
                    turn((what, at[0], e), "t")
            if what == "qkv":
                turn((at[2], at[0], at[1]), "g")
            if what == "wo" or what == "w2":
                turn((what, *at), "g")
            if what == "w1":
                turn(("w1g", *at), "g")
                turn(("w1a", *at), "g")
            if what == "Tqk":
                turn(("Tq", *at), "t")
                turn(("Tk", *at), "t")
            if what == "T":
                turn(("T", *at, 0), "t")
                turn(("T", *at, 1), "t")
            if what == "AV":
                take(("O", at[0]), 5)
            if what == "S":
                for h in range(2):
                    take(("S", at[0], h, 0), 0)
                    take(("S", at[0], h, 1), 1)

        def wait_free(pe, use):
            bank, n = use
            if not (isinstance(n, int) and n == 0):
                pe.wait_ge(read[bank], n)
            return psum[bank]

        def wait_full(eng, use):
            bank, n = use
            eng.wait_ge(full[bank], n + 1)
            return psum[bank]

        def wait_read(eng, use):
            bank, n = use
            eng.wait_ge(read[bank], n + 1)

        def pass_wait(eng, passed):
            eng.sem_inc(passed, 1)

        def frows(f):
            return FT if f < NF - 1 else FL

        def x2_back(b):
            return lqz[:, 0, b, :, :].rearrange("p h s -> p (h s)").rearrange("p (t e) -> p t e", e=D)

        block = ctx.enter_context(nc.Block())

        @block.sync
        def _(sp):
            for name, t in (("c_ident", ident), ("c_causal", causal), ("c_local", local)):
                sp.dma_start(t[:, :], a[name]).then_inc(ld_const, 16)
            for b in range(B):
                sp.dma_start(x[:, b, :, :], a["x"][b].rearrange("(t p) e -> p t e", p=P)).then_inc(ld_x[b], 16)
            sp.dma_start(wst[:, 0:2], a["w_pairs"][0, :, 0:2]).then_inc(ld_qk, 16)
            sp.dma_start(wst[:, 2], a["w_pairs"][0, :, 2]).then_inc(ld_v, 16)
            sp.dma_start(woT[:, :, :], a["attn_wo"].rearrange("(k p) e -> p k e", p=P)).then_inc(ld_wo, 16)
            for t, src in ((xwq, "xwq"), (xwkv, "xwkv"), (xwo, "xwo")):
                sp.dma_start(t[:, :, :], a[src].rearrange("(k p) e -> p k e", p=P)).then_inc(ld_xw, 16)
            sp.dma_start(xbkv[:, :], a["xbkv"].partition_broadcast(P)).then_inc(ld_xw, 16)
            sp.dma_start(xbo[:, :], a["xbo"].partition_broadcast(P)).then_inc(ld_xw, 16)
            sp.dma_start(xbq[:, :], a["xbq"]).then_inc(ld_xw, 16)
            sp.dma_start(xmask[:, :, :], a["mask"]).then_inc(ld_xw, 16)
            sp.dma_start(heads[:, :], a["c_heads"]).then_inc(ld_xw, 16)

            def layer_w1(l):
                sp.dma_start(w1[:, :, :], a["w1"][l].rearrange("(k p) c -> p k c", p=P)).then_inc(ld_w1, 16)

            def layer_wo(l):
                sp.dma_start(wo[:, :, :], a["wo"][l].rearrange("(k p) c -> p k c", p=P)).then_inc(ld_lwo, 16)

            def layer_w2(l):
                main = a["w2"][l, 0:FT * (NF - 1), :].rearrange("(k p) c -> p k c", p=FT)
                sp.dma_start(w2[:, 0:NF - 1, :], main).then_inc(ld_w2, 16)
                sp.dma_start(w2[0:FL, NF - 1, :], a["w2"][l, FT * (NF - 1):HID, :]).then_inc(ld_w2, 16)

            sp.dma_start(wqkv_raw[:, :, :], a["wqkv"][0].rearrange("(k p) c -> p k c", p=P)).then_inc(ld_wqkv, 16)
            layer_wo(0)
            def other_half(u):
                wait_read(sp, use_k(u))
                sp.dma_start(k2[ADH:P, 0].bitcast(F32), k2[0:ADH, 0].bitcast(F32)).then_inc(k_both, 16)
                sp.dma_start(k2[0:ADH, 1].bitcast(F32), k2[ADH:P, 1].bitcast(F32)).then_inc(k_both, 16)

            with sp.Fori(0, PAIRS - 1) as p:
                for j in range(B):
                    other_half(p * B + j)
                wait_full(sp, use_q(p * B + (B - 1)))
                sp.dma_start(wst[:, 0:2], a["w_pairs"][p + 1, :, 0:2]).then_inc(ld_qk, 16)
                wait_full(sp, use_v(p * B + (B - 1)))
                sp.dma_start(wst[:, 2], a["w_pairs"][p + 1, :, 2]).then_inc(ld_v, 16)
            for j in range(B):
                other_half(NU - B + j)
            wait_full(sp, use_z(NU - 1))
            for b in range(B):
                sp.dma_start(ctxT[:, :, b, :], a["ctxT"][b].rearrange("(k p) s -> p k s", p=P)).then_inc(ld_ctx[b], 16)
            for b in range(B):
                wait_read(sp, plan["xw", b, 0])
                wait_read(sp, plan["xw", b, 1])
                sp.dma_start(x2_dram[b].rearrange("(t p) e -> p t e", p=P), x[:, b, :, :]).then_inc(x2_st, 16)
            sp.wait_ge(ln_done, 3 * B)
            sp.wait_ge(x2_st, 16 * B)
            sp.dma_start(rot[:, :, :, :], a["c_rot"]).then_inc(ld_rot, 16)
            sp.dma_start(qk_scale[:, :, 0, :], a["q_scale"].partition_broadcast(P)).then_inc(ld_rot, 16)
            sp.dma_start(qk_scale[:, :, 1, :], a["k_scale"].partition_broadcast(P)).then_inc(ld_rot, 16)
            for l in range(DEPTH):
                sp.dma_start(lng[:, l, :], a["ln_g"][l]).then_inc(ld_small, 16)
                sp.dma_start(lnb[:, l, :], a["ln_b"][l]).then_inc(ld_small, 16)
                sp.dma_start(b1[:, l, :, :], a["b1"][l]).then_inc(ld_small, 16)
            sp.dma_start(b2[:, :, :], a["b2"].partition_broadcast(P)).then_inc(ld_small, 16)
            layer_w1(0)
            layer_w2(0)
            sp.wait_ge(set1, SET1)
            for m in range(STEPS):
                l, b = divmod(m, B)
                for tp in range(2):
                    wait_read(sp, plan["wo", m, tp])
                if m:
                    sp.wait_ge(f_hn, m)
                sp.dma_start(hs[1:P, :, :], y[0:P - 1, b, :, P:D]).then_inc(hs_ld, 16)
                sp.dma_start(hs[0:1, 1:T, :], y[P - 1:P, b, 0:T - 1, P:D]).then_inc(hs_ld, 16)
                if b == B - 3 and l + 1 < DEPTH:
                    for tp in range(2):
                        wait_full(sp, plan["w2", m, tp])
                    src = a["wqkv"][l + 1].rearrange("(k p) c -> p k c", p=P)
                    sp.dma_start(wqkv_next[:, :, :], src).then_inc(ld_wqkv, 16)
                if b == B - 1 and l + 1 < DEPTH:
                    layer_wo(l + 1)
                    wait_full(sp, plan["w1a", m, NF - 1])
                    layer_w1(l + 1)
                    for tp in range(2):
                        wait_full(sp, plan["w2", m, tp])
                    layer_w2(l + 1)
                if m == STEPS - 3:
                    for h in range(2):
                        for k in range(2):
                            wait_full(sp, plan["S", UNITS - FPAIRS - 1, h, k])
                    for i in range(B):
                        sp.dma_start(x2_back(i), x2_dram[i].rearrange("(t p) e -> p t e", p=P)).then_inc(x2_ld[i], 16)
            for b in range(B):
                dst = out[b].rearrange("(t p) e -> p t e", p=P)
                if b < B - 2:
                    sp.wait_ge(fin_done, b + 1)
                    sp.dma_start(dst, y[:, b, :, :]).then_inc(out_st, 16)
                else:
                    for tp in range(2):
                        wait_read(sp, plan["w2", STEPS - B + b, tp])
                        rows = slice(2 * tp, 2 * tp + 2)
                        sp.dma_start(dst[:, rows], y[:, b, rows, :]).then_inc(out_st, 16)
            sp.wait_ge(out_st, 16 * (B + 2))

        @block.gpsimd
        def _(pool):
            pool.memset(neg_half[:, :], -0.5).then_inc(set0, 1)
            pool.wait_ge(set0, 1)

            def norm_rstd(n):
                pool.wait_ge(ln_mv, T * (n + 1))
                pool.tensor_scalar(rstd[:, n % 2, :], mv[:, n % 2, :, 1], LN_EPS, None, ALU.add).then_inc(ln_eps, 1)
                pool.wait_ge(ln_eps, n + 1)
                pool.tensor_tensor(rstd[:, n % 2, :], rstd[:, n % 2, :], neg_half[:, 0:T], ALU.pow)\
                    .then_inc(ln_rstd, 1)

            for b in range(B):
                norm_rstd(b)

            def probabilities(u, j):
                for h in range(2):
                    pool.wait_ge(s_rden, 2 * u + (h + 1))
                    for i in range(T):
                        pr = probs[:, j % 2, h, TRI_AT[i]:TRI_AT[i + 1]]
                        ins = pool.tensor_tensor(pr, pr, rden[:, j % 2, h, i:i + 1].broadcast_to([P, TRI[i]]),
                                                 ALU.mult)
                    ins.then_inc(s_prob, 1)

            with pool.Fori(0, PAIRS) as p:
                for j in range(B):
                    probabilities(p * B + j, j)

            pool.wait_ge(ld_xw, 16 * 8)
            for b in range(B):
                norm_rstd(B + b)
                pool.wait_ge(ln_done, B + b + 1)
                for t in range(T):
                    ins = pool.tensor_tensor(x[:, b, t, :], x[:, b, t, :], xbo[:, :], ALU.add)
                ins.then_inc(bo_done, 1)
            for s in range(B + 2):
                if s < B:
                    pool.wait_ge(q_max, s + 1)
                    pool.tensor_tensor(qss[:, s % 2, :], qss[:, s % 2, :], neg_half[:, 0:E2], ALU.pow)\
                        .then_inc(q_rn, 1)
                if s >= 2:
                    norm_rstd(2 * B + s - 2)

            pool.wait_ge(ln_done, 3 * B)
            pool.wait_ge(x2_st, 16 * B)
            pool.memset(lqz[:, :, :, :, :], 0.0).then_inc(set1, 1)
            pool.memset(hT_hi[:, 1, 0:1].bitcast(F32), 0.0).then_inc(set1, 1)
            pool.memset(hT_lo[:, 1, 0:1].bitcast(F32), 0.0).then_inc(set1, 1)
            pool.memset(hs[0:1, 0, :], 0.0).then_inc(set1, 1)

            def local_probabilities(u):
                for h in range(2):
                    pool.wait_ge(l_rden, 2 * u + h + 1)
                    pr = lp[:, h, 0:P]
                    pool.tensor_tensor(pr, pr, lrden[:, u % 2, h, 0:1].broadcast_to([P, P]), ALU.mult)
                    pr = lp[:, h, P:LOC_N].rearrange("p (w c) -> p w c", c=LOC)
                    r = lrden[:, u % 2, h, 1:T].rearrange("p (w o) -> p w o", o=1).broadcast_to([P, T - 1, LOC])
                    pool.tensor_tensor(pr, pr, r, ALU.mult).then_inc(l_prob, 1)

            def rotate_q(m, t):
                wait_read(pool, plan["q", m, t])
                pool.tensor_tensor(ra[:, 0, :], ra[:, 0, :], rb[:, 0, :], ALU.add).then_inc(l_q, 1)

            def inverse_norms(m, t, i):
                pool.wait_ge(l_ssm, 2 * (T * m + t) + i + 1)
                pool.tensor_tensor(rn[:, m % 2, t, i, :], ss[:, i, :], neg_half[:, 0:FH], ALU.pow).then_inc(l_rn, 1)

            def rotate_k(m, t):
                n = T * m + t + 1
                wait_read(pool, plan["k", m, t])
                pool.tensor_tensor(ra[:, 1, :], ra[:, 1, :], rb[:, 1, :], ALU.add).then_inc(l_kadd, 1)
                inverse_norms(m, t, 1)
                pool.wait_ge(l_rn, 2 * n)
                pool.wait_ge(l_kadd, n)
                k3 = ra[:, 1, :].rearrange("p (h d) -> p h d", d=FDH)
                r = rn[:, m % 2, t, 1, :].rearrange("p (h o) -> p h o", o=1).broadcast_to([P, FH, FDH])
                pool.tensor_tensor(k3, k3, r, ALU.mult).then_inc(l_k, 1)

            def mlp_rstd(m):
                pool.wait_ge(f_mv, T * (m + 1))
                pool.tensor_scalar(rstd[:, 0, :], mv[:, 0, :, 1], LN_EPS, None, ALU.add).then_inc(f_eps, 1)
                pool.wait_ge(f_eps, m + 1)
                pool.tensor_tensor(rstd[:, 0, :], rstd[:, 0, :], neg_half[:, 0:T], ALU.pow).then_inc(f_rstd, 1)

            def mlp_bias(m):
                l, b = divmod(m, B)
                pool.wait_ge(f_hn, m + 1)
                if m == 0:
                    pool.wait_ge(ld_small, 16 * (3 * DEPTH + 1))
                if m >= STEPS - 2:
                    pool.wait_ge(x2_ld[b], 16)
                    xb = x2_back(b)
                    for t in range(T):
                        ins = pool.tensor_tensor(xb[:, t, :], xb[:, t, :], b2[:, l, :], ALU.add)
                    ins.then_inc(x2_b2, 1)
                    pool.wait_ge(x2_b2, m - (STEPS - 2) + 1)
                    pool.tensor_tensor(y[:, b, :, :], y[:, b, :, :], xb, ALU.add).then_inc(f_b2, 1)
                else:
                    for t in range(T):
                        ins = pool.tensor_tensor(y[:, b, t, :], y[:, b, t, :], b2[:, l, :], ALU.add)
                    ins.then_inc(f_b2, 1)

            def final_sum(b):
                for tp in range(2):
                    wait_read(pool, plan["w2", STEPS - B + b, tp])
                pool.wait_ge(x2_ld[b], 16)
                pool.tensor_tensor(y[:, b, :, :], y[:, b, :, :], x2_back(b), ALU.add).then_inc(fin_done, 1)

            for what, *at in order:
                if what == "soft":
                    local_probabilities(*at)
                if what == "qkv" and at[2] == "q":
                    rotate_q(at[0], at[1])
                    inverse_norms(at[0], at[1], 0)
                if what == "qkv" and at[2] == "k":
                    rotate_k(at[0], at[1])
                if what == "norm":
                    mlp_rstd(*at)
                if what == "bias":
                    mlp_bias(*at)
                if what == "sum":
                    final_sum(*at)

        @block.scalar
        def _(act):
            def copy(dst, src):
                return act.activation(dst, src, ACT.Copy)

            for b in range(B):
                for e in range(E2):
                    bank = wait_full(act, use_x(b, e))
                    copy(xnT[:, e, b, :], bank[:, :]).then_inc(read[use_x(b, e)[0]], 1)

            def round_q(u):
                bank = wait_full(act, use_q(u))
                copy(q2[0:ADH, 0, :], bank[0:ADH, :])
                copy(q2[ADH:P, 1, :], bank[ADH:P, :]).then_inc(q_hi, 1)

            def round_k(u):
                bank = wait_full(act, use_k(u))
                copy(k2[0:ADH, 0, 0, :], bank[0:ADH, :])
                copy(k2[ADH:P, 1, 0, :], bank[ADH:P, :]).then_inc(k_hi, 1)

            def evac_v(u, j):
                bank = wait_full(act, use_v(u))
                copy(v[:, j % 2, :, :], bank[:, :].rearrange("p (t c) -> p t c", c=P)).then_inc(read[use_v(u)[0]], 1)

            def exponentials(u, j, h):
                act.wait_ge(s_neg, 2 * u + (h + 1))
                for i in range(T):
                    pr = probs[:, j % 2, h, TRI_AT[i]:TRI_AT[i + 1]]
                    ins = act.activation(pr, pr, ACT.Exp, bias=negmax[:, j % 2, h, i:i + 1], scale=ADH ** -0.5,
                                         accum_out=den[:, j % 2, h, i:i + 1])
                ins.then_inc(s_exp, 1)

            def evac_pT(u, n):
                h, k = divmod(n, 3)
                bank = wait_full(act, use_t(u, h, k))
                at = KEYB_AT[T_TILES[k][0]]
                w = sum(KEYB[j] for j in T_TILES[k])
                copy(pT[:, h, at:at + w], bank[:, 0:w]).then_inc(read[use_t(u, h, k)[0]], 1)

            def attention_slot(u, j, ahead):
                evac_pT(u, 1)
                if ahead >= 1:
                    exponentials(u + 1, j + 1, 0)
                evac_pT(u, 3)
                if ahead >= 2:
                    round_k(u + 2)
                evac_pT(u, 5)
                if ahead >= 1:
                    exponentials(u + 1, j + 1, 1)
                if ahead >= 2:
                    round_q(u + 2)
                if ahead >= 2:
                    evac_v(u + 2, j)

            round_k(0)
            round_q(0)
            evac_v(0, 0)
            exponentials(0, 0, 0)
            exponentials(0, 0, 1)
            round_k(1)
            round_q(1)
            evac_v(1, 1)
            with act.Fori(0, PAIRS - 1) as p:
                for j in range(B):
                    attention_slot(p * B + j, j, 2)
            for j in range(B):
                attention_slot(NU - B + j, j, B - 1 - j)

            for b in range(B):
                for e in range(E2):
                    bank = wait_full(act, plan["x1T", b, e])
                    copy(xnT[:, e, b, :], bank[:, :]).then_inc(read[plan["x1T", b, e][0]], 1)
                act.wait_ge(k_min, b + 1)
                act.activation(ktmp[:, :, :], ktmp[:, :, :], ACT.Exp).then_inc(k_exp, 1)
                act.wait_ge(k_fin, b + 1)
                act.activation(ktmp[:, :, :], kf[:, b % 2, :, :], ACT.Square).then_inc(k_sq, 1)
                act.wait_ge(k_ss, b + 1)
                act.activation(knorm[:, b % 2, :, :], knorm[:, b % 2, :, :], ACT.Sqrt).then_inc(k_sqrt, 1)
            for s in range(B + 1):
                if s < B:
                    for e in range(E2):
                        bank = wait_full(act, plan["xq", s, e])
                        act.activation(qr[:, e, :], bank[:, :], ACT.Relu, bias=xbq[:, e:e + 1]).then_inc(q_relu, 1)
                    for e in range(E2):
                        wait_read(act, plan["xq", s, e])
                        act.activation(qm[:, e, :], qm[:, e, :], ACT.Exp).then_inc(q_exp, 1)
                    for e in range(E2):
                        act.wait_ge(q_fin, 2 * s + e + 1)
                        act.activation(qm[:, e, :], qT[:, s % 2, e, :], ACT.Square,
                                       accum_out=qss[:, s % 2, e:e + 1]).then_inc(q_sq, 1)
                if s >= 1:
                    for e in range(E2):
                        use = plan["xo", s - 1, e]
                        bank = wait_full(act, use)
                        copy(oxT[:, (s - 1) % 2, e, :], bank[:, :]).then_inc(read[use[0]], 1)

            def round_weights(l):
                act.wait_ge(ld_wqkv, 16 * (l + 1))
                if l:
                    wait_full(act, plan["k", B * l - 1, T - 1])
                src = wqkv_next if l else wqkv_raw
                for c in (2, 0, 1):
                    cols = slice(c * INNER, (c + 1) * INNER)
                    copy(wqkv_hi[:, :, cols], src[:, :, cols]).then_inc(w_hi, 1)

            def evac_hT(m):
                for e in range(E2):
                    bank = wait_full(act, plan["hT", m, e])
                    copy(hT_hi[:, e, e:S + e], bank[:, :]).then_inc(h_hi, 1)

            def qkv_tile(m, t, what):
                use = plan[what, m, t]
                bank = wait_full(act, use)
                if what == "v":
                    copy(lv[:, m % 2, t, :], bank[:, :]).then_inc(read[use[0]], 1)
                    return
                i = "qk".index(what)
                if m or t:
                    act.wait_ge(l_ss, 2 * (T * m + t - 1) + i + 1)
                act.activation(sq[:, i, :], bank[:, :], ACT.Square).then_inc(l_sq, 1)

            def evac_tq(m, t):
                use = plan["Tq", m, t]
                src = wait_full(act, use)[:, :].rearrange("p (j s) -> p j s", s=P)
                cols = slice(t * P, (t + 1) * P)
                copy(lqz[0:FDH, m % 2, :, 0, cols], src[0:FDH])
                copy(lqz[FDH:P, m % 2, :, 1, cols], src[FDH:P]).then_inc(read[use[0]], 1)

            def local_exponentials(u):
                m, j = divmod(u, FPAIRS)
                for h in range(2):
                    act.wait_ge(l_neg, 2 * u + h + 1)
                    for w in range(T):
                        pr = lp[:, h, loc_at(w):loc_at(w + 1)]
                        ins = act.activation(pr, pr, ACT.Exp, bias=lneg[:, u % 2, h, w:w + 1],
                                             scale=rn[:, m % 2, w, 0, 2 * j + h:2 * j + h + 1],
                                             accum_out=lden[:, u % 2, h, w:w + 1])
                    ins.then_inc(l_exp, 1)

            def evac_T(u, h):
                use = plan["T", u, h, 0]
                bank = wait_full(act, use)
                copy(lpT[:, h, 0:S], bank[:, :]).then_inc(read[use[0]], 1)

            def evac_O(u):
                use = plan["O", u]
                bank = wait_full(act, use)
                copy(loT[:, u % FPAIRS, :], bank[:, :]).then_inc(read[use[0]], 1)

            def evac_hnT(m):
                l = m // B
                for e in range(E2):
                    use = plan["hnT", m, e]
                    bank = wait_full(act, use)
                    act.activation(hnT[:, e, :], bank[:, :], ACT.Identity, bias=lnb[:, l, e:e + 1],
                                   scale=lng[:, l, e:e + 1]).then_inc(read[use[0]], 1)

            def gates(m, f):
                use = plan["w1g", m, f]
                bank = wait_full(act, use)
                if f >= GELU_T:
                    wait_read(act, plan["w1a", m, f - GELU_T])
                rows = frows(f)
                act.activation(gl[0:rows, f % GELU_T, :], bank[0:rows, :], ACT.Gelu,
                               bias=b1[0:rows, m // B, 1, f:f + 1]).then_inc(read[use[0]], 1)

            act.wait_ge(set1, SET1)
            round_weights(0)
            for what, *at in order:
                if what == "soft" and at[0] == (B - 1) * FPAIRS:
                    round_weights(1)
                if what == "hT":
                    evac_hT(*at)
                if what == "qkv":
                    qkv_tile(*at)
                if what == "Tqk":
                    evac_tq(*at)
                if what == "S":
                    local_exponentials(*at)
                if what == "T":
                    evac_T(*at)
                if what == "AV":
                    evac_O(*at)
                if what == "hnT":
                    if at[0] == 0:
                        act.wait_ge(ld_small, 16 * (3 * DEPTH + 1))
                    evac_hnT(*at)
                if what == "w1":
                    gates(*at)

        @block.vector
        def _(dve):
            def norm_stats(n, src):
                for t in range(T):
                    dve.bn_stats(stats[:, n % 2, t, 0:6], src[:, t, :]).then_inc(ln_stats, 1)
                dve.wait_ge(ln_stats, T * (n + 1))
                for t in range(T):
                    dve.bn_aggr(mv[:, n % 2, t, :], stats[:, n % 2, t, 0:6]).then_inc(ln_mv, 1)

            def norm_apply(n, src, dst):
                dve.wait_ge(ln_mv, T * (n + 1))
                dve.wait_ge(ln_rstd, n + 1)
                for t in range(T):
                    ins = dve.tensor_scalar(dst[:, t, :], src[:, t, :], mv[:, n % 2, t, 0:1], rstd[:, n % 2, t:t + 1],
                                            ALU.subtract, ALU.mult)
                ins.then_inc(ln_done, 1)

            dve.wait_ge(ld_const, 16 * 3)
            for b in range(B + 1):
                if b < B:
                    dve.wait_ge(ld_x[b], 16)
                    norm_stats(b, x[:, b])
                if b >= 1:
                    if b >= 3:
                        wait_full(dve, use_x(b - 3, 0))
                        wait_full(dve, use_x(b - 3, 1))
                    norm_apply(b - 1, x[:, b - 1], xn[:, (b - 1) % 2])

            def rest_of_q(u):
                bank = wait_full(dve, use_q(u))
                dve.wait_ge(q_hi, u + 1)
                dve.tensor_tensor(q2[ADH:P, 0, :], bank[0:ADH, :], q2[0:ADH, 0, :], ALU.subtract)
                dve.tensor_tensor(q2[0:ADH, 1, :], bank[ADH:P, :], q2[ADH:P, 1, :], ALU.subtract)\
                    .then_inc(read[use_q(u)[0]], 1)

            def rest_of_k(u):
                bank = wait_full(dve, use_k(u))
                dve.wait_ge(k_hi, u + 1)
                dve.tensor_tensor(k2[0:ADH, 0, 1, :], bank[0:ADH, :], k2[0:ADH, 0, 0, :], ALU.subtract)
                dve.tensor_tensor(k2[ADH:P, 1, 1, :], bank[ADH:P, :], k2[ADH:P, 1, 0, :], ALU.subtract)\
                    .then_inc(read[use_k(u)[0]], 1)

            def masked_scores(u, j, h):
                for k, blocks in enumerate(S_TILES):
                    bank = wait_full(dve, use_s(u, h, k))
                    pass_wait(dve, passed_v)
                    at = 0
                    for i in blocks:
                        ins = dve.tensor_tensor_reduce(
                            probs[:, j % 2, h, TRI_AT[i]:TRI_AT[i + 1]], bank[:, at:at + TRI[i]],
                            causal[:, S - TRI[i]:S], 1.0, -3e38, ALU.add, ALU.max, rowmax[:, j % 2, h, i:i + 1])
                        at += TRI[i]
                    ins.then_inc(read[k], 1)
                for k in range(3):
                    wait_read(dve, use_s(u, h, k))
                dve.tensor_scalar(negmax[:, j % 2, h, :], rowmax[:, j % 2, h, :], -ADH ** -0.5, None, ALU.mult)\
                    .then_inc(s_neg, 1)

            def inverse_sums(u, j, h):
                dve.wait_ge(s_exp, 2 * u + (h + 1))
                dve.reciprocal(rden[:, j % 2, h, :], den[:, j % 2, h, :]).then_inc(s_rden, 1)

            def evac_pT(u, n):
                h, k = divmod(n, 3)
                bank = wait_full(dve, use_t(u, h, k))
                at = KEYB_AT[T_TILES[k][0]]
                w = sum(KEYB[j] for j in T_TILES[k])
                dve.tensor_copy(pT[:, h, at:at + w], bank[:, 0:w]).then_inc(read[use_t(u, h, k)[0]], 1)

            def attention_slot(u, j, ahead, z):
                for h in range(2):
                    if ahead >= 1:
                        masked_scores(u + 1, j + 1, h)
                    evac_pT(u, 2 * h)
                if ahead >= 1:
                    inverse_sums(u + 1, j + 1, 0)
                evac_pT(u, 4)
                if ahead >= 2:
                    rest_of_k(u + 2)
                if ahead >= 1:
                    inverse_sums(u + 1, j + 1, 1)
                if ahead >= 2:
                    rest_of_q(u + 2)
                bank = wait_full(dve, use_z(u))
                dve.tensor_copy(z, bank[:, :]).then_inc(read[5], 1)

            rest_of_k(0)
            rest_of_q(0)
            for h in range(2):
                masked_scores(0, 0, h)
            for h in range(2):
                inverse_sums(0, 0, h)
            rest_of_k(1)
            rest_of_q(1)
            zflat = zT[:, :, :, :].rearrange("p k b s -> p (k b s)")
            with dve.Fori(0, PAIRS - 1) as p:
                for j in range(B):
                    attention_slot(p * B + j, j, 2, zflat[:, bass.ds((p * B + j) * S, S)])
            for j in range(B):
                attention_slot(NU - B + j, j, B - 1 - j, zT[:, PAIRS - 1, j, :])

            dve.wait_ge(ld_xw, 16 * 8)
            dve.tensor_scalar(xkeep[:, :, :], xmask[:, :, :], -1.0, 1.0, ALU.mult, ALU.add).then_inc(k_keep, 1)

            def add_attention(b):
                for tp in range(2):
                    use = plan["awo", b, tp]
                    bank = wait_full(dve, use)
                    xs = x[:, b, 2 * tp:2 * tp + 2, :]
                    dve.tensor_tensor(xs, bank[:, :].rearrange("p (t e) -> p t e", e=D), xs, ALU.add)\
                        .then_inc(read[use[0]], 1)

            def norm2_stats(b):
                wait_read(dve, plan["awo", b, 0])
                wait_read(dve, plan["awo", b, 1])
                norm_stats(B + b, x[:, b])

            def norm2_apply(b):
                if b >= 2:
                    wait_full(dve, plan["x1T", b - 2, 0])
                    wait_full(dve, plan["x1T", b - 2, 1])
                norm_apply(B + b, x[:, b], xn[:, b % 2])

            def add_kv_bias(b):
                for t in range(T):
                    use = plan["kv", b, t]
                    bank = wait_full(dve, use)
                    dve.tensor_tensor(kv[:, b % 2, t, :], bank[:, :], xbkv[:, :], ALU.add).then_inc(read[use[0]], 1)

            def keys(b):
                for t in range(T):
                    wait_read(dve, plan["kv", b, t])
                k = kv[:, b % 2, :, 0:D]
                dve.tensor_scalar(ktmp[:, :, :], k, 0.0, None, ALU.min).then_inc(k_min, 1)
                dve.wait_ge(k_exp, b + 1)
                dve.scalar_tensor_tensor(kf[:, b % 2, :, :], k, 0.0, ktmp[:, :, :], ALU.max, ALU.add).then_inc(k_fin, 1)
                dve.wait_ge(k_sq, b + 1)
                norm = knorm[:, b % 2, :, :]
                dve.tensor_reduce(norm.rearrange("p t h -> p (t h)"),
                                  ktmp[:, :, :].rearrange("p t (h d) -> p (t h) d", d=XDH), AX.X, ALU.add)\
                    .then_inc(k_ss, 1)
                dve.wait_ge(k_sqrt, b + 1)
                dve.tensor_scalar(norm, norm, NORM_EPS, None, ALU.max).then_inc(k_rec, 1)
                dve.wait_ge(k_rec, 3 * b + 1)
                dve.reciprocal(norm, norm).then_inc(k_rec, 1)
                dve.wait_ge(k_rec, 3 * b + 2)
                dve.wait_ge(k_keep, 1)
                keep = xkeep[:, b, :].rearrange("p (t o) -> p t o", o=1).broadcast_to([P, T, XH])
                dve.tensor_tensor(norm, norm, keep, ALU.mult).then_inc(k_rec, 1)
                dve.wait_ge(k_rec, 3 * b + 3)
                k3 = kf[:, b % 2, :, :].rearrange("p t (h d) -> p (t h) d", d=XDH)
                r = norm.rearrange("p t h -> p (t h)").rearrange("p (g o) -> p g o", o=1)\
                    .broadcast_to([P, T * XH, XDH])
                dve.tensor_tensor(k3, k3, r, ALU.mult).then_inc(k_done, 1)

            def mask_kv(b):
                use = plan["KV", b]
                bank = wait_full(dve, use)
                for e in range(E2):
                    ins = dve.tensor_tensor(kvm[:, b, e, :], bank[:, e * P:(e + 1) * P], heads[:, :], ALU.mult)
                ins.then_inc(read[use[0]], 1)

            add_attention(0)
            norm2_stats(0)
            add_attention(1)
            norm2_stats(1)
            norm2_apply(0)
            add_attention(2)
            norm2_apply(1)
            add_attention(3)
            add_kv_bias(0)
            norm2_stats(2)
            norm2_apply(2)
            keys(0)
            add_kv_bias(1)
            norm2_stats(3)
            norm2_apply(3)
            keys(1)
            mask_kv(0)
            add_kv_bias(2)
            keys(2)
            mask_kv(1)
            add_kv_bias(3)
            keys(3)
            mask_kv(2)
            mask_kv(3)

            for s in range(B + 2):
                if s < B:
                    for e in range(E2):
                        use = plan["xq", s, e]
                        bank = wait_full(dve, use)
                        dve.wait_ge(q_relu, 2 * s + e + 1)
                        dve.tensor_scalar(qm[:, e, :], bank[:, :], xbq[:, e:e + 1], 0.0, ALU.add, ALU.min)\
                            .then_inc(read[use[0]], 1)
                    for e in range(E2):
                        dve.wait_ge(q_exp, 2 * s + e + 1)
                        dve.tensor_tensor(qT[:, s % 2, e, :], qr[:, e, :], qm[:, e, :], ALU.add).then_inc(q_fin, 1)
                if s >= 2:
                    b = s - 2
                    dve.wait_ge(bo_done, b + 1)
                    for tp in range(2):
                        use = plan["xw", b, tp]
                        bank = wait_full(dve, use)
                        xs = x[:, b, 2 * tp:2 * tp + 2, :]
                        dve.tensor_tensor(xs, bank[:, :].rearrange("p (t e) -> p t e", e=D), xs, ALU.add)\
                            .then_inc(read[use[0]], 1)
                    for tp in range(2):
                        wait_read(dve, plan["xw", b, tp])
                    norm_stats(2 * B + b, x[:, b])
                if s < B:
                    dve.wait_ge(q_sq, 2 * s + 2)
                    dve.tensor_scalar(qss[:, s % 2, :], qss[:, s % 2, :], NORM_EPS ** 2, None, ALU.max).then_inc(q_max, 1)
                    dve.wait_ge(q_rn, s + 1)
                    for tp in range(2):
                        wait_read(dve, plan["KV", s])
                    for e in range(E2):
                        dve.tensor_scalar(kvs[:, s % 2, e, :], kvm[:, s, e, :], qss[:, s % 2, e:e + 1], None, ALU.mult)\
                            .then_inc(kvs_done, 1)
                if s >= 2:
                    norm_apply(2 * B + s - 2, x[:, s - 2], y[:, s - 2])

            def tables(l):
                H = FDH // 2
                for i in range(2):
                    sc = qk_scale[:, l, i, :].rearrange("p (o d) -> p o d", o=1)
                    by = 1.0 if i else QK_SCALE
                    dve.scalar_tensor_tensor(tab[l][:, 2 * i, :, :], rot[:, 2 * i, :, :], by,
                                             sc.broadcast_to([P, T, FDH]), ALU.mult, ALU.mult).then_inc(l_tab, 1)
                    for lo, other in ((0, H), (H, 0)):
                        dve.scalar_tensor_tensor(tab[l][:, 2 * i + 1, :, lo:lo + H], rot[:, 2 * i + 1, :, lo:lo + H],
                                                 by, sc[:, :, other:other + H].broadcast_to([P, T, H]),
                                                 ALU.mult, ALU.mult).then_inc(l_tab, 1)

            def rest_of_weights(l):
                src = wqkv_next if l else wqkv_raw
                for i, c in enumerate((2, 0, 1)):
                    cols = slice(c * INNER, (c + 1) * INNER)
                    dve.wait_ge(w_hi, 3 * l + i + 1)
                    dve.tensor_tensor(wqkv_lo[:, :, cols], src[:, :, cols], wqkv_hi[:, :, cols], ALU.subtract)\
                        .then_inc(w_lo, 1)

            def evac_hT(m):
                for e in range(E2):
                    use = plan["hT", m, e]
                    bank = wait_full(dve, use)
                    dve.wait_ge(h_hi, E2 * m + e + 1)
                    dve.tensor_tensor(hT_lo[:, e, e:S + e], bank[:, :], hT_hi[:, e, e:S + e], ALU.subtract)\
                        .then_inc(read[use[0]], 1)

            def qkv_tile(m, t, what):
                n = T * m + t
                l = m // B
                i = "qk".index(what)
                use = plan[what, m, t]
                bank = wait_full(dve, use)
                dve.wait_ge(l_sq, 2 * n + i + 1)
                src = bank[:, :].rearrange("p (h d) -> p h d", d=FDH)
                cos = tab[l][:, 2 * i, t:t + 1, :].broadcast_to([P, FH, FDH])
                dve.tensor_tensor(ra[:, i, :].rearrange("p (h d) -> p h d", d=FDH), src, cos, ALU.mult)
                swapped = bank[:, :].rearrange("p (h a d) -> p h a d", a=2, d=FDH // 2)[:, :, ::-1, :]
                sin = tab[l][:, 2 * i + 1, t:t + 1, :].broadcast_to([P, FH, FDH])\
                    .rearrange("p h (a d) -> p h a d", a=2)
                dve.tensor_tensor(rb[:, i, :].rearrange("p (h a d) -> p h a d", a=2, d=FDH // 2), swapped, sin,
                                  ALU.mult).then_inc(read[use[0]], 1)
                if n:
                    dve.wait_ge(l_rn, 2 * (n - 1) + i + 1)
                dve.tensor_reduce(ss[:, i, :], sq[:, i, :].rearrange("p (h d) -> p h d", d=FDH), AX.X, ALU.add)\
                    .then_inc(l_ss, 1)
                dve.wait_ge(l_ss, 2 * n + i + 1)
                dve.tensor_scalar(ss[:, i, :], ss[:, i, :], NORM_EPS ** 2, None, ALU.max).then_inc(l_ssm, 1)

            def evac_tk(m, t):
                use = plan["Tk", m, t]
                bank = wait_full(dve, use)
                dve.tensor_copy(lkT[:, m % 2, :, t * P:(t + 1) * P], bank[:, :].rearrange("p (j s) -> p j s", s=P))\
                    .then_inc(read[use[0]], 1)

            def local_scores(u):
                m, j = divmod(u, FPAIRS)
                if j == 0:
                    dve.wait_ge(l_rn, 2 * T * (m + 1))
                for h in range(2):
                    for k in range(2):
                        use = plan["S", u, h, k]
                        bank = wait_full(dve, use)
                        at = 0
                        for w in (2 * k, 2 * k + 1):
                            lo, hi = loc_at(w), loc_at(w + 1)
                            ins = dve.tensor_tensor_reduce(
                                lp[:, h, lo:hi], bank[:, at:at + hi - lo], local[:, LOC - (hi - lo):LOC], 1.0,
                                -3e38, ALU.add, ALU.max, lmax[:, u % 2, h, w:w + 1])
                            at += hi - lo
                        ins.then_inc(read[use[0]], 1)
                    for k in range(2):
                        wait_read(dve, plan["S", u, h, k])
                    dve.scalar_tensor_tensor(lneg[:, u % 2, h, :], lmax[:, u % 2, h, :], -1.0,
                                             rn[:, m % 2, :, 0, 2 * j + h], ALU.mult, ALU.mult).then_inc(l_neg, 1)

            def local_inverse_sums(u):
                for h in range(2):
                    dve.wait_ge(l_exp, 2 * u + h + 1)
                    dve.reciprocal(lrden[:, u % 2, h, :], lden[:, u % 2, h, :]).then_inc(l_rden, 1)

            def evac_T(u, h):
                use = plan["T", u, h, 1]
                bank = wait_full(dve, use)
                dve.tensor_copy(lpT[:, h, S:LOC_N], bank[:, 0:LOC_N - S]).then_inc(read[use[0]], 1)

            def add_to_y(what, m, tp):
                use = plan[what, m, tp]
                bank = wait_full(dve, use)
                ys = y[:, m % B, 2 * tp:2 * tp + 2, :]
                dve.tensor_tensor(ys, bank[:, :].rearrange("p (t e) -> p t e", e=D), ys, ALU.add)\
                    .then_inc(read[use[0]], 1)

            def mlp_stats(m):
                for tp in range(2):
                    wait_read(dve, plan["wo", m, tp])
                for t in range(T):
                    dve.bn_stats(stats[:, 0, t, 0:6], y[:, m % B, t, 0:P]).then_inc(f_stats, 1)

            def mlp_norm(m):
                dve.wait_ge(hs_ld, 32 * (m + 1))
                for t in range(T):
                    dve.bn_stats(stats[:, 0, t, 6:12], hs[:, t, :]).then_inc(f_stats, 1)
                dve.wait_ge(f_stats, 2 * T * (m + 1))
                for t in range(T):
                    dve.bn_aggr(mv[:, 0, t, :], stats[:, 0, t, :]).then_inc(f_mv, 1)

            def mlp_apply(m):
                b = m % B
                dve.wait_ge(f_mv, T * (m + 1))
                dve.wait_ge(f_rstd, m + 1)
                for t in range(T):
                    dve.tensor_scalar(hn[:, t, 0:P], y[:, b, t, 0:P], mv[:, 0, t, 0:1], rstd[:, 0, t:t + 1],
                                      ALU.subtract, ALU.mult)
                    ins = dve.tensor_scalar(hn[:, t, P:D], hs[:, t, :], mv[:, 0, t, 0:1], rstd[:, 0, t:t + 1],
                                            ALU.subtract, ALU.mult)
                ins.then_inc(f_hn, 1)

            def hidden(m, f):
                use = plan["w1a", m, f]
                wait_read(dve, plan["w1g", m, f])
                bank = wait_full(dve, use)
                rows = frows(f)
                dve.scalar_tensor_tensor(hid[0:rows, f, :], bank[0:rows, :], b1[0:rows, m // B, 0, f:f + 1],
                                         gl[0:rows, f % GELU_T, :], ALU.add, ALU.mult).then_inc(read[use[0]], 1)

            dve.wait_ge(x2_st, 16 * B)
            dve.wait_ge(ln_done, 3 * B)
            dve.wait_ge(set1, SET1)
            rest_of_weights(0)
            dve.wait_ge(ld_rot, 16 * 3)
            tables(0)
            for what, *at in order:
                if what == "hT":
                    if at[0] == 0:
                        evac_hT(0)
                        dve.wait_ge(l_tab, 6)
                        continue
                    if at[0] == 2:
                        tables(1)
                        dve.wait_ge(l_tab, 12)
                    evac_hT(*at)
                if what == "qkv" and at[2] != "v":
                    if at[0] == 0 and at[1] and at[2] == "q":
                        wait_full(dve, plan["Tk", 0, at[1] - 1])
                    qkv_tile(*at)
                if what == "Tqk":
                    evac_tk(*at)
                if what == "S":
                    local_scores(*at)
                if what == "soft":
                    if at[0] == (B - 1) * FPAIRS:
                        rest_of_weights(1)
                    local_inverse_sums(*at)
                if what == "T":
                    evac_T(*at)
                if what == "wo":
                    add_to_y("wo", *at)
                if what == "stats":
                    mlp_stats(*at)
                if what == "norm":
                    mlp_norm(*at)
                if what == "apply":
                    mlp_apply(*at)
                if what == "w1":
                    if at[0] == 0 and at[1] == 0:
                        dve.wait_ge(ld_small, 16 * (3 * DEPTH + 1))
                    hidden(*at)
                if what == "w2":
                    dve.wait_ge(f_b2, at[0] + 1)
                    add_to_y("w2", *at)

        @block.tensor
        def _(pe):
            mm = pe.matmul

            def product(dst, pairs, last=None, **kw):
                for i, (lhsT, rhs) in enumerate(pairs):
                    ins = mm(dst, lhsT, rhs, start=i == 0, stop=i == len(pairs) - 1, **kw)
                return ins

            pe.wait_ge(ld_const, 16 * 3)
            for b in range(B):
                pe.wait_ge(ln_done, b + 1)
                for e in range(E2):
                    bank = wait_free(pe, use_x(b, e))
                    for t in range(T):
                        ins = pe.transpose(bank[:, t * P:(t + 1) * P], xn[:, b % 2, t, e * P:(e + 1) * P], ident[:, :])
                    ins.then_inc(full[use_x(b, e)[0]], 1)

            def project_qk(u, b, p, i):
                if i == 1:
                    pe.wait_ge(ld_qk, 16 * (p + 1))
                use = use_k(u) if i else use_q(u)
                bank = wait_free(pe, use)
                product(bank[:, :], [(wst[:, i, e, :], xnT[:, e, b, :]) for e in range(E2)]).then_inc(full[use[0]], 1)

            def project_v(u, b, p):
                pe.wait_ge(ld_v, 16 * (p + 1))
                use = use_v(u)
                bank = wait_free(pe, use)
                for t in range(T):
                    ins = product(bank[:, t * P:(t + 1) * P],
                                  [(xnT[:, e, b, t * P:(t + 1) * P], wst[:, 2, e, :]) for e in range(E2)])
                ins.then_inc(full[use[0]], 1)

            def scores(u, h):
                if h == 0:
                    wait_read(pe, use_q(u))
                    pe.wait_ge(k_both, 32 * u + 32)
                for k, blocks in enumerate(S_TILES):
                    bank = wait_free(pe, use_s(u, h, k))
                    at = 0
                    for i in blocks:
                        n = max(TRI[i], LOC)
                        ins = product(bank[:, at:at + n], [(k2[:, h, part, i * P:(i + 1) * P], q2[:, h, 0:n])
                                                           for part in (1, 0)])
                        at += TRI[i]
                    ins.then_inc(full[k], 1)

            def transposes(u, j, n):
                h, k = divmod(n, 3)
                if k == 0:
                    pe.wait_ge(s_prob, 2 * u + (h + 1))
                use = use_t(u, h, k)
                bank = wait_free(pe, use)
                at = 0
                for c in T_TILES[k]:
                    for i in range(c, T):
                        lo = TRI_AT[i] + c * P
                        ins = pe.transpose(bank[:, at:at + P], probs[:, j % 2, h, lo:lo + P], ident[:, :])
                        at += P
                ins.then_inc(full[use[0]], 1)

            def weighted_values(u, j):
                for k in (1, 2):
                    wait_read(pe, use_t(u, 1, k))
                wait_read(pe, use_v(u))
                bank = wait_free(pe, use_z(u))
                for c in range(T):
                    for h in range(2):
                        rows = slice(h * ADH, (h + 1) * ADH)
                        ins = mm(bank[rows, c * P:S], v[:, j % 2, c, rows],
                                 pT[:, h, KEYB_AT[c]:KEYB_AT[c] + KEYB[c]], start=c == 0, stop=c == T - 1)
                ins.then_inc(full[5], 1)

            def attention_slot(u, j, p, ahead):
                at = ((j + 2) % B, p + (j + 2) // B)
                if ahead >= 1:
                    scores(u + 1, 0)
                transposes(u, j, 0)
                transposes(u, j, 1)
                if ahead >= 1:
                    scores(u + 1, 1)
                transposes(u, j, 2)
                transposes(u, j, 3)
                if ahead >= 2:
                    project_qk(u + 2, *at, 1)
                transposes(u, j, 4)
                transposes(u, j, 5)
                if ahead >= 2:
                    project_qk(u + 2, *at, 0)
                weighted_values(u, j)
                if ahead >= 2:
                    project_v(u + 2, *at)

            wait_read(pe, use_x(B - 1, 0))
            wait_read(pe, use_x(B - 2, 1))
            wait_read(pe, use_x(B - 1, 1))
            for b in range(2):
                project_qk(b, b, 0, 1)
                project_qk(b, b, 0, 0)
                project_v(b, b, 0)
                if b == 0:
                    scores(0, 0)
                    scores(0, 1)
            with pe.Fori(0, PAIRS - 1) as p:
                for j in range(B):
                    attention_slot(p * B + j, j, p, 2)
            for j in range(B):
                attention_slot(NU - B + j, j, PAIRS - 1, B - 1 - j)

            pe.wait_ge(ld_wo, 16)
            for b in range(B):
                wait_read(pe, use_z(NU - B + b))
                for tp in range(2):
                    use = plan["awo", b, tp]
                    bank = wait_free(pe, use)
                    for i in range(2):
                        t = 2 * tp + i
                        ins = product(bank[:, i * D:(i + 1) * D],
                                      [(zT[:, k, b, t * P:(t + 1) * P], woT[:, k, :]) for k in range(PAIRS)])
                    ins.then_inc(full[use[0]], 1)

            def keys_values(b):
                for t in range(T):
                    use = plan["kv", b, t]
                    bank = wait_free(pe, use)
                    product(bank[:, :], [(ctxT[:, e, b, t * P:(t + 1) * P], xwkv[:, e, :]) for e in range(E2)])\
                        .then_inc(full[use[0]], 1)

            def norm2_T(b):
                pe.wait_ge(ln_done, B + b + 1)
                for e in range(E2):
                    use = plan["x1T", b, e]
                    bank = wait_free(pe, use)
                    for t in range(T):
                        ins = pe.transpose(bank[:, t * P:(t + 1) * P], xn[:, b % 2, t, e * P:(e + 1) * P], ident[:, :])
                    ins.then_inc(full[use[0]], 1)

            def k_t_v(b):
                pe.wait_ge(k_done, b + 1)
                use = plan["KV", b]
                bank = wait_free(pe, use)
                for e in range(E2):
                    ins = product(bank[:, e * P:(e + 1) * P],
                                  [(kf[:, b % 2, t, e * P:(e + 1) * P], kv[:, b % 2, t, D + e * P:D + (e + 1) * P])
                                   for t in range(T)])
                ins.then_inc(full[use[0]], 1)

            pe.wait_ge(ld_xw, 16 * 8)
            for b in range(B):
                pe.wait_ge(ld_ctx[b], 16)
                keys_values(b)
                norm2_T(b)
                if b:
                    k_t_v(b - 1)
            k_t_v(B - 1)
            for s in range(B + 2):
                if s < B:
                    for e in range(E2):
                        wait_read(pe, plan["x1T", s, e])
                    for c in range(E2):
                        use = plan["xq", s, c]
                        bank = wait_free(pe, use)
                        product(bank[:, :], [(xwq[:, e, c * P:(c + 1) * P], xnT[:, e, s, :]) for e in range(E2)])\
                            .then_inc(full[use[0]], 1)
                if 1 <= s <= B:
                    b = s - 1
                    pe.wait_ge(kvs_done, 2 * (b + 1))
                    for e in range(E2):
                        use = plan["xo", b, e]
                        bank = wait_free(pe, use)
                        product(bank[:, :], [(kvs[:, b % 2, e, :], qT[:, b % 2, e, :])]).then_inc(full[use[0]], 1)
                if s >= 2:
                    b = s - 2
                    for e in range(E2):
                        wait_read(pe, plan["xo", b, e])
                    for tp in range(2):
                        use = plan["xw", b, tp]
                        bank = wait_free(pe, use)
                        for i in range(2):
                            t = 2 * tp + i
                            ins = product(bank[:, i * D:(i + 1) * D],
                                          [(oxT[:, b % 2, e, t * P:(t + 1) * P], xwo[:, e, :]) for e in range(E2)])
                        ins.then_inc(full[use[0]], 1)

            def transposed_y(m):
                l, b = divmod(m, B)
                if l:
                    for tp in range(2):
                        wait_read(pe, plan["w2", m - B, tp])
                for e in range(E2):
                    use = plan["hT", m, e]
                    bank = wait_free(pe, use)
                    for t in range(T):
                        ins = pe.transpose(bank[:, t * P:(t + 1) * P], y[:, b, t, e * P:(e + 1) * P], ident[:, :])
                    ins.then_inc(full[use[0]], 1)

            def qkv_tile(m, t, what):
                l = m // B
                if t == 0:
                    if what == "v":
                        for e in range(E2):
                            wait_read(pe, plan["hT", m, e])
                    if m % B == 0:
                        pe.wait_ge(w_lo, 3 * l + "vqk".index(what) + 1)
                use = plan[what, m, t]
                bank = wait_free(pe, use)
                cols = slice("qkv".index(what) * INNER, ("qkv".index(what) + 1) * INNER)
                rows = slice(t * P, (t + 1) * P)
                product(bank[:, :], [(h[:, e, rows], w[:, e, cols]) for e in range(E2)
                                     for h, w in ((hT_lo, wqkv_hi), (hT_hi, wqkv_lo), (hT_hi, wqkv_hi))])\
                    .then_inc(full[use[0]], 1)

            def transposed_qk(m, t):
                for i, (what, done) in enumerate((("Tq", l_q), ("Tk", l_k))):
                    pe.wait_ge(done, T * m + t + 1)
                    use = plan[what, m, t]
                    bank = wait_free(pe, use)
                    for j in range(FPAIRS):
                        ins = pe.transpose(bank[:, j * P:(j + 1) * P], ra[:, i, j * P:(j + 1) * P], ident[:, :])
                    ins.then_inc(full[use[0]], 1)

            def local_scores(u):
                m, j = divmod(u, FPAIRS)
                if j == 0:
                    wait_read(pe, plan["Tq", m, T - 1])
                    wait_read(pe, plan["Tk", m, T - 1])
                for h in range(2):
                    for k in range(2):
                        use = plan["S", u, h, k]
                        bank = wait_free(pe, use)
                        at = 0
                        for w in (2 * k, 2 * k + 1):
                            lo = max(w - 1, 0) * P
                            n = (w + 1) * P - lo
                            ins = mm(bank[:, at:at + n], lqz[:, m % 2, j, h, w * P:(w + 1) * P],
                                     lkT[:, m % 2, j, lo:lo + n], start=True, stop=True)
                            at += n
                        ins.then_inc(full[use[0]], 1)

            def local_transposes(u, h):
                pe.wait_ge(l_prob, 2 * u + h + 1)
                for k in range(2):
                    use = plan["T", u, h, k]
                    bank = wait_free(pe, use)
                    at = 0
                    for c in (2 * k, 2 * k + 1):
                        for w in range(c, min(c + 2, T)):
                            lo = loc_at(w) + (P if w == c and w else 0)
                            ins = pe.transpose(bank[:, at:at + P], lp[:, h, lo:lo + P], ident[:, :])
                            at += P
                    ins.then_inc(full[use[0]], 1)

            def local_values(u):
                m, j = divmod(u, FPAIRS)
                for k in range(2):
                    wait_read(pe, plan["T", u, 1, k])
                if j == 0:
                    wait_read(pe, plan["v", m, T - 1])
                use = plan["O", u]
                bank = wait_free(pe, use)
                for c in range(T):
                    n = LOC if c < T - 1 else P
                    for h in range(2):
                        rows = slice(h * FDH, (h + 1) * FDH)
                        cols = slice((2 * j + h) * FDH, (2 * j + h + 1) * FDH)
                        ins = mm(bank[rows, c * P:c * P + n], lv[:, m % 2, c, cols],
                                 lpT[:, h, c * LOC:c * LOC + n], start=c == 0, stop=c == T - 1, skip_group_check=True)
                ins.then_inc(full[use[0]], 1)

            def output_part(m, tp):
                wait_read(pe, plan["O", m * FPAIRS + FPAIRS - 1])
                if m % B == 0:
                    pe.wait_ge(ld_lwo, 16 * (m // B + 1))
                use = plan["wo", m, tp]
                bank = wait_free(pe, use)
                for i in range(2):
                    t = 2 * tp + i
                    ins = product(bank[:, i * D:(i + 1) * D],
                                  [(loT[:, k, t * P:(t + 1) * P], wo[:, k, :]) for k in range(FPAIRS)])
                ins.then_inc(full[use[0]], 1)

            def transposed_norm(m):
                pe.wait_ge(f_hn, m + 1)
                for e in range(E2):
                    use = plan["hnT", m, e]
                    bank = wait_free(pe, use)
                    for t in range(T):
                        ins = pe.transpose(bank[:, t * P:(t + 1) * P], hn[:, t, e * P:(e + 1) * P], ident[:, :])
                    ins.then_inc(full[use[0]], 1)

            def hidden_part(m, f):
                if f == 0:
                    for e in range(E2):
                        wait_read(pe, plan["hnT", m, e])
                    if m % B == 0:
                        pe.wait_ge(ld_w1, 16 * (m // B + 1))
                rows = frows(f)
                for what, lo in (("w1g", HID + f * FT), ("w1a", f * FT)):
                    use = plan[what, m, f]
                    bank = wait_free(pe, use)
                    product(bank[0:rows, :], [(w1[:, e, lo:lo + rows], hnT[:, e, :]) for e in range(E2)])\
                        .then_inc(full[use[0]], 1)

            def second_part(m, tp):
                for f in range(NF - 3, NF):
                    wait_read(pe, plan["w1a", m, f])
                if m % B == 0:
                    pe.wait_ge(ld_w2, 32 * (m // B + 1))
                use = plan["w2", m, tp]
                bank = wait_free(pe, use)
                for i in range(2):
                    t = 2 * tp + i
                    ins = product(bank[:, i * D:(i + 1) * D],
                                  [(hid[0:frows(f), f, t * P:(t + 1) * P], w2[0:frows(f), f, :]) for f in range(NF)])
                ins.then_inc(full[use[0]], 1)

            pe.wait_ge(ln_done, 3 * B)
            for what, *at in order:
                if what == "hT":
                    transposed_y(*at)
                if what == "qkv":
                    qkv_tile(*at)
                if what == "Tqk":
                    transposed_qk(*at)
                if what == "S":
                    local_scores(*at)
                if what == "T":
                    local_transposes(*at)
                if what == "AV":
                    local_values(*at)
                if what == "wo":
                    output_part(*at)
                if what == "hnT":
                    transposed_norm(*at)
                if what == "w1":
                    hidden_part(*at)
                if what == "w2":
                    second_part(*at)


def kernel(x, ctx_1024, mask_BxS2_bk1, L0_attn_W_Q, L0_attn_W_K, L0_attn_W_V, L0_attn_W_O, L0_xattn_Wq, L0_xattn_bq,
           L0_xattn_Wk, L0_xattn_bk, L0_xattn_Wv, L0_xattn_bv, L0_xattn_Wo, L0_xattn_bo, L0_ffn_wqkv, L0_ffn_q_scale,
           L0_ffn_k_scale, L0_ffn_wo, L0_ffn_ln_g, L0_ffn_ln_b, L0_ffn_w1, L0_ffn_b1, L0_ffn_w2, L0_ffn_b2):
    import concourse.bacc as bacc
    from concourse.bass_utils import run_bass_kernel_spmd

    def by_pairs(w):
        return np.asarray(w).reshape(PAIRS, P, E2, P).transpose(0, 3, 2, 1)

    def by_rows(w):
        return np.asarray(w).reshape(*np.shape(w)[:-1], E2, P).swapaxes(-1, -2)

    def hidden_rows(w):
        parts = np.asarray(w).reshape(DEPTH, 2, HID)
        filled = np.concatenate([parts, np.zeros((DEPTH, 2, FT * NF - HID), parts.dtype)], 2)
        return filled.reshape(DEPTH, 2, NF, FT).transpose(0, 3, 1, 2)

    arrays = {
        "x": x,
        "ctxT": np.asarray(ctx_1024).transpose(0, 2, 1),
        "mask": np.asarray(mask_BxS2_bk1).reshape(B, T, P).transpose(2, 0, 1),
        "w_pairs": np.stack([by_pairs(L0_attn_W_Q), by_pairs(L0_attn_W_K), by_pairs(L0_attn_W_V)], 2),
        "attn_wo": np.asarray(L0_attn_W_O).transpose(0, 2, 1).reshape(AH * ADH, D),
        "xwq": np.asarray(L0_xattn_Wq).T, "xbq": by_rows(L0_xattn_bq),
        "xwkv": np.concatenate([np.asarray(L0_xattn_Wk).T, np.asarray(L0_xattn_Wv).T], 1),
        "xbkv": np.concatenate([np.asarray(L0_xattn_bk), np.asarray(L0_xattn_bv)]),
        "xwo": np.asarray(L0_xattn_Wo).T, "xbo": L0_xattn_bo,
        "wqkv": L0_ffn_wqkv, "q_scale": L0_ffn_q_scale, "k_scale": L0_ffn_k_scale, "wo": L0_ffn_wo,
        "ln_g": by_rows(L0_ffn_ln_g), "ln_b": by_rows(L0_ffn_ln_b), "w1": L0_ffn_w1, "b1": hidden_rows(L0_ffn_b1), "w2": L0_ffn_w2, "b2": L0_ffn_b2,
    }
    arrays.update(constants())
    nc = bacc.Bacc("TRN2", target_bir_lowering=False, num_devices=1)
    aps, feeds = {}, {}
    for name, value in arrays.items():
        value = np.ascontiguousarray(value)
        feeds[f"in_{name}"] = value
        aps[name] = nc.dram_tensor(f"in_{name}", value.shape, mybir.dt.from_np(value.dtype), kind="ExternalInput").ap()
    out = nc.dram_tensor("out", (B, S, D), F32, kind="ExternalOutput").ap()
    x2_dram = nc.dram_tensor("x2_scratch", (B, S, D), F32).ap()
    build(nc, aps, out, x2_dram)
    result = run_bass_kernel_spmd(nc, [feeds], core_ids=[0])
    return result.results[0]["out"]
```

```python
from contextlib import ExitStack

import numpy as np

import concourse.bass as bass
from concourse import mybir

F32 = mybir.dt.float32
F32R = mybir.dt.float32r
U8 = mybir.dt.uint8
ALU = mybir.AluOpType
ACT = mybir.ActivationFunctionType
AX = mybir.AxisListType

P = 128
B, S, D = 4, 512, 256
T = S // P
E2 = D // P
AH, ADH = 16, 64
PAIRS = AH // 2
QUADS = PAIRS // 2
QUNITS = 2 * B
XH, XDH = 16, 16
DEPTH, FH, FDH = 2, 8, 64
INNER = FH * FDH
FPAIRS = FH // 2
HID = int(D * 4 * 2 / 3)
NF = 6
FT = -(-HID // NF)
FL = HID - FT * (NF - 1)
W = 128
QK_SCALE = 8.0
NEG = -1e30
LN_EPS = 1e-5
NORM_EPS = 1e-12
TRI = [P * (i + 1) for i in range(T)]
S_TILES = ((3,), (2,), (1, 0))
TRI_AT = [sum(TRI[:i]) for i in range(T + 1)]
KEYB = [S - P * j for j in range(T)]
KEYB_AT = [0, 512, 1024, 896]
T_TILES = ((0,), (1, 3), (2,))
LOC = 2 * P
LOC_N = P + LOC * (T - 1)
GELU_T = 2


def loc_at(w):
    return 0 if w == 0 else P + LOC * (w - 1)


def constants():
    ident = np.eye(P, dtype=np.float32)
    i = np.arange(P)[:, None]
    j = np.arange(P)[None, :]
    causal = np.zeros((P, S), np.float32)
    causal[:, S - P:] = np.where(j <= i, 0.0, NEG)
    local = np.concatenate([np.where(i <= j, 0.0, NEG), np.where(j <= i, 0.0, NEG)], 1).astype(np.float32)
    heads = (i // XDH == j // XDH).astype(np.float32)
    half = np.arange(0, FDH, 2, dtype=np.float32)
    inv_freq = (1.0 / np.float32(10000.0) ** (half / np.float32(FDH))).astype(np.float32)
    t = np.arange(S, dtype=np.float32)
    freqs = t[:, None] * inv_freq[None, :]
    freqs = np.concatenate([freqs, freqs], -1)
    base = ((half + np.float32(0.4 * FDH)) / np.float32(1.4 * FDH)).astype(np.float32)
    power = ((t - S // 2) / np.float32(W // 2)).astype(np.float32)
    scale = (base[None, :] ** power[:, None]).astype(np.float32)
    scale = np.concatenate([scale, scale], -1)
    cos, sin = np.cos(freqs), np.sin(freqs)
    sign = np.where(np.arange(FDH) < FDH // 2, -1.0, 1.0).astype(np.float32)
    rot = np.stack([cos * scale, sin * sign * scale, cos / scale, sin * sign / scale])
    rot = rot.reshape(4, T, P, FDH).transpose(2, 0, 1, 3).astype(np.float32)
    return {"c_ident": ident, "c_causal": causal, "c_local": local, "c_heads": heads,
            "c_rot": np.ascontiguousarray(rot)}


def build(nc, a, out, x2_dram):
    with ExitStack() as ctx:
        def sem(name):
            return ctx.enter_context(nc.semaphore(name))

        def sbt(stack, name, shape, dt=F32):
            return stack.enter_context(nc.sbuf_tensor(name, shape, dt))

        psum = [ctx.enter_context(nc.psum_tensor(f"psum{i}", [P, 512], F32)) for i in range(8)]
        full = [sem(f"full{i}") for i in range(8)]
        read = [sem(f"read{i}") for i in range(8)]

        ident = sbt(ctx, "ident", [P, P])
        neg_half = sbt(ctx, "neg_half", [P, 16])
        y = sbt(ctx, "y", [P, B, T, D])
        raw = ExitStack()
        aw_hi = sbt(raw, "aw_hi", [P, 3, E2, 2 * P], F32R)
        aw_lo = sbt(raw, "aw_lo", [P, 3, E2, 2 * P], F32R)
        raw.close()
        raw = ExitStack()
        wqkv_raw = sbt(raw, "wqkv_raw", [P, E2, 3 * INNER])
        raw.close()
        wqkv_lo = sbt(ctx, "wqkv_lo", [P, E2, 3 * INNER], F32R)
        stats = sbt(ctx, "stats", [P, 2, T, 12])
        mv = sbt(ctx, "mv", [P, 2, T, 2])
        rstd = sbt(ctx, "rstd", [P, 2, T])

        ab = ExitStack()
        raw = ExitStack()
        xnT_lo = sbt(raw, "xnT_lo", [P, B, E2, S], F32R)
        raw.close()
        x = sbt(ab, "x", [P, B, T, D])
        raw = ExitStack()
        xnT_hi = sbt(raw, "xnT_hi", [P, B, E2, S], F32R)
        raw.close()
        xnT = sbt(ab, "xnT", [P, E2, B, S])
        xwq = sbt(ab, "xwq", [P, E2, D])
        xwo = sbt(ab, "xwo", [P, E2, D])
        xbo = sbt(ab, "xbo", [P, D])
        xbq = sbt(ab, "xbq", [P, E2])
        xmask = sbt(ab, "xmask", [P, B, T], U8)
        xkeep = sbt(ab, "xkeep", [P, B, T])
        heads = sbt(ab, "heads", [P, P])
        kvm = sbt(ab, "kvm", [P, B, E2, P])
        r2 = ExitStack()
        kvs = sbt(r2, "kvs", [P, 2, E2, P])
        qm = sbt(r2, "qm", [P, E2, S])
        qr = sbt(r2, "qr", [P, E2, S])
        qT = sbt(r2, "qT", [P, 2, E2, S])
        qss = sbt(r2, "qss", [P, 2, E2])
        oxT = sbt(r2, "oxT", [P, 2, E2, S])
        r2.close()
        r2 = ExitStack()
        xn1 = sbt(r2, "xn1", [P, 2, T, D])
        r2.close()
        zT = sbt(ab, "zT", [P, B, PAIRS, S])
        woT = sbt(ab, "woT", [P, PAIRS, D])
        causal = sbt(ab, "causal", [P, S])
        xwkv = sbt(ab, "xwkv", [P, E2, 2 * D])
        xbkv = sbt(ab, "xbkv", [P, 2 * D])
        r1 = ExitStack()
        rowmax = sbt(r1, "rowmax", [P, 2, 2, T])
        negmax = sbt(r1, "negmax", [P, 2, 2, T])
        den = sbt(r1, "den", [P, 2, 2, T])
        rden = sbt(r1, "rden", [P, 2, 2, T])
        q2 = sbt(r1, "q2", [P, 2, S], F32R)
        aw = sbt(r1, "aw", [P, 3, E2, 2 * P])
        k_round = sbt(r1, "k_round", [P, S], F32R)
        k_rest = sbt(r1, "k_rest", [P, S], F32R)
        k2 = sbt(r1, "k2", [P, 2, S], F32R)
        v = sbt(r1, "v", [P, 2, T, 2 * P])
        pT = sbt(r1, "pT", [P, 2, TRI_AT[T]])
        probs = sbt(r1, "probs", [P, 2, 2, TRI_AT[T]])
        r1.close()
        r1 = ExitStack()
        ctxT = sbt(r1, "ctxT", [P, 2, E2, S])
        kv = sbt(r1, "kv", [P, 2, T, 2 * D])
        xn = sbt(r1, "xn", [P, 2, T, D])
        kf = sbt(r1, "kf", [P, 2, T, D])
        ktmp = sbt(r1, "ktmp", [P, T, D])
        knorm = sbt(r1, "knorm", [P, 2, T, XH])
        r1.close()
        ab.close()

        raw = ExitStack()
        w1_raw = sbt(raw, "w1_raw", [P, E2, 2 * HID])
        raw.close()
        w1_lo = sbt(ctx, "w1_lo", [P, E2, 2 * HID], F32R)
        w1_hi = sbt(ctx, "w1_hi", [P, E2, 2 * HID], F32R)
        w2 = sbt(ctx, "w2", [FT, NF, D])
        wo = sbt(ctx, "wo", [P, FPAIRS, D])
        lng = sbt(ctx, "lng", [P, DEPTH, E2])
        lnb = sbt(ctx, "lnb", [P, DEPTH, E2])
        b1 = sbt(ctx, "b1", [FT, DEPTH, 2, NF])
        b2 = sbt(ctx, "b2", [P, D])
        hs = sbt(ctx, "hs", [P, T, P])
        hn = sbt(ctx, "hn", [P, T, D])
        hnT_hi = sbt(ctx, "hnT_hi", [P, E2, S], F32R)
        hnT_lo = sbt(ctx, "hnT_lo", [P, E2, S], F32R)
        raw = ExitStack()
        hnT = sbt(raw, "hnT", [P, E2, S])
        raw.close()
        gl = sbt(ctx, "gl", [P, GELU_T, S])
        raw = ExitStack()
        wqkv_next = sbt(raw, "wqkv_next", [P, E2, 3 * INNER])
        raw.close()
        hid = sbt(ctx, "hid", [FT, NF, S])
        loT = sbt(ctx, "loT", [P, FPAIRS, S])
        local = sbt(ctx, "local", [P, LOC])
        lp = sbt(ctx, "lp", [P, 2, 2, LOC_N])
        lpT = sbt(ctx, "lpT", [P, 2, LOC_N])
        lmax = sbt(ctx, "lmax", [P, 2, 2, T])
        lneg = sbt(ctx, "lneg", [P, 2, 2, T])
        lden = sbt(ctx, "lden", [P, 2, 2, T])
        lrden = sbt(ctx, "lrden", [P, 2, 2, T])
        raw = ExitStack()
        x2 = sbt(raw, "x2", [P, B, T, D])
        raw.close()
        wqkv_hi = sbt(ctx, "wqkv_hi", [P, E2, 3 * INNER], F32R)
        sq = sbt(ctx, "sq", [P, 2, INNER])
        tab = [sbt(ctx, f"tab{l}", [P, 4, T, FDH]) for l in range(DEPTH)]
        rot = tab[DEPTH - 1]
        qk_scale = sbt(ctx, "qk_scale", [P, DEPTH, 2, FDH])
        hT_hi = sbt(ctx, "hT_hi", [P, E2, S + 1], F32R)
        hT_lo = sbt(ctx, "hT_lo", [P, E2, S + 1], F32R)
        ra = sbt(ctx, "ra", [P, 2, 2, INNER])
        rb = sbt(ctx, "rb", [P, 2, INNER])
        ss = sbt(ctx, "ss", [P, 2, FH])
        rn = sbt(ctx, "rn", [P, 2, T, 2, FH])
        lqz = sbt(ctx, "lqz", [P, FPAIRS, T, 2, P])
        lkT = sbt(ctx, "lkT", [P, FPAIRS, T, P])
        lv = sbt(ctx, "lv", [P, 2, T, INNER])

        ld_causal = sem("ld_causal")
        ld_local, ld_const, ld_xw, ld_wo = sem("ld_local"), sem("ld_const"), sem("ld_xw"), sem("ld_wo")
        ld_ctx = [sem(f"ld_ctx{b}") for b in range(B)]
        ld_x = [sem(f"ld_x{b}") for b in range(B)]
        ld_aw = sem("ld_aw")
        x_hi, a_hi, a_lo = sem("x_hi"), sem("a_hi"), sem("a_lo")
        set0 = sem("set0")
        ln_stats, ln_mv = sem("ln_stats"), sem("ln_mv")
        ln_eps, ln_rstd = sem("ln_eps"), sem("ln_rstd")
        ln_done = sem("ln_done")
        q_hi, k_hi, k_both = sem("q_hi"), sem("k_hi"), sem("k_both")
        s_neg, s_rden = sem("s_neg"), sem("s_rden")
        s_exp, s_prob = sem("s_exp"), sem("s_prob")
        k_keep, k_min, k_fin, k_ss, k_rec, k_done = (
            sem(n) for n in ("k_keep", "k_min", "k_fin", "k_ss", "k_rec", "k_done"))
        k_exp, k_sq, k_sqrt = sem("k_exp"), sem("k_sq"), sem("k_sqrt")
        q_relu, q_exp, q_sq = sem("q_relu"), sem("q_exp"), sem("q_sq")
        q_fin, q_max, kvs_done = sem("q_fin"), sem("q_max"), sem("kvs_done")
        q_rn, bo_done = sem("q_rn"), sem("bo_done")
        x2_st = sem("x2_st")
        ld_rot, ld_small, ld_wqkv, ld_lwo, ld_w1, ld_w2 = (
            sem(n) for n in ("ld_rot", "ld_small", "ld_wqkv", "ld_lwo", "ld_w1", "ld_w2"))
        x2_b2 = sem("x2_b2")
        set1 = sem("set1")
        set2 = sem("set2")
        w_hi, w_lo = sem("w_hi"), sem("w_lo")
        w1_hi_ok, w1_lo_ok = sem("w1_hi_ok"), sem("w1_lo_ok")
        hn_hi, hn_lo = sem("hn_hi"), sem("hn_lo")
        h_hi = sem("h_hi")
        l_tab, l_ss, l_ssm, l_neg, l_rden = (
            sem(n) for n in ("l_tab", "l_ss", "l_ssm", "l_neg", "l_rden"))
        l_sq, l_exp = sem("l_sq"), sem("l_exp")
        l_q, l_rn, l_kadd, l_k, l_prob = (sem(n) for n in ("l_q", "l_rn", "l_kadd", "l_k", "l_prob"))
        hs_ld = sem("hs_ld")
        f_stats, f_mv, f_hn = (sem(n) for n in ("f_stats", "f_mv", "f_hn"))
        f_eps, f_rstd, f_b2 = (sem(n) for n in ("f_eps", "f_rstd", "f_b2"))
        x2_ld = [sem(f"x2_ld{b}") for b in range(B)]
        fin_done, out_st = sem("fin_done"), sem("out_st")
        passed_v, passed_p = sem("passed_v"), sem("passed_p")

        NU = PAIRS * B
        K_DMAS = 16 * 2 * 2

        def use_s(u, h, k):
            return k, 2 * u + h

        def use_x(b, e):
            return (3, b) if e == 0 else (4 + b % 2, b // 2)

        def use_t(u, h, k):
            n = 3 * h + k
            return 3 + n % 3, (3 if n % 3 == 2 else 2) * u + n // 3 + (B // 2 if n % 3 else B)

        def use_z(u):
            return 5, 3 * u + 2 + B // 2

        def use_q(u):
            return 6, u

        def use_v(u):
            return 7, 2 * u + 1

        def use_k(u):
            return 7, 2 * u

        count = [2 * NU] * 3 + [B + 2 * NU, B // 2 + 2 * NU, B // 2 + 3 * NU, NU, 2 * NU]
        plan = {}

        def take(key, bank):
            plan[key] = (bank, count[bank])
            count[bank] += 1

        STEPS = DEPTH * B
        SET1 = 3
        UNITS = STEPS * FPAIRS

        WO_PART = ("wo_0", "wo_1", "stats")
        SLOTS = ("wo_0 v q soft_now k wo_1 S T0 T1 stats norm exp AV Tqk apply bias",
                 "v soft_now S hnT q k T0 hid_0 hid_1 T1 hid_2 exp Tqk AV",
                 "soft_now v q hid_3 k T0 hid_4 T1 hid_5 AV S exp",
                 "Tqk_before soft_now v q k T0 w2_0 T1 hT w2_1 Tqk AV S exp")

        def slot(m, j):
            u = m * FPAIRS + j
            names = SLOTS[j].split()
            if m == B - 1 and j == 0:
                names = ["weights", *WO_PART] + [n for n in names if n not in WO_PART]
            if j == 0 and m % B == 1 and m > B:
                names = ["w1_parts"] + names
            items = []
            for name in names:
                if name in ("v", "q", "k"):
                    items.append(("qkv", m + 1, j, name))
                if name in ("Tqk", "Tqk_before"):
                    items.append(("Tqk", m + 1, j - (name == "Tqk_before")))
                if name == "hT" and m + 2 < STEPS:
                    items.append(("hT", m + 2))
                if name in ("S", "exp", "soft"):
                    items.append((name, u + 1))
                if name == "soft_now":
                    items.append(("soft", u))
                if name in ("T0", "T1"):
                    items.append(("T", u, int(name[1])))
                if name == "AV":
                    items.append(("AV", u))
                if name in ("stats", "norm", "apply", "hnT", "bias"):
                    items.append((name, m - 1))
                if name.split("_")[0] in ("wo", "hid", "w2"):
                    what, i = name.split("_")
                    items.append(({"hid": "w1"}.get(what, what), m - 1, int(i)))
                if name == "weights":
                    items.append((name, 1))
                if name == "w1_parts":
                    items.append((name, m // B))
            return items

        cross = [("awo", 0), ("norm2", 0), ("kv", 0), ("keys", 0), ("awo", 1), ("x1T", 0), ("norm2", 1), ("kv", 1),
                 ("KV", 0), ("keys", 1), ("x1T", 1), ("kv", 2), ("xq", 0), ("keys", 2), ("qadd", 0), ("kvs", 0),
                 ("awo", 2), ("norm2", 2), ("KV", 1), ("xq", 1), ("KV", 2), ("xo", 0), ("qadd", 1), ("kvs", 1),
                 ("kv", 3), ("xo", 1), ("xw", 0), ("y", 0), ("keys", 3), ("awo", 3), ("norm2", 3), ("xw", 1),
                 ("KV", 3), ("x1T", 2), ("x1T", 3), ("weights", 0), ("hT", 0), ("xq", 2), ("qadd", 2), ("kvs", 2),
                 ("xq", 3), ("tab", 0), ("y", 1), ("xo", 2), ("qadd", 3), ("qkv", 0, 0, "v"), ("kvs", 3),
                 ("qkv", 0, 0, "q"), ("qkv", 0, 0, "k"), ("qkv", 0, 1, "q"), ("qkv", 0, 1, "v"), ("xw", 2), ("xo", 3),
                 ("qkv", 0, 1, "k"), ("Tqk", 0, 0), ("xw", 3), ("y", 2), ("y", 3), ("qkv", 0, 2, "v"),
                 ("qkv", 0, 2, "q"), ("qkv", 0, 2, "k"), ("Tqk", 0, 1), ("qkv", 0, 3, "q"), ("qkv", 0, 3, "k"),
                 ("Tqk", 0, 2), ("qkv", 0, 3, "v"), ("hT", 1), ("Tqk", 0, 3), ("S", 0), ("exp", 0), ("soft", 0),
                 ("qkv", 1, 0, "q"), ("qkv", 1, 0, "v"), ("qkv", 1, 0, "k"), ("T", 0, 0), ("qkv", 1, 1, "v"),
                 ("S", 1), ("T", 0, 1), ("exp", 1), ("S", 2), ("soft", 1), ("qkv", 1, 1, "q"), ("tab", 1),
                 ("qkv", 1, 2, "v"), ("AV", 0), ("Tqk", 1, 0), ("T", 1, 0), ("qkv", 1, 1, "k"), ("T", 1, 1),
                 ("exp", 2), ("soft", 2), ("qkv", 1, 2, "q"), ("AV", 1), ("w1_parts", 0), ("qkv", 1, 3, "v"),
                 ("T", 2, 0), ("qkv", 1, 2, "k"), ("Tqk", 1, 1), ("qkv", 1, 3, "q"), ("T", 2, 1), ("S", 3),
                 ("exp", 3), ("soft", 3), ("Tqk", 1, 2), ("qkv", 1, 3, "k"), ("AV", 2), ("T", 3, 0), ("T", 3, 1),
                 ("hT", 2), ("AV", 3), ("Tqk", 1, 3), ("S", 4), ("exp", 4)]
        norm_no = {key: B + i for i, key in enumerate(k for k in cross if k[0] in ("norm2", "y"))}
        assert [k[1:] for k in cross if k[0] in ("awo", "xw")] == [k[1:] for k in norm_no]
        closing = [("soft", 28), ("sum", 0), ("wo", 6, 0), ("S", 29), ("wo", 6, 1), ("exp", 29), ("T", 28, 0),
                 ("T", 28, 1), ("stats", 6), ("norm", 6), ("apply", 6), ("soft", 29), ("AV", 28), ("S", 30),
                 ("hnT", 6), ("T", 29, 0), ("sum", 1), ("T", 29, 1), ("w1", 6, 0), ("w1", 6, 1), ("w1", 6, 2),
                 ("exp", 30), ("soft", 30), ("AV", 29), ("w1", 6, 3), ("T", 30, 0), ("bias", 6), ("w1", 6, 4),
                 ("T", 30, 1), ("AV", 30), ("w1", 6, 5), ("S", 31), ("exp", 31), ("wo_early", 7, 0), ("soft", 31),
                 ("T", 31, 0), ("wo_early", 7, 1), ("T", 31, 1), ("AV", 31), ("wo", 7, 0), ("wo", 7, 1), ("stats", 7),
                 ("norm", 7), ("w2", 6, 0), ("apply", 7), ("w2", 6, 1), ("hnT", 7), ("w1", 7, 0), ("w1", 7, 1),
                 ("w1", 7, 2), ("w1", 7, 3), ("w1", 7, 4), ("bias", 7), ("w1", 7, 5), ("w2", 7, 0), ("w2", 7, 1)]
        order = list(cross)
        for m in range(1, STEPS - 1):
            for j in range(FPAIRS):
                order += slot(m, j)
        order += closing

        banks = {"g": (2, 5, 6, 7), "t": (3, 4), "a": (0, 1), "c": (5, 6, 7), "x": (2, 5, 0, 1)}
        turns = {which: 0 for which in banks}

        def turn(key, which):
            take(key, banks[which][turns[which] % len(banks[which])])
            turns[which] += 1

        for what, *at in order:
            if what == "awo":
                for tp in range(2):
                    turn(("awo", at[0], tp), "a")
            if what == "kv":
                for t in range(T):
                    turn(("kv", at[0], t), "c")
            if what == "KV":
                turn((what, *at), "x")
            if what in ("xq", "xo", "xw"):
                for e in range(2):
                    turn((what, at[0], e), "x")
            if what in ("x1T", "hT", "hnT"):
                for e in range(E2):
                    turn((what, at[0], e), "t")
            if what == "qkv":
                turn((at[2], at[0], at[1]), "g")
            if what == "wo" and at[0] < STEPS - 1 or what in ("wo_early", "w2"):
                turn((what.split("_")[0], *at), "g")
            if what == "w1":
                turn(("w1g", *at), "g")
                turn(("w1a", *at), "g")
            if what == "Tqk":
                turn(("Tq", *at), "t")
                turn(("Tk", *at), "t")
            if what == "T":
                turn(("T", *at, 0), "t")
                turn(("T", *at, 1), "t")
            if what == "AV":
                turn(("O", at[0]), "g")
            if what == "S":
                for h in range(2):
                    take(("S", at[0], h, 0), 0)
                    take(("S", at[0], h, 1), 1)

        def wait_free(pe, use):
            bank, n = use
            if not (isinstance(n, int) and n == 0):
                pe.wait_ge(read[bank], n)
            return psum[bank]

        def wait_full(eng, use):
            bank, n = use
            eng.wait_ge(full[bank], n + 1)
            return psum[bank]

        def wait_read(eng, use):
            bank, n = use
            eng.wait_ge(read[bank], n + 1)

        def pass_wait(eng, passed):
            eng.sem_inc(passed, 1)

        def wait_early(eng):
            wait_full(eng, plan["KV", B - 1])
            wait_full(eng, plan["x1T", B - 1, 1])

        def frows(f):
            return FT if f < NF - 1 else FL

        def q_at(m, j, t):
            return (j, t) if m % 2 == 0 else (t, j)

        block = ctx.enter_context(nc.Block())

        @block.sync
        def _(sp):
            def quad_weights(c):
                sp.dma_start(aw[:, :, :, :], a["w_quads"][c]).then_inc(ld_aw, 16)

            def load_x(b):
                sp.dma_start(x[:, b, :, :], a["x"][b].rearrange("(t p) e -> p t e", p=P)).then_inc(ld_x[b], 16)

            load_x(0)
            sp.dma_start(ident[:, :], a["c_ident"]).then_inc(ld_const, 16)
            quad_weights(0)
            load_x(1)
            sp.dma_start(causal[:, :], a["c_causal"]).then_inc(ld_causal, 16)
            load_x(2)
            load_x(3)
            sp.dma_start(woT[:, :, :], a["attn_wo"].rearrange("(k p) e -> p k e", p=P)).then_inc(ld_wo, 16)
            for t, src in ((xwq, "xwq"), (xwkv, "xwkv"), (xwo, "xwo")):
                sp.dma_start(t[:, :, :], a[src].rearrange("(k p) e -> p k e", p=P)).then_inc(ld_xw, 16)
            sp.dma_start(xbkv[:, :], a["xbkv"].partition_broadcast(P)).then_inc(ld_xw, 16)
            sp.dma_start(xbo[:, :], a["xbo"].partition_broadcast(P)).then_inc(ld_xw, 16)
            sp.dma_start(xbq[:, :], a["xbq"]).then_inc(ld_xw, 16)
            sp.dma_start(xmask[:, :, :], a["mask"]).then_inc(ld_xw, 16)
            sp.dma_start(heads[:, :], a["c_heads"]).then_inc(ld_xw, 16)

            def layer_w1(l):
                sp.dma_start(w1_raw[:, :, :], a["w1"][l].rearrange("(k p) c -> p k c", p=P)).then_inc(ld_w1, 16)

            def layer_wo(l):
                sp.dma_start(wo[:, :, :], a["wo"][l].rearrange("(k p) c -> p k c", p=P)).then_inc(ld_lwo, 16)

            def layer_w2(l):
                main = a["w2"][l, 0:FT * (NF - 1), :].rearrange("(k p) c -> p k c", p=FT)
                sp.dma_start(w2[:, 0:NF - 1, :], main).then_inc(ld_w2, 16)
                sp.dma_start(w2[0:FL, NF - 1, :], a["w2"][l, FT * (NF - 1):HID, :]).then_inc(ld_w2, 16)

            sp.wait_ge(a_lo, 3)
            quad_weights(1)

            def other_half(u):
                sp.wait_ge(k_hi, u + 1)
                for h in range(2):
                    for half in range(2):
                        sp.dma_start(k2[half * ADH:(half + 1) * ADH, h].bitcast(F32),
                                     k_round[h * ADH:(h + 1) * ADH].bitcast(F32)).then_inc(k_both, 16)

            with sp.Fori(0, QUADS - 2) as c:
                for j in range(QUNITS):
                    other_half(c * QUNITS + j)
                sp.wait_ge(a_lo, 3 * c + 6)
                quad_weights(c + 2)
            for u in range(NU - 2 * QUNITS, NU):
                other_half(u)
            wait_full(sp, use_v(NU - 1))
            for b in range(B):
                load_x(b)
            sp.dma_start(wqkv_raw[:, :, :], a["wqkv"][0].rearrange("(k p) c -> p k c", p=P)).then_inc(ld_wqkv, 16)
            wait_full(sp, use_z(NU - 1))
            for b in range(B):
                if b >= 2:
                    wait_full(sp, plan["kv", b - 2, T - 1])
                sp.dma_start(ctxT[:, b % 2], a["ctxT"][b].rearrange("(k p) s -> p k s", p=P)).then_inc(ld_ctx[b], 16)
            wait_early(sp)
            sp.dma_start(local[:, :], a["c_local"]).then_inc(ld_local, 16)
            sp.dma_start(rot[:, :, :, :], a["c_rot"]).then_inc(ld_rot, 16)
            sp.dma_start(qk_scale[:, :, 0, :], a["q_scale"].partition_broadcast(P)).then_inc(ld_rot, 16)
            sp.dma_start(qk_scale[:, :, 1, :], a["k_scale"].partition_broadcast(P)).then_inc(ld_rot, 16)
            for b in range(B):
                wait_read(sp, plan["xw", b, 0])
                wait_read(sp, plan["xw", b, 1])
                sp.dma_start(x2_dram[b].rearrange("(t p) e -> p t e", p=P), x[:, b, :, :]).then_inc(x2_st, 16)
            sp.wait_ge(ln_done, 3 * B)
            sp.wait_ge(x2_st, 16 * B)
            layer_wo(0)
            layer_w1(0)
            layer_w2(0)
            for l in range(DEPTH):
                sp.dma_start(lng[:, l, :], a["ln_g"][l]).then_inc(ld_small, 16)
                sp.dma_start(lnb[:, l, :], a["ln_b"][l]).then_inc(ld_small, 16)
                sp.dma_start(b1[:, l, :, :], a["b1"][l]).then_inc(ld_small, 16)
            sp.dma_start(b2[:, :], a["b2"][0].partition_broadcast(P)).then_inc(ld_small, 16)
            sp.wait_ge(set2, 1)
            for m in range(STEPS):
                l, b = divmod(m, B)
                for tp in range(2):
                    wait_read(sp, plan["wo", m, tp])
                if m:
                    sp.wait_ge(f_hn, m)
                sp.dma_start(hs[1:P, :, :], y[0:P - 1, b, :, P:D]).then_inc(hs_ld, 16)
                sp.dma_start(hs[0:1, 1:T, :], y[P - 1:P, b, 0:T - 1, P:D]).then_inc(hs_ld, 16)
                if b == B - 3 and l + 1 < DEPTH:
                    for tp in range(2):
                        wait_full(sp, plan["w2", m, tp])
                    src = a["wqkv"][l + 1].rearrange("(k p) c -> p k c", p=P)
                    sp.dma_start(wqkv_next[:, :, :], src).then_inc(ld_wqkv, 16)
                if b == B - 1 and l + 1 < DEPTH:
                    layer_wo(l + 1)
                    wait_full(sp, plan["w1a", m, NF - 1])
                    layer_w1(l + 1)
                    for tp in range(2):
                        wait_full(sp, plan["w2", m, tp])
                    layer_w2(l + 1)
                    sp.wait_ge(f_b2, B * (l + 1))
                    sp.dma_start(b2[:, :], a["b2"][l + 1].partition_broadcast(P)).then_inc(ld_small, 16)
                if m == STEPS - 3:
                    wait_full(sp, plan["k", STEPS - 1, T - 1])
                    sp.wait_ge(l_ssm, 2 * T * STEPS)
                    for i in range(B):
                        sp.dma_start(x2[:, i, :, :], x2_dram[i].rearrange("(t p) e -> p t e", p=P))\
                            .then_inc(x2_ld[i], 16)
            for b in range(B):
                dst = out[b].rearrange("(t p) e -> p t e", p=P)
                if b < B - 2:
                    sp.wait_ge(fin_done, b + 1)
                    sp.dma_start(dst, y[:, b, :, :]).then_inc(out_st, 16)
                else:
                    for tp in range(2):
                        wait_read(sp, plan["w2", STEPS - B + b, tp])
                        rows = slice(2 * tp, 2 * tp + 2)
                        sp.dma_start(dst[:, rows], y[:, b, rows, :]).then_inc(out_st, 16)
            sp.wait_ge(out_st, 16 * (B + 2))

        @block.gpsimd
        def _(pool):
            pool.memset(neg_half[:, :], -0.5).then_inc(set0, 1)
            pool.wait_ge(set0, 1)

            def norm_rstd(n):
                pool.wait_ge(ln_mv, T * (n + 1))
                pool.tensor_scalar(rstd[:, n % 2, :], mv[:, n % 2, :, 1], LN_EPS, None, ALU.add).then_inc(ln_eps, 1)
                pool.wait_ge(ln_eps, n + 1)
                pool.tensor_tensor(rstd[:, n % 2, :], rstd[:, n % 2, :], neg_half[:, 0:T], ALU.pow)\
                    .then_inc(ln_rstd, 1)

            for b in range(B):
                norm_rstd(b)

            def probabilities(u, j):
                for h in range(2):
                    pool.wait_ge(s_rden, 2 * u + (h + 1))
                    for i in range(T):
                        pr = probs[:, j % 2, h, TRI_AT[i]:TRI_AT[i + 1]]
                        ins = pool.tensor_tensor(pr, pr, rden[:, j % 2, h, i:i + 1].broadcast_to([P, TRI[i]]),
                                                 ALU.mult)
                    ins.then_inc(s_prob, 1)

            with pool.Fori(0, QUADS) as c:
                for j in range(QUNITS):
                    probabilities(c * QUNITS + j, j)

            def add_output_bias(b):
                if b == 0:
                    pool.wait_ge(ld_xw, 16 * 8)
                pool.wait_ge(ln_done, norm_no["norm2", b] + 1)
                for t in range(T):
                    ins = pool.tensor_tensor(x[:, b, t, :], x[:, b, t, :], xbo[:, :], ALU.add)
                ins.then_inc(bo_done, 1)

            def query_norms(s):
                pool.wait_ge(q_max, s + 1)
                pool.tensor_tensor(qss[:, s % 2, :], qss[:, s % 2, :], neg_half[:, 0:E2], ALU.pow).then_inc(q_rn, 1)

            def set_zeros():
                wait_early(pool)
                pool.memset(lqz[:, :, :, :, :], 0.0).then_inc(set1, 1)
                pool.memset(hT_hi[:, 1, 0:1].bitcast(F32), 0.0).then_inc(set1, 1)
                pool.memset(hT_lo[:, 1, 0:1].bitcast(F32), 0.0).then_inc(set1, 1)

            def set_first_shifted():
                pool.wait_ge(ln_done, 3 * B)
                pool.wait_ge(x2_st, 16 * B)
                pool.memset(hs[0:1, 0, :], 0.0).then_inc(set2, 1)

            def local_probabilities(u):
                for h in range(2):
                    pool.wait_ge(l_rden, 2 * u + h + 1)
                    pr = lp[:, u % 2, h, 0:P]
                    pool.tensor_tensor(pr, pr, lrden[:, u % 2, h, 0:1].broadcast_to([P, P]), ALU.mult)
                    pr = lp[:, u % 2, h, P:LOC_N].rearrange("p (w c) -> p w c", c=LOC)
                    r = lrden[:, u % 2, h, 1:T].rearrange("p (w o) -> p w o", o=1).broadcast_to([P, T - 1, LOC])
                    pool.tensor_tensor(pr, pr, r, ALU.mult).then_inc(l_prob, 1)

            def rotate_q(m, t):
                wait_read(pool, plan["q", m, t])
                q3 = ra[:, t % 2, 0, :]
                pool.tensor_tensor(q3, q3, rb[:, 0, :], ALU.add).then_inc(l_q, 1)

            def inverse_norms(m, t, i):
                pool.wait_ge(l_ssm, 2 * (T * m + t) + i + 1)
                pool.tensor_tensor(rn[:, m % 2, t, i, :], ss[:, i, :], neg_half[:, 0:FH], ALU.pow).then_inc(l_rn, 1)

            def rotate_k(m, t):
                n = T * m + t + 1
                wait_read(pool, plan["k", m, t])
                k3 = ra[:, t % 2, 1, :]
                pool.tensor_tensor(k3, k3, rb[:, 1, :], ALU.add).then_inc(l_kadd, 1)
                inverse_norms(m, t, 1)
                pool.wait_ge(l_rn, 2 * n)
                pool.wait_ge(l_kadd, n)
                k3 = k3.rearrange("p (h d) -> p h d", d=FDH)
                r = rn[:, m % 2, t, 1, :].rearrange("p (h o) -> p h o", o=1).broadcast_to([P, FH, FDH])
                pool.tensor_tensor(k3, k3, r, ALU.mult).then_inc(l_k, 1)

            def mlp_rstd(m):
                pool.wait_ge(f_mv, T * (m + 1))
                pool.tensor_scalar(rstd[:, 0, :], mv[:, 0, :, 1], LN_EPS, None, ALU.add).then_inc(f_eps, 1)
                pool.wait_ge(f_eps, m + 1)
                pool.tensor_tensor(rstd[:, 0, :], rstd[:, 0, :], neg_half[:, 0:T], ALU.pow).then_inc(f_rstd, 1)

            def mlp_bias(m):
                l, b = divmod(m, B)
                pool.wait_ge(f_hn, m + 1)
                if b == 0:
                    pool.wait_ge(ld_small, 16 * (3 * DEPTH + 1 + l))
                if m >= STEPS - 2:
                    pool.wait_ge(x2_ld[b], 16)
                    xb = x2[:, b, :, :]
                    for t in range(T):
                        ins = pool.tensor_tensor(xb[:, t, :], xb[:, t, :], b2[:, :], ALU.add)
                    ins.then_inc(x2_b2, 1)
                    pool.wait_ge(x2_b2, m - (STEPS - 2) + 1)
                    pool.tensor_tensor(y[:, b, :, :], y[:, b, :, :], xb, ALU.add).then_inc(f_b2, 1)
                else:
                    for t in range(T):
                        ins = pool.tensor_tensor(y[:, b, t, :], y[:, b, t, :], b2[:, :], ALU.add)
                    ins.then_inc(f_b2, 1)

            def final_sum(b):
                for tp in range(2):
                    wait_read(pool, plan["w2", STEPS - B + b, tp])
                pool.wait_ge(x2_ld[b], 16)
                pool.tensor_tensor(y[:, b, :, :], y[:, b, :, :], x2[:, b, :, :], ALU.add).then_inc(fin_done, 1)

            for what, *at in order:
                if what == "norm2":
                    norm_rstd(norm_no["norm2", at[0]])
                    add_output_bias(*at)
                if what == "kvs":
                    query_norms(*at)
                if what == "weights" and at[0] == 0:
                    set_zeros()
                if what == "y":
                    norm_rstd(norm_no["y", at[0]])
                if what == "w1_parts" and at[0] == 0:
                    set_first_shifted()
                if what == "soft":
                    local_probabilities(*at)
                if what == "qkv" and at[2] == "q":
                    rotate_q(at[0], at[1])
                    inverse_norms(at[0], at[1], 0)
                if what == "qkv" and at[2] == "k":
                    rotate_k(at[0], at[1])
                if what == "norm":
                    mlp_rstd(*at)
                if what == "bias":
                    mlp_bias(*at)
                if what == "sum":
                    final_sum(*at)

        @block.scalar
        def _(act):
            def copy(dst, src):
                return act.activation(dst, src, ACT.Copy)

            def round_weights_of_quad(c, i):
                act.wait_ge(ld_aw, 16 * c + 16)
                copy(aw_hi[:, i], aw[:, i]).then_inc(a_hi, 1)

            def round_norm(b):
                for e in range(E2):
                    bank = wait_full(act, use_x(b, e))
                    copy(xnT_hi[:, b, e, :], bank[:, :]).then_inc(x_hi, 1)

            def round_q(u):
                bank = wait_full(act, use_q(u))
                copy(q2[0:ADH, 0, :], bank[0:ADH, :])
                copy(q2[ADH:P, 1, :], bank[ADH:P, :]).then_inc(q_hi, 1)

            def round_k(u):
                bank = wait_full(act, use_k(u))
                if not (isinstance(u, int) and u == 0):
                    act.wait_ge(k_both, K_DMAS * u)
                copy(k_round[:, :], bank[:, :]).then_inc(k_hi, 1)

            def evac_v(u, j):
                bank = wait_full(act, use_v(u))
                b, i = divmod(j % QUNITS, 2)
                copy(v[:, b % 2, 2 * i:2 * i + 2, :], bank[:, :].rearrange("p (t c) -> p t c", c=2 * P))\
                    .then_inc(read[use_v(u)[0]], 1)

            def exponentials(u, j, h):
                act.wait_ge(s_neg, 2 * u + (h + 1))
                for i in range(T):
                    pr = probs[:, j % 2, h, TRI_AT[i]:TRI_AT[i + 1]]
                    ins = act.activation(pr, pr, ACT.Exp, bias=negmax[:, j % 2, h, i:i + 1], scale=ADH ** -0.5,
                                         accum_out=den[:, j % 2, h, i:i + 1])
                ins.then_inc(s_exp, 1)

            def evac_pT(u, n):
                h, k = divmod(n, 3)
                bank = wait_full(act, use_t(u, h, k))
                at = KEYB_AT[T_TILES[k][0]]
                w = sum(KEYB[j] for j in T_TILES[k])
                copy(pT[:, h, at:at + w], bank[:, 0:w]).then_inc(read[use_t(u, h, k)[0]], 1)

            def attention_slot(u, j, ahead, c=None):
                last = c is not None and j == QUNITS - 3
                evac_pT(u, 1)
                if ahead >= 1:
                    exponentials(u + 1, j + 1, 0)
                evac_pT(u, 3)
                if ahead >= 2:
                    round_k(u + 2)
                if last:
                    round_weights_of_quad(c, 0)
                evac_pT(u, 5)
                if ahead >= 1:
                    exponentials(u + 1, j + 1, 1)
                if ahead >= 2:
                    round_q(u + 2)
                if last:
                    round_weights_of_quad(c, 1)
                if ahead >= 2:
                    evac_v(u + 2, j + 2)
                if last:
                    round_weights_of_quad(c, 2)

            round_norm(0)
            round_weights_of_quad(0, 0)
            round_weights_of_quad(0, 1)
            round_weights_of_quad(0, 2)
            round_k(0)
            round_q(0)
            round_norm(1)
            evac_v(0, 0)
            round_norm(2)
            round_norm(3)
            exponentials(0, 0, 0)
            round_k(1)
            exponentials(0, 0, 1)
            round_q(1)
            evac_v(1, 1)
            with act.Fori(0, QUADS - 1) as c:
                for j in range(QUNITS):
                    attention_slot(c * QUNITS + j, j, 2, c + 1)
            for j in range(QUNITS):
                attention_slot(NU - QUNITS + j, j, QUNITS - 1 - j)

            def evac_x1T(b):
                for e in range(E2):
                    bank = wait_full(act, plan["x1T", b, e])
                    copy(xnT[:, e, b, :], bank[:, :]).then_inc(read[plan["x1T", b, e][0]], 1)

            def keys(b):
                act.wait_ge(k_min, b + 1)
                act.activation(ktmp[:, :, :], ktmp[:, :, :], ACT.Exp).then_inc(k_exp, 1)
                act.wait_ge(k_fin, b + 1)
                act.activation(ktmp[:, :, :], kf[:, b % 2, :, :], ACT.Square).then_inc(k_sq, 1)
                act.wait_ge(k_ss, b + 1)
                act.activation(knorm[:, b % 2, :, :], knorm[:, b % 2, :, :], ACT.Sqrt).then_inc(k_sqrt, 1)

            def queries(s):
                for e in range(E2):
                    bank = wait_full(act, plan["xq", s, e])
                    act.activation(qr[:, e, :], bank[:, :], ACT.Relu, bias=xbq[:, e:e + 1]).then_inc(q_relu, 1)
                for e in range(E2):
                    wait_read(act, plan["xq", s, e])
                    act.activation(qm[:, e, :], qm[:, e, :], ACT.Exp).then_inc(q_exp, 1)

            def query_squares(s):
                for e in range(E2):
                    act.wait_ge(q_fin, 2 * s + e + 1)
                    act.activation(qm[:, e, :], qT[:, s % 2, e, :], ACT.Square,
                                   accum_out=qss[:, s % 2, e:e + 1]).then_inc(q_sq, 1)

            def evac_xo(b):
                for e in range(E2):
                    use = plan["xo", b, e]
                    bank = wait_full(act, use)
                    copy(oxT[:, b % 2, e, :], bank[:, :]).then_inc(read[use[0]], 1)

            def round_weights(l):
                act.wait_ge(ld_wqkv, 16 * (l + 1))
                if l:
                    wait_full(act, plan["k", B * l - 1, T - 1])
                else:
                    wait_early(act)
                src = wqkv_next if l else wqkv_raw
                for c in (2, 0, 1):
                    cols = slice(c * INNER, (c + 1) * INNER)
                    copy(wqkv_hi[:, :, cols], src[:, :, cols]).then_inc(w_hi, 1)

            def evac_hT(m):
                for e in range(E2):
                    bank = wait_full(act, plan["hT", m, e])
                    copy(hT_hi[:, e, e:S + e], bank[:, :]).then_inc(h_hi, 1)

            def qkv_tile(m, t, what):
                use = plan[what, m, t]
                bank = wait_full(act, use)
                if what == "v":
                    copy(lv[:, m % 2, t, :], bank[:, :]).then_inc(read[use[0]], 1)
                    return
                i = "qk".index(what)
                if m or t:
                    act.wait_ge(l_ss, 2 * (T * m + t - 1) + i + 1)
                act.activation(sq[:, i, :], bank[:, :], ACT.Square).then_inc(l_sq, 1)

            def evac_tq(m, t):
                use = plan["Tq", m, t]
                src = wait_full(act, use)[:, :].rearrange("p (j s) -> p j s", s=P)
                dst = lqz[:, t] if m % 2 else lqz[:, :, t]
                copy(dst[0:FDH, :, 0, :], src[0:FDH])
                copy(dst[FDH:P, :, 1, :], src[FDH:P]).then_inc(read[use[0]], 1)

            def local_exponentials(u):
                m, j = divmod(u, FPAIRS)
                for h in range(2):
                    act.wait_ge(l_neg, 2 * u + h + 1)
                    for w in range(T):
                        pr = lp[:, u % 2, h, loc_at(w):loc_at(w + 1)]
                        ins = act.activation(pr, pr, ACT.Exp, bias=lneg[:, u % 2, h, w:w + 1],
                                             scale=rn[:, m % 2, w, 0, 2 * j + h:2 * j + h + 1],
                                             accum_out=lden[:, u % 2, h, w:w + 1])
                    ins.then_inc(l_exp, 1)

            def evac_T(u, h):
                use = plan["T", u, h, 0]
                bank = wait_full(act, use)
                copy(lpT[:, h, 0:S], bank[:, :]).then_inc(read[use[0]], 1)

            def evac_O(u):
                use = plan["O", u]
                bank = wait_full(act, use)
                copy(loT[:, FPAIRS - 1 - u % FPAIRS, :], bank[:, :]).then_inc(read[use[0]], 1)

            def split_w1(l):
                act.wait_ge(ld_w1, 16 * (l + 1))
                for e in range(E2):
                    copy(w1_hi[:, e, :], w1_raw[:, e, :]).then_inc(w1_hi_ok, 1)

            def evac_hnT(m):
                l = m // B
                if m:
                    wait_read(act, plan["w1a", m - 1, NF - 1])
                for e in range(E2):
                    use = plan["hnT", m, e]
                    bank = wait_full(act, use)
                    for dst, done in ((hnT, hn_hi), (hnT_hi, read[use[0]])):
                        act.activation(dst[:, e, :], bank[:, :], ACT.Identity, bias=lnb[:, l, e:e + 1],
                                       scale=lng[:, l, e:e + 1]).then_inc(done, 1)

            def gates(m, f):
                use = plan["w1g", m, f]
                bank = wait_full(act, use)
                if f >= GELU_T:
                    wait_read(act, plan["w1a", m, f - GELU_T])
                rows = frows(f)
                act.activation(gl[0:rows, f % GELU_T, :], bank[0:rows, :], ACT.Gelu,
                               bias=b1[0:rows, m // B, 1, f:f + 1]).then_inc(read[use[0]], 1)

            for what, *at in order:
                if what == "x1T":
                    evac_x1T(*at)
                if what == "keys":
                    keys(*at)
                if what == "xq":
                    queries(*at)
                if what == "qadd":
                    query_squares(*at)
                if what == "xo":
                    evac_xo(*at)
                if what == "weights":
                    round_weights(*at)
                if what == "w1_parts":
                    split_w1(*at)
                if what == "hT":
                    if at[0] == 0:
                        act.wait_ge(set1, SET1)
                    evac_hT(*at)
                if what == "qkv":
                    qkv_tile(*at)
                if what == "Tqk":
                    evac_tq(*at)
                if what == "exp":
                    local_exponentials(*at)
                if what == "T":
                    evac_T(*at)
                if what == "AV":
                    evac_O(*at)
                if what == "hnT":
                    if at[0] == 0:
                        act.wait_ge(ld_small, 16 * (3 * DEPTH + 1))
                    evac_hnT(*at)
                if what == "w1":
                    gates(*at)

        @block.vector
        def _(dve):
            def norm_stats(n, src):
                for t in range(T):
                    dve.bn_stats(stats[:, n % 2, t, 0:6], src[:, t, :]).then_inc(ln_stats, 1)
                dve.wait_ge(ln_stats, T * (n + 1))
                for t in range(T):
                    dve.bn_aggr(mv[:, n % 2, t, :], stats[:, n % 2, t, 0:6]).then_inc(ln_mv, 1)

            def norm_apply(n, src, dst):
                dve.wait_ge(ln_mv, T * (n + 1))
                dve.wait_ge(ln_rstd, n + 1)
                for t in range(T):
                    ins = dve.tensor_scalar(dst[:, t, :], src[:, t, :], mv[:, n % 2, t, 0:1], rstd[:, n % 2, t:t + 1],
                                            ALU.subtract, ALU.mult)
                ins.then_inc(ln_done, 1)

            def rest_of_norm(b):
                for e in range(E2):
                    bank = wait_full(dve, use_x(b, e))
                    dve.wait_ge(x_hi, E2 * b + e + 1)
                    dve.tensor_tensor(xnT_lo[:, b, e, :], bank[:, :], xnT_hi[:, b, e, :], ALU.subtract)\
                        .then_inc(read[use_x(b, e)[0]], 1)

            def rest_of_weights_of_quad(c, i):
                dve.wait_ge(a_hi, 3 * c + (i + 1))
                dve.tensor_tensor(aw_lo[:, i], aw[:, i], aw_hi[:, i], ALU.subtract).then_inc(a_lo, 1)

            def rest_of_q(u):
                bank = wait_full(dve, use_q(u))
                dve.wait_ge(q_hi, u + 1)
                dve.tensor_tensor(q2[ADH:P, 0, :], bank[0:ADH, :], q2[0:ADH, 0, :], ALU.subtract)
                dve.tensor_tensor(q2[0:ADH, 1, :], bank[ADH:P, :], q2[ADH:P, 1, :], ALU.subtract)\
                    .then_inc(read[use_q(u)[0]], 1)

            def rest_of_k(u):
                bank = wait_full(dve, use_k(u))
                dve.wait_ge(k_hi, u + 1)
                dve.tensor_tensor(k_rest[:, :], bank[:, :], k_round[:, :], ALU.subtract)\
                    .then_inc(read[use_k(u)[0]], 1)

            def masked_scores(u, j, h):
                for k, blocks in enumerate(S_TILES):
                    bank = wait_full(dve, use_s(u, h, k))
                    pass_wait(dve, passed_v)
                    at = 0
                    for i in blocks:
                        ins = dve.tensor_tensor_reduce(
                            probs[:, j % 2, h, TRI_AT[i]:TRI_AT[i + 1]], bank[:, at:at + TRI[i]],
                            causal[:, S - TRI[i]:S], 1.0, -3e38, ALU.add, ALU.max, rowmax[:, j % 2, h, i:i + 1])
                        at += TRI[i]
                    ins.then_inc(read[k], 1)
                for k in range(3):
                    wait_read(dve, use_s(u, h, k))
                dve.tensor_scalar(negmax[:, j % 2, h, :], rowmax[:, j % 2, h, :], -ADH ** -0.5, None, ALU.mult)\
                    .then_inc(s_neg, 1)

            def inverse_sums(u, j, h):
                dve.wait_ge(s_exp, 2 * u + (h + 1))
                dve.reciprocal(rden[:, j % 2, h, :], den[:, j % 2, h, :]).then_inc(s_rden, 1)

            def evac_pT(u, n):
                h, k = divmod(n, 3)
                bank = wait_full(dve, use_t(u, h, k))
                at = KEYB_AT[T_TILES[k][0]]
                w = sum(KEYB[j] for j in T_TILES[k])
                dve.tensor_copy(pT[:, h, at:at + w], bank[:, 0:w]).then_inc(read[use_t(u, h, k)[0]], 1)

            def attention_slot(u, j, ahead, z, c=None):
                evac_pT(u, 0)
                if ahead >= 1:
                    masked_scores(u + 1, j + 1, 0)
                if c is not None and j == QUNITS - 2:
                    rest_of_weights_of_quad(c, 2)
                evac_pT(u, 2)
                if ahead >= 1:
                    masked_scores(u + 1, j + 1, 1)
                evac_pT(u, 4)
                if ahead >= 2:
                    rest_of_k(u + 2)
                if ahead >= 1:
                    inverse_sums(u + 1, j + 1, 0)
                if c is not None and j == QUNITS - 3:
                    rest_of_weights_of_quad(c, 0)
                if ahead >= 1:
                    inverse_sums(u + 1, j + 1, 1)
                if ahead >= 2:
                    rest_of_q(u + 2)
                if c is not None and j == QUNITS - 3:
                    rest_of_weights_of_quad(c, 1)
                bank = wait_full(dve, use_z(u))
                dve.tensor_copy(z, bank[:, :]).then_inc(read[use_z(u)[0]], 1)

            def stats_of_x(b):
                dve.wait_ge(ld_x[b], 16)
                norm_stats(b, x[:, b])

            def normalize_x(b):
                if b >= 2:
                    wait_full(dve, use_x(b - 2, 0))
                    wait_full(dve, use_x(b - 2, 1))
                norm_apply(b, x[:, b], xn1[:, b % 2])

            stats_of_x(0)
            normalize_x(0)
            stats_of_x(1)
            stats_of_x(2)
            rest_of_weights_of_quad(0, 0)
            rest_of_norm(0)
            normalize_x(1)
            rest_of_weights_of_quad(0, 1)
            normalize_x(2)
            rest_of_weights_of_quad(0, 2)
            stats_of_x(3)
            rest_of_k(0)
            rest_of_q(0)
            rest_of_norm(1)
            normalize_x(3)
            dve.wait_ge(ld_causal, 16)
            masked_scores(0, 0, 0)
            rest_of_norm(2)
            masked_scores(0, 0, 1)
            rest_of_norm(3)
            inverse_sums(0, 0, 0)
            inverse_sums(0, 0, 1)
            rest_of_k(1)
            rest_of_q(1)
            with dve.Fori(0, QUADS - 1) as c:
                for j in range(QUNITS):
                    z = zT[:, j // 2, :, :].rearrange("p k s -> p (k s)")[:, bass.ds((c * 2 + j % 2) * S, S)]
                    attention_slot(c * QUNITS + j, j, 2, z, c + 1)
            for j in range(QUNITS):
                attention_slot(NU - QUNITS + j, j, QUNITS - 1 - j, zT[:, j // 2, PAIRS - 2 + j % 2, :])

            dve.wait_ge(ld_xw, 16 * 8)
            dve.tensor_scalar(xkeep[:, :, :], xmask[:, :, :], -1.0, 1.0, ALU.mult, ALU.add).then_inc(k_keep, 1)

            def add_attention(b):
                dve.wait_ge(ld_x[b], 32)
                for tp in range(2):
                    use = plan["awo", b, tp]
                    bank = wait_full(dve, use)
                    xs = x[:, b, 2 * tp:2 * tp + 2, :]
                    dve.tensor_tensor(xs, bank[:, :].rearrange("p (t e) -> p t e", e=D), xs, ALU.add)\
                        .then_inc(read[use[0]], 1)

            def norm2_stats(b):
                wait_read(dve, plan["awo", b, 0])
                wait_read(dve, plan["awo", b, 1])
                norm_stats(norm_no["norm2", b], x[:, b])

            def norm2_apply(b):
                if b >= 2:
                    wait_full(dve, plan["x1T", b - 2, 0])
                    wait_full(dve, plan["x1T", b - 2, 1])
                norm_apply(norm_no["norm2", b], x[:, b], xn[:, b % 2])

            def add_kv_bias(b):
                for t in range(T):
                    use = plan["kv", b, t]
                    bank = wait_full(dve, use)
                    dve.tensor_tensor(kv[:, b % 2, t, :], bank[:, :], xbkv[:, :], ALU.add).then_inc(read[use[0]], 1)
                for t in range(T):
                    wait_read(dve, plan["kv", b, t])
                dve.tensor_scalar(ktmp[:, :, :], kv[:, b % 2, :, 0:D], 0.0, None, ALU.min).then_inc(k_min, 1)

            def keys(b):
                k = kv[:, b % 2, :, 0:D]
                dve.wait_ge(k_exp, b + 1)
                dve.scalar_tensor_tensor(kf[:, b % 2, :, :], k, 0.0, ktmp[:, :, :], ALU.max, ALU.add).then_inc(k_fin, 1)
                dve.wait_ge(k_sq, b + 1)
                norm = knorm[:, b % 2, :, :]
                dve.tensor_reduce(norm.rearrange("p t h -> p (t h)"),
                                  ktmp[:, :, :].rearrange("p t (h d) -> p (t h) d", d=XDH), AX.X, ALU.add)\
                    .then_inc(k_ss, 1)
                dve.wait_ge(k_sqrt, b + 1)
                dve.tensor_scalar(norm, norm, NORM_EPS, None, ALU.max).then_inc(k_rec, 1)
                dve.wait_ge(k_rec, 3 * b + 1)
                dve.reciprocal(norm, norm).then_inc(k_rec, 1)
                dve.wait_ge(k_rec, 3 * b + 2)
                dve.wait_ge(k_keep, 1)
                keep = xkeep[:, b, :].rearrange("p (t o) -> p t o", o=1).broadcast_to([P, T, XH])
                dve.tensor_tensor(norm, norm, keep, ALU.mult).then_inc(k_rec, 1)
                dve.wait_ge(k_rec, 3 * b + 3)
                k3 = kf[:, b % 2, :, :].rearrange("p t (h d) -> p (t h) d", d=XDH)
                r = norm.rearrange("p t h -> p (t h)").rearrange("p (g o) -> p g o", o=1)\
                    .broadcast_to([P, T * XH, XDH])
                dve.tensor_tensor(k3, k3, r, ALU.mult).then_inc(k_done, 1)

            def mask_kv(b):
                use = plan["KV", b]
                bank = wait_full(dve, use)
                for e in range(E2):
                    ins = dve.tensor_tensor(kvm[:, b, e, :], bank[:, e * P:(e + 1) * P], heads[:, :], ALU.mult)
                ins.then_inc(read[use[0]], 1)

            def queries(s):
                for e in range(E2):
                    use = plan["xq", s, e]
                    bank = wait_full(dve, use)
                    dve.wait_ge(q_relu, 2 * s + e + 1)
                    dve.tensor_scalar(qm[:, e, :], bank[:, :], xbq[:, e:e + 1], 0.0, ALU.add, ALU.min)\
                        .then_inc(read[use[0]], 1)

            def add_queries(s):
                for e in range(E2):
                    dve.wait_ge(q_exp, 2 * s + e + 1)
                    dve.tensor_tensor(qT[:, s % 2, e, :], qr[:, e, :], qm[:, e, :], ALU.add).then_inc(q_fin, 1)

            def scale_kv(s):
                dve.wait_ge(q_sq, 2 * s + 2)
                dve.tensor_scalar(qss[:, s % 2, :], qss[:, s % 2, :], NORM_EPS ** 2, None, ALU.max).then_inc(q_max, 1)
                dve.wait_ge(q_rn, s + 1)
                wait_read(dve, plan["KV", s])
                for e in range(E2):
                    dve.tensor_scalar(kvs[:, s % 2, e, :], kvm[:, s, e, :], qss[:, s % 2, e:e + 1], None, ALU.mult)\
                        .then_inc(kvs_done, 1)

            def add_cross(b):
                dve.wait_ge(bo_done, b + 1)
                for tp in range(2):
                    use = plan["xw", b, tp]
                    bank = wait_full(dve, use)
                    xs = x[:, b, 2 * tp:2 * tp + 2, :]
                    dve.tensor_tensor(xs, bank[:, :].rearrange("p (t e) -> p t e", e=D), xs, ALU.add)\
                        .then_inc(read[use[0]], 1)
                for tp in range(2):
                    wait_read(dve, plan["xw", b, tp])
                norm_stats(norm_no["y", b], x[:, b])

            def tables(l):
                H = FDH // 2
                for i in range(2):
                    sc = qk_scale[:, l, i, :].rearrange("p (o d) -> p o d", o=1)
                    by = 1.0 if i else QK_SCALE
                    dve.scalar_tensor_tensor(tab[l][:, 2 * i, :, :], rot[:, 2 * i, :, :], by,
                                             sc.broadcast_to([P, T, FDH]), ALU.mult, ALU.mult).then_inc(l_tab, 1)
                    for lo, other in ((0, H), (H, 0)):
                        dve.scalar_tensor_tensor(tab[l][:, 2 * i + 1, :, lo:lo + H], rot[:, 2 * i + 1, :, lo:lo + H],
                                                 by, sc[:, :, other:other + H].broadcast_to([P, T, H]),
                                                 ALU.mult, ALU.mult).then_inc(l_tab, 1)

            def rest_of_weights(l):
                src = wqkv_next if l else wqkv_raw
                for i, c in enumerate((2, 0, 1)):
                    cols = slice(c * INNER, (c + 1) * INNER)
                    dve.wait_ge(w_hi, 3 * l + i + 1)
                    dve.tensor_tensor(wqkv_lo[:, :, cols], src[:, :, cols], wqkv_hi[:, :, cols], ALU.subtract)\
                        .then_inc(w_lo, 1)

            def evac_hT(m):
                for e in range(E2):
                    use = plan["hT", m, e]
                    bank = wait_full(dve, use)
                    dve.wait_ge(h_hi, E2 * m + e + 1)
                    dve.tensor_tensor(hT_lo[:, e, e:S + e], bank[:, :], hT_hi[:, e, e:S + e], ALU.subtract)\
                        .then_inc(read[use[0]], 1)

            def qkv_tile(m, t, what):
                n = T * m + t
                l = m // B
                i = "qk".index(what)
                use = plan[what, m, t]
                bank = wait_full(dve, use)
                dve.wait_ge(l_sq, 2 * n + i + 1)
                src = bank[:, :].rearrange("p (h d) -> p h d", d=FDH)
                cos = tab[l][:, 2 * i, t:t + 1, :].broadcast_to([P, FH, FDH])
                dve.tensor_tensor(ra[:, t % 2, i, :].rearrange("p (h d) -> p h d", d=FDH), src, cos, ALU.mult)
                if n:
                    dve.wait_ge(l_kadd if i else l_q, n)
                swapped = bank[:, :].rearrange("p (h a d) -> p h a d", a=2, d=FDH // 2)[:, :, ::-1, :]
                sin = tab[l][:, 2 * i + 1, t:t + 1, :].broadcast_to([P, FH, FDH])\
                    .rearrange("p h (a d) -> p h a d", a=2)
                dve.tensor_tensor(rb[:, i, :].rearrange("p (h a d) -> p h a d", a=2, d=FDH // 2), swapped, sin,
                                  ALU.mult).then_inc(read[use[0]], 1)
                if n:
                    dve.wait_ge(l_rn, 2 * (n - 1) + i + 1)
                dve.tensor_reduce(ss[:, i, :], sq[:, i, :].rearrange("p (h d) -> p h d", d=FDH), AX.X, ALU.add)\
                    .then_inc(l_ss, 1)
                dve.wait_ge(l_ss, 2 * n + i + 1)
                dve.tensor_scalar(ss[:, i, :], ss[:, i, :], NORM_EPS ** 2, None, ALU.max).then_inc(l_ssm, 1)

            def evac_tk(m, t):
                use = plan["Tk", m, t]
                bank = wait_full(dve, use)
                dst = lkT[:, t] if m % 2 else lkT[:, :, t]
                dve.tensor_copy(dst, bank[:, :].rearrange("p (j s) -> p j s", s=P)).then_inc(read[use[0]], 1)

            def rest_of_w1(l):
                for e in range(E2):
                    dve.wait_ge(w1_hi_ok, E2 * l + e + 1)
                    dve.tensor_tensor(w1_lo[:, e, :], w1_raw[:, e, :], w1_hi[:, e, :], ALU.subtract)\
                        .then_inc(w1_lo_ok, 1)

            def rest_of_hnT(m):
                for e in range(E2):
                    dve.wait_ge(hn_hi, E2 * m + e + 1)
                    wait_read(dve, plan["hnT", m, e])
                    dve.tensor_tensor(hnT_lo[:, e, :], hnT[:, e, :], hnT_hi[:, e, :], ALU.subtract).then_inc(hn_lo, 1)

            def local_scores(u):
                m, j = divmod(u, FPAIRS)
                if j == 0:
                    dve.wait_ge(l_rn, 2 * T * (m + 1))
                for h in range(2):
                    for k in range(2):
                        use = plan["S", u, h, k]
                        bank = wait_full(dve, use)
                        at = 0
                        for w in (2 * k, 2 * k + 1):
                            lo, hi = loc_at(w), loc_at(w + 1)
                            ins = dve.tensor_tensor_reduce(
                                lp[:, u % 2, h, lo:hi], bank[:, at:at + hi - lo], local[:, LOC - (hi - lo):LOC], 1.0,
                                -3e38, ALU.add, ALU.max, lmax[:, u % 2, h, w:w + 1])
                            at += hi - lo
                        ins.then_inc(read[use[0]], 1)
                    for k in range(2):
                        wait_read(dve, plan["S", u, h, k])
                    dve.scalar_tensor_tensor(lneg[:, u % 2, h, :], lmax[:, u % 2, h, :], -1.0,
                                             rn[:, m % 2, :, 0, 2 * j + h], ALU.mult, ALU.mult).then_inc(l_neg, 1)

            def local_inverse_sums(u):
                for h in range(2):
                    dve.wait_ge(l_exp, 2 * u + h + 1)
                    dve.reciprocal(lrden[:, u % 2, h, :], lden[:, u % 2, h, :]).then_inc(l_rden, 1)

            def evac_T(u, h):
                use = plan["T", u, h, 1]
                bank = wait_full(dve, use)
                dve.tensor_copy(lpT[:, h, S:LOC_N], bank[:, 0:LOC_N - S]).then_inc(read[use[0]], 1)

            def add_to_y(what, m, tp):
                use = plan[what, m, tp]
                bank = wait_full(dve, use)
                ys = y[:, m % B, 2 * tp:2 * tp + 2, :]
                dve.tensor_tensor(ys, bank[:, :].rearrange("p (t e) -> p t e", e=D), ys, ALU.add)\
                    .then_inc(read[use[0]], 1)

            def mlp_stats(m):
                for tp in range(2):
                    wait_read(dve, plan["wo", m, tp])
                for t in range(T):
                    dve.bn_stats(stats[:, 0, t, 0:6], y[:, m % B, t, 0:P]).then_inc(f_stats, 1)

            def mlp_norm(m):
                dve.wait_ge(hs_ld, 32 * (m + 1))
                for t in range(T):
                    dve.bn_stats(stats[:, 0, t, 6:12], hs[:, t, :]).then_inc(f_stats, 1)
                dve.wait_ge(f_stats, 2 * T * (m + 1))
                for t in range(T):
                    dve.bn_aggr(mv[:, 0, t, :], stats[:, 0, t, :]).then_inc(f_mv, 1)

            def mlp_apply(m):
                b = m % B
                dve.wait_ge(f_mv, T * (m + 1))
                dve.wait_ge(f_rstd, m + 1)
                for t in range(T):
                    dve.tensor_scalar(hn[:, t, 0:P], y[:, b, t, 0:P], mv[:, 0, t, 0:1], rstd[:, 0, t:t + 1],
                                      ALU.subtract, ALU.mult)
                    ins = dve.tensor_scalar(hn[:, t, P:D], hs[:, t, :], mv[:, 0, t, 0:1], rstd[:, 0, t:t + 1],
                                            ALU.subtract, ALU.mult)
                ins.then_inc(f_hn, 1)

            def hidden(m, f):
                use = plan["w1a", m, f]
                wait_read(dve, plan["w1g", m, f])
                bank = wait_full(dve, use)
                rows = frows(f)
                dve.scalar_tensor_tensor(hid[0:rows, f, :], bank[0:rows, :], b1[0:rows, m // B, 0, f:f + 1],
                                         gl[0:rows, f % GELU_T, :], ALU.add, ALU.mult).then_inc(read[use[0]], 1)

            for what, *at in order:
                if what == "awo":
                    add_attention(*at)
                    norm2_stats(*at)
                if what == "kv":
                    add_kv_bias(*at)
                if what == "norm2":
                    norm2_apply(*at)
                if what == "keys":
                    keys(*at)
                if what == "KV":
                    mask_kv(*at)
                if what == "xq":
                    queries(*at)
                if what == "qadd":
                    add_queries(*at)
                if what == "kvs":
                    scale_kv(*at)
                if what == "xw":
                    add_cross(*at)
                if what == "y":
                    norm_apply(norm_no["y", at[0]], x[:, at[0]], y[:, at[0]])
                if what == "weights":
                    rest_of_weights(*at)
                if what == "w1_parts":
                    rest_of_w1(*at)
                if what == "tab":
                    dve.wait_ge(ld_rot, 16 * 3)
                    tables(*at)
                    dve.wait_ge(l_tab, 6 * (at[0] + 1))
                if what == "hT":
                    evac_hT(*at)
                if what == "hnT":
                    rest_of_hnT(*at)
                if what == "qkv" and at[2] != "v":
                    qkv_tile(*at)
                if what == "Tqk":
                    evac_tk(*at)
                if what == "S":
                    if at[0] == 0:
                        dve.wait_ge(ld_local, 16)
                    local_scores(*at)
                if what == "soft":
                    local_inverse_sums(*at)
                if what == "T":
                    evac_T(*at)
                if what == "wo":
                    add_to_y("wo", *at)
                if what == "stats":
                    mlp_stats(*at)
                if what == "norm":
                    mlp_norm(*at)
                if what == "apply":
                    mlp_apply(*at)
                if what == "w1":
                    if at[0] == 0 and at[1] == 0:
                        dve.wait_ge(ld_small, 16 * (3 * DEPTH + 1))
                    hidden(*at)
                if what == "w2":
                    dve.wait_ge(f_b2, at[0] + 1)
                    add_to_y("w2", *at)

        @block.tensor
        def _(pe):
            mm = pe.matmul

            def product(dst, pairs, **kw):
                for i, (lhsT, rhs) in enumerate(pairs):
                    ins = mm(dst, lhsT, rhs, start=i == 0, stop=i == len(pairs) - 1, **kw)
                return ins

            def transposed_x(b):
                pe.wait_ge(ln_done, b + 1)
                for e in range(E2):
                    bank = wait_free(pe, use_x(b, e))
                    for t in range(T):
                        ins = pe.transpose(bank[:, t * P:(t + 1) * P], xn1[:, b % 2, t, e * P:(e + 1) * P], ident[:, :])
                    ins.then_inc(full[use_x(b, e)[0]], 1)

            def project_qk(u, b, j, c, i):
                pe.wait_ge(a_lo, 3 * c + (i + 1))
                use = use_q(u) if i else use_k(u)
                bank = wait_free(pe, use)
                cols = slice(j % 2 * P, (j % 2 + 1) * P)
                product(bank[:, :], [(w[:, i, e, cols], x[:, b, e, :]) for e in range(E2)
                                     for w, x in ((aw_hi, xnT_lo), (aw_lo, xnT_hi), (aw_hi, xnT_hi))])\
                    .then_inc(full[use[0]], 1)

            def project_v(u, b, j, c):
                pe.wait_ge(a_lo, 3 * c + 3)
                use = use_v(u)
                bank = wait_free(pe, use)
                for i in range(2):
                    t = 2 * (j % 2) + i
                    ins = product(bank[:, i * 2 * P:(i + 1) * 2 * P],
                                  [(x[:, b, e, t * P:(t + 1) * P], w[:, 2, e, :]) for e in range(E2)
                                   for w, x in ((aw_hi, xnT_lo), (aw_lo, xnT_hi), (aw_hi, xnT_hi))])
                ins.then_inc(full[use[0]], 1)

            def scores(u, h):
                if h == 0:
                    wait_read(pe, use_q(u))
                    wait_read(pe, use_k(u))
                    pe.wait_ge(k_both, K_DMAS * u + K_DMAS)
                rows = slice(h * ADH, (h + 1) * ADH)
                for k, blocks in enumerate(S_TILES):
                    bank = wait_free(pe, use_s(u, h, k))
                    at = 0
                    for i in blocks:
                        n = max(TRI[i], LOC)
                        cols = slice(i * P, (i + 1) * P)
                        ins = product(bank[:, at:at + n], [(k_rest[rows, cols], q2[rows, h, 0:n]),
                                                           (k2[:, h, cols], q2[:, h, 0:n])])
                        at += TRI[i]
                    ins.then_inc(full[k], 1)

            def transposes(u, j, n):
                h, k = divmod(n, 3)
                if k == 0:
                    pe.wait_ge(s_prob, 2 * u + (h + 1))
                use = use_t(u, h, k)
                bank = wait_free(pe, use)
                at = 0
                for c in T_TILES[k]:
                    for i in range(c, T):
                        lo = TRI_AT[i] + c * P
                        ins = pe.transpose(bank[:, at:at + P], probs[:, j % 2, h, lo:lo + P], ident[:, :])
                        at += P
                ins.then_inc(full[use[0]], 1)

            def weighted_values(u, j):
                for k in range(3):
                    wait_read(pe, use_t(u, 1, k))
                b, i = divmod(j, 2)
                if i == 0:
                    wait_read(pe, use_v(u + 1))
                bank = wait_free(pe, use_z(u))
                for c in range(T):
                    for h in range(2):
                        rows = slice(h * ADH, (h + 1) * ADH)
                        cols = slice(i * P + h * ADH, i * P + (h + 1) * ADH)
                        ins = mm(bank[rows, c * P:S], v[:, b % 2, c, cols],
                                 pT[:, h, KEYB_AT[c]:KEYB_AT[c] + KEYB[c]], start=c == 0, stop=c == T - 1)
                ins.then_inc(full[5], 1)

            def attention_slot(u, j, c, ahead):
                n = (j + 2) % QUNITS
                at = (n // 2, n, c + (j + 2) // QUNITS)
                transposes(u, j, 0)
                if ahead >= 1:
                    scores(u + 1, 0)
                transposes(u, j, 1)
                transposes(u, j, 2)
                if ahead >= 1:
                    scores(u + 1, 1)
                transposes(u, j, 3)
                if ahead >= 2:
                    project_qk(u + 2, *at, 0)
                transposes(u, j, 4)
                transposes(u, j, 5)
                if ahead >= 2:
                    project_qk(u + 2, *at, 1)
                weighted_values(u, j)
                if ahead >= 2:
                    project_v(u + 2, *at)

            pe.wait_ge(ld_const, 16)
            transposed_x(0)
            wait_read(pe, use_x(0, 0))
            wait_read(pe, use_x(0, 1))
            project_qk(0, 0, 0, 0, 0)
            project_qk(0, 0, 0, 0, 1)
            transposed_x(1)
            project_v(0, 0, 0, 0)
            transposed_x(2)
            scores(0, 0)
            scores(0, 1)
            transposed_x(3)
            project_qk(1, 0, 1, 0, 1)
            project_qk(1, 0, 1, 0, 0)
            project_v(1, 0, 1, 0)
            wait_read(pe, use_x(B - 1, 0))
            wait_read(pe, use_x(B - 2, 1))
            wait_read(pe, use_x(B - 1, 1))
            with pe.Fori(0, QUADS - 1) as c:
                for j in range(QUNITS):
                    attention_slot(c * QUNITS + j, j, c, 2)
            for j in range(QUNITS):
                attention_slot(NU - QUNITS + j, j, QUADS - 1, QUNITS - 1 - j)

            def attention_output(b):
                if b == 0:
                    pe.wait_ge(ld_wo, 16)
                wait_read(pe, use_z(NU - QUNITS + 2 * b + 1))
                for tp in range(2):
                    use = plan["awo", b, tp]
                    bank = wait_free(pe, use)
                    for i in range(2):
                        t = 2 * tp + i
                        ins = product(bank[:, i * D:(i + 1) * D],
                                      [(zT[:, b, k, t * P:(t + 1) * P], woT[:, k, :]) for k in range(PAIRS)])
                    ins.then_inc(full[use[0]], 1)

            def keys_values(b):
                if b == 0:
                    pe.wait_ge(ld_xw, 16 * 8)
                pe.wait_ge(ld_ctx[b], 16)
                for t in range(T):
                    use = plan["kv", b, t]
                    bank = wait_free(pe, use)
                    product(bank[:, :], [(ctxT[:, b % 2, e, t * P:(t + 1) * P], xwkv[:, e, :]) for e in range(E2)])\
                        .then_inc(full[use[0]], 1)

            def norm2_T(b):
                pe.wait_ge(ln_done, norm_no["norm2", b] + 1)
                for e in range(E2):
                    use = plan["x1T", b, e]
                    bank = wait_free(pe, use)
                    for t in range(T):
                        ins = pe.transpose(bank[:, t * P:(t + 1) * P], xn[:, b % 2, t, e * P:(e + 1) * P], ident[:, :])
                    ins.then_inc(full[use[0]], 1)

            def k_t_v(b):
                pe.wait_ge(k_done, b + 1)
                use = plan["KV", b]
                bank = wait_free(pe, use)
                for e in range(E2):
                    ins = product(bank[:, e * P:(e + 1) * P],
                                  [(kf[:, b % 2, t, e * P:(e + 1) * P], kv[:, b % 2, t, D + e * P:D + (e + 1) * P])
                                   for t in range(T)])
                ins.then_inc(full[use[0]], 1)

            def queries(s):
                for e in range(E2):
                    wait_read(pe, plan["x1T", s, e])
                for c in range(E2):
                    use = plan["xq", s, c]
                    bank = wait_free(pe, use)
                    product(bank[:, :], [(xwq[:, e, c * P:(c + 1) * P], xnT[:, e, s, :]) for e in range(E2)])\
                        .then_inc(full[use[0]], 1)

            def cross_values(b):
                pe.wait_ge(kvs_done, 2 * (b + 1))
                for e in range(E2):
                    use = plan["xo", b, e]
                    bank = wait_free(pe, use)
                    product(bank[:, :], [(kvs[:, b % 2, e, :], qT[:, b % 2, e, :])]).then_inc(full[use[0]], 1)

            def cross_output(b):
                for e in range(E2):
                    wait_read(pe, plan["xo", b, e])
                for tp in range(2):
                    use = plan["xw", b, tp]
                    bank = wait_free(pe, use)
                    for i in range(2):
                        t = 2 * tp + i
                        ins = product(bank[:, i * D:(i + 1) * D],
                                      [(oxT[:, b % 2, e, t * P:(t + 1) * P], xwo[:, e, :]) for e in range(E2)])
                    ins.then_inc(full[use[0]], 1)

            def transposed_y(m):
                l, b = divmod(m, B)
                if l:
                    for tp in range(2):
                        wait_read(pe, plan["w2", m - B, tp])
                else:
                    pe.wait_ge(ln_done, norm_no["y", b] + 1)
                for e in range(E2):
                    use = plan["hT", m, e]
                    bank = wait_free(pe, use)
                    for t in range(T):
                        ins = pe.transpose(bank[:, t * P:(t + 1) * P], y[:, b, t, e * P:(e + 1) * P], ident[:, :])
                    ins.then_inc(full[use[0]], 1)

            def qkv_tile(m, t, what):
                l = m // B
                if t == 0:
                    if what == "v":
                        for e in range(E2):
                            wait_read(pe, plan["hT", m, e])
                    if m % B == 0:
                        pe.wait_ge(w_lo, 3 * l + "vqk".index(what) + 1)
                use = plan[what, m, t]
                bank = wait_free(pe, use)
                cols = slice("qkv".index(what) * INNER, ("qkv".index(what) + 1) * INNER)
                rows = slice(t * P, (t + 1) * P)
                product(bank[:, :], [(h[:, e, rows], w[:, e, cols]) for e in range(E2)
                                     for h, w in ((hT_lo, wqkv_hi), (hT_hi, wqkv_lo), (hT_hi, wqkv_hi))])\
                    .then_inc(full[use[0]], 1)

            def transposed_qk(m, t):
                for i, (what, done) in enumerate((("Tq", l_q), ("Tk", l_k))):
                    pe.wait_ge(done, T * m + t + 1)
                    use = plan[what, m, t]
                    bank = wait_free(pe, use)
                    for j in range(FPAIRS):
                        ins = pe.transpose(bank[:, j * P:(j + 1) * P], ra[:, t % 2, i, j * P:(j + 1) * P], ident[:, :])
                    ins.then_inc(full[use[0]], 1)

            def local_scores(u):
                m, j = divmod(u, FPAIRS)
                if j == 0:
                    wait_read(pe, plan["Tq", m, T - 1])
                    wait_read(pe, plan["Tk", m, T - 1])
                for h in range(2):
                    for k in range(2):
                        use = plan["S", u, h, k]
                        bank = wait_free(pe, use)
                        at = 0
                        for w in (2 * k, 2 * k + 1):
                            c, d = q_at(m, j, w)
                            lo = max(w - 1, 0)
                            n = (w + 1 - lo) * P
                            keys = lkT[:, lo:w + 1, j, :] if m % 2 else lkT[:, j, lo:w + 1, :]
                            ins = mm(bank[:, at:at + n].rearrange("p (w k) -> p w k", k=P), lqz[:, c, d, h, :], keys,
                                     start=True, stop=True)
                            at += n
                        ins.then_inc(full[use[0]], 1)

            def local_transposes(u, h):
                pe.wait_ge(l_prob, 2 * u + h + 1)
                for k in range(2):
                    use = plan["T", u, h, k]
                    bank = wait_free(pe, use)
                    at = 0
                    for c in (2 * k, 2 * k + 1):
                        for w in range(c, min(c + 2, T)):
                            lo = loc_at(w) + (P if w == c and w else 0)
                            ins = pe.transpose(bank[:, at:at + P], lp[:, u % 2, h, lo:lo + P], ident[:, :])
                            at += P
                    ins.then_inc(full[use[0]], 1)

            def local_values(u):
                m, j = divmod(u, FPAIRS)
                for k in range(2):
                    wait_read(pe, plan["T", u, 1, k])
                if j == 0:
                    wait_read(pe, plan["v", m, T - 1])
                use = plan["O", u]
                bank = wait_free(pe, use)
                for c in range(T):
                    n = LOC if c < T - 1 else P
                    for h in range(2):
                        rows = slice(h * FDH, (h + 1) * FDH)
                        cols = slice((2 * j + h) * FDH, (2 * j + h + 1) * FDH)
                        ins = mm(bank[rows, c * P:c * P + n], lv[:, m % 2, c, cols],
                                 lpT[:, h, c * LOC:c * LOC + n], start=c == 0, stop=c == T - 1, skip_group_check=True)
                ins.then_inc(full[use[0]], 1)

            def output_part(m, tp, pairs=range(FPAIRS)):
                wait_read(pe, plan["O", m * FPAIRS + pairs[-1]])
                if m % B == 0:
                    pe.wait_ge(ld_lwo, 16 * (m // B + 1))
                use = plan["wo", m, tp]
                bank = wait_free(pe, use) if 0 in pairs else psum[use[0]]
                for i in range(2):
                    t = 2 * tp + i
                    for k in pairs:
                        ins = mm(bank[:, i * D:(i + 1) * D], loT[:, FPAIRS - 1 - k, t * P:(t + 1) * P], wo[:, k, :],
                                 start=i == 0 and k == 0, stop=i == 1 and k == FPAIRS - 1, skip_group_check=True)
                if FPAIRS - 1 in pairs:
                    ins.then_inc(full[use[0]], 1)

            def transposed_norm(m):
                pe.wait_ge(f_hn, m + 1)
                for e in range(E2):
                    use = plan["hnT", m, e]
                    bank = wait_free(pe, use)
                    for t in range(T):
                        ins = pe.transpose(bank[:, t * P:(t + 1) * P], hn[:, t, e * P:(e + 1) * P], ident[:, :])
                    ins.then_inc(full[use[0]], 1)

            def hidden_part(m, f):
                if f == 0:
                    pe.wait_ge(hn_lo, E2 * (m + 1))
                    if m % B == 0:
                        pe.wait_ge(w1_lo_ok, E2 * (m // B + 1))
                rows = frows(f)
                for what, lo in (("w1g", HID + f * FT), ("w1a", f * FT)):
                    use = plan[what, m, f]
                    bank = wait_free(pe, use)
                    product(bank[0:rows, :], [(w[:, e, lo:lo + rows], h[:, e, :]) for e in range(E2)
                                              for w, h in ((w1_hi, hnT_lo), (w1_lo, hnT_hi), (w1_hi, hnT_hi))])\
                        .then_inc(full[use[0]], 1)

            def second_part(m, tp):
                for f in range(NF - 3, NF):
                    wait_read(pe, plan["w1a", m, f])
                if m % B == 0:
                    pe.wait_ge(ld_w2, 32 * (m // B + 1))
                use = plan["w2", m, tp]
                bank = wait_free(pe, use)
                for i in range(2):
                    t = 2 * tp + i
                    ins = product(bank[:, i * D:(i + 1) * D],
                                  [(hid[0:frows(f), f, t * P:(t + 1) * P], w2[0:frows(f), f, :]) for f in range(NF)])
                ins.then_inc(full[use[0]], 1)

            for what, *at in order:
                if what == "awo":
                    attention_output(*at)
                if what == "kv":
                    keys_values(*at)
                if what == "x1T":
                    norm2_T(*at)
                if what == "KV":
                    k_t_v(*at)
                if what == "xq":
                    queries(*at)
                if what == "xo":
                    cross_values(*at)
                if what == "xw":
                    cross_output(*at)
                if what == "hT":
                    transposed_y(*at)
                if what == "qkv":
                    qkv_tile(*at)
                if what == "Tqk":
                    transposed_qk(*at)
                if what == "S":
                    local_scores(*at)
                if what == "T":
                    local_transposes(*at)
                if what == "AV":
                    local_values(*at)
                if what == "wo_early":
                    output_part(*at, range(FPAIRS - 1))
                if what == "wo":
                    output_part(*at, range(FPAIRS - 1, FPAIRS) if at[0] == STEPS - 1 else range(FPAIRS))
                if what == "hnT":
                    transposed_norm(*at)
                if what == "w1":
                    hidden_part(*at)
                if what == "w2":
                    second_part(*at)


def kernel(x, ctx_1024, mask_BxS2_bk1, L0_attn_W_Q, L0_attn_W_K, L0_attn_W_V, L0_attn_W_O, L0_xattn_Wq, L0_xattn_bq,
           L0_xattn_Wk, L0_xattn_bk, L0_xattn_Wv, L0_xattn_bv, L0_xattn_Wo, L0_xattn_bo, L0_ffn_wqkv, L0_ffn_q_scale,
           L0_ffn_k_scale, L0_ffn_wo, L0_ffn_ln_g, L0_ffn_ln_b, L0_ffn_w1, L0_ffn_b1, L0_ffn_w2, L0_ffn_b2):
    import concourse.bacc as bacc
    from concourse.bass_utils import run_bass_kernel_spmd

    def by_quads(w):
        return np.asarray(w).reshape(QUADS, 2 * P, E2, P).transpose(0, 3, 2, 1)

    def by_rows(w):
        return np.asarray(w).reshape(*np.shape(w)[:-1], E2, P).swapaxes(-1, -2)

    def hidden_rows(w):
        parts = np.asarray(w).reshape(DEPTH, 2, HID)
        filled = np.concatenate([parts, np.zeros((DEPTH, 2, FT * NF - HID), parts.dtype)], 2)
        return filled.reshape(DEPTH, 2, NF, FT).transpose(0, 3, 1, 2)

    arrays = {
        "x": x,
        "ctxT": np.asarray(ctx_1024).transpose(0, 2, 1),
        "mask": np.asarray(mask_BxS2_bk1).reshape(B, T, P).transpose(2, 0, 1),
        "w_quads": np.stack([by_quads(L0_attn_W_K), by_quads(L0_attn_W_Q), by_quads(L0_attn_W_V)], 2),
        "attn_wo": np.asarray(L0_attn_W_O).transpose(0, 2, 1).reshape(AH * ADH, D),
        "xwq": np.asarray(L0_xattn_Wq).T, "xbq": by_rows(L0_xattn_bq),
        "xwkv": np.concatenate([np.asarray(L0_xattn_Wk).T, np.asarray(L0_xattn_Wv).T], 1),
        "xbkv": np.concatenate([np.asarray(L0_xattn_bk), np.asarray(L0_xattn_bv)]),
        "xwo": np.asarray(L0_xattn_Wo).T, "xbo": L0_xattn_bo,
        "wqkv": L0_ffn_wqkv, "q_scale": L0_ffn_q_scale, "k_scale": L0_ffn_k_scale, "wo": L0_ffn_wo,
        "ln_g": by_rows(L0_ffn_ln_g), "ln_b": by_rows(L0_ffn_ln_b), "w1": L0_ffn_w1, "b1": hidden_rows(L0_ffn_b1),
        "w2": L0_ffn_w2, "b2": L0_ffn_b2,
    }
    arrays.update(constants())
    nc = bacc.Bacc("TRN2", target_bir_lowering=False, num_devices=1)
    aps, feeds = {}, {}
    for name, value in arrays.items():
        value = np.ascontiguousarray(value)
        feeds[f"in_{name}"] = value
        aps[name] = nc.dram_tensor(f"in_{name}", value.shape, mybir.dt.from_np(value.dtype), kind="ExternalInput").ap()
    out = nc.dram_tensor("out", (B, S, D), F32, kind="ExternalOutput").ap()
    x2_dram = nc.dram_tensor("x2_scratch", (B, S, D), F32).ap()
    build(nc, aps, out, x2_dram)
    result = run_bass_kernel_spmd(nc, [feeds], core_ids=[0])
    return result.results[0]["out"]
```
